# Optimizing a Trainium2 kernel written in Bass

```python
import numpy as np
import jax
import jax.numpy as jnp

def _softmax(x, axis=-1):
    return jax.nn.softmax(x, axis=axis)

def _gelu(x):
    return jax.nn.gelu(x, approximate=True)

def _silu(x):
    return jax.nn.silu(x)

def _sigmoid(x):
    return jax.nn.sigmoid(x)

def _layernorm(x, axis=-1, eps=1e-05):
    m = jnp.mean(x, axis=axis, keepdims=True)
    v = jnp.var(x, axis=axis, keepdims=True)
    return (x - m) / jnp.sqrt(v + eps)

def _scatter_add(tgt, idx, src, axis=0):
    return tgt.at[idx].add(src)

def _segment_sum(src, seg, n):
    return jax.ops.segment_sum(src, seg, n)
kernel_name = 'mk_prb_d1_jaxref_r8_4d68ab'

def setup_inputs(seed: int=0):
    np.random.seed(seed)
    _w = jnp.asarray

    def _L0_attn_setup():
        import jax, jax.numpy as jnp
        import numpy as np
        BATCH, SEQ, D_MODEL = (4, 256, 128)
        D_STATE, D_CONV, EXPAND, HEADDIM = (64, 4, 2, 64)
        D_INNER = EXPAND * D_MODEL
        NHEADS = D_INNER // HEADDIM
        CONV_DIM = D_INNER + 2 * D_STATE
        D_IN_PROJ = 2 * D_INNER + 2 * D_STATE + NHEADS
        EPS = 1e-05

        def mamba2(X, W_in, conv_w, conv_b, dt_bias, A_log, D, norm_w, W_out):
            b, l, _ = X.shape
            zxbcdt = X @ W_in.T
            z, xBC, dt = jnp.split(zxbcdt, [D_INNER, D_INNER + CONV_DIM], axis=-1)
            dt = jax.nn.softplus(dt + dt_bias)
            xBC_t = xBC.transpose(0, 2, 1)
            ker = conv_w[:, None, :]
            xBC_c = jax.lax.conv_general_dilated(xBC_t, ker, window_strides=(1,), padding=[(D_CONV - 1, 0)], feature_group_count=CONV_DIM)
            xBC = jax.nn.silu(xBC_c.transpose(0, 2, 1) + conv_b)
            x, Bm, Cm = jnp.split(xBC, [D_INNER, D_INNER + D_STATE], axis=-1)
            xh = x.reshape(b, l, NHEADS, HEADDIM)
            A = -jnp.exp(A_log)
            dA = jnp.exp(dt * A)
            dBx = jnp.einsum('blh,bln,blhp->blhpn', dt, Bm, xh)

            def step(h, inp):
                dA_t, dBx_t, C_t = inp
                h = h * dA_t[:, :, None, None] + dBx_t
                y = jnp.einsum('bhpn,bn->bhp', h, C_t)
                return (h, y)
            h0 = jnp.zeros((b, NHEADS, HEADDIM, D_STATE), X.dtype)
            _, ys = jax.lax.scan(step, h0, (dA.transpose(1, 0, 2), dBx.transpose(1, 0, 2, 3, 4), Cm.transpose(1, 0, 2)))
            y = ys.transpose(1, 0, 2, 3) + D[None, None, :, None] * xh
            y = y.reshape(b, l, D_INNER)
            y = y * jax.nn.silu(z)
            y = y * jax.lax.rsqrt(jnp.mean(y * y, axis=-1, keepdims=True) + EPS) * norm_w
            return y @ W_out.T
        key = jax.random.key(seed)
        ks = jax.random.split(key, 6)
        s = 0.02
        return {'X': jax.random.normal(ks[0], (BATCH, SEQ, D_MODEL), jnp.float32), 'W_in': jax.random.normal(ks[1], (D_IN_PROJ, D_MODEL), jnp.float32) * s, 'conv_w': jax.random.normal(ks[2], (CONV_DIM, D_CONV), jnp.float32) * s, 'conv_b': jnp.zeros((CONV_DIM,), jnp.float32), 'dt_bias': jax.random.uniform(ks[3], (NHEADS,), jnp.float32), 'A_log': jnp.log(jax.random.uniform(ks[4], (NHEADS,), jnp.float32, minval=1.0, maxval=16.0)), 'D': jnp.ones((NHEADS,), jnp.float32), 'norm_w': jnp.ones((D_INNER,), jnp.float32), 'W_out': jax.random.normal(ks[5], (D_MODEL, D_INNER), jnp.float32) * s}
    _L0_attn_in = _L0_attn_setup()

    def _L0_ffn_setup():
        import jax, jax.numpy as jnp
        import numpy as np
        E, D, F = (16, 128, 256)
        B, N = (2, 256)
        LN_EPS = 1e-05
        key = jax.random.key(seed)
        ks = jax.random.split(key, 8)
        s = 0.02
        return {'x': jax.random.normal(ks[0], (B, N, D), dtype=jnp.float32), 'router_w': jax.random.normal(ks[1], (E, D), dtype=jnp.float32) * s, 'router_b': jnp.zeros((E,), dtype=jnp.float32), 'w1': jax.random.normal(ks[2], (E, F, D), dtype=jnp.float32) * s, 'w2': jax.random.normal(ks[3], (E, D, F), dtype=jnp.float32) * s, 'w3': jax.random.normal(ks[4], (E, F, D), dtype=jnp.float32) * s, 'ln_g': jnp.ones((E, D), dtype=jnp.float32), 'ln_b': jnp.zeros((E, D), dtype=jnp.float32)}
    _L0_ffn_in = _L0_ffn_setup()
    _d = {'L0_attn_X': _L0_attn_in['X'], 'L0_attn_W_in': _L0_attn_in['W_in'], 'L0_attn_conv_w': _L0_attn_in['conv_w'], 'L0_attn_conv_b': _L0_attn_in['conv_b'], 'L0_attn_dt_bias': _L0_attn_in['dt_bias'], 'L0_attn_A_log': _L0_attn_in['A_log'], 'L0_attn_D': _L0_attn_in['D'], 'L0_attn_norm_w': _L0_attn_in['norm_w'], 'L0_attn_W_out': _L0_attn_in['W_out'], 'L0_ffn_router_w': _L0_ffn_in['router_w'], 'L0_ffn_router_b': _L0_ffn_in['router_b'], 'L0_ffn_w1': _L0_ffn_in['w1'], 'L0_ffn_w2': _L0_ffn_in['w2'], 'L0_ffn_w3': _L0_ffn_in['w3'], 'L0_ffn_ln_g': _L0_ffn_in['ln_g'], 'L0_ffn_ln_b': _L0_ffn_in['ln_b']}
    _x0 = _d['L0_attn_X']
    _d['L0_attn_X'] = jax.random.normal(jax.random.fold_in(jax.random.key(seed), 1), (2, 2048, 128), dtype=_x0.dtype)
    del _x0
    return _d

def reference(L0_attn_X, L0_attn_W_in, L0_attn_conv_w, L0_attn_conv_b, L0_attn_dt_bias, L0_attn_A_log, L0_attn_D, L0_attn_norm_w, L0_attn_W_out, L0_ffn_router_w, L0_ffn_router_b, L0_ffn_w1, L0_ffn_w2, L0_ffn_w3, L0_ffn_ln_g, L0_ffn_ln_b):

    def _L0_attn_ref(X, W_in, conv_w, conv_b, dt_bias, A_log, D, norm_w, W_out):
        import jax, jax.numpy as jnp
        import numpy as np
        BATCH, SEQ, D_MODEL = (4, 256, 128)
        D_STATE, D_CONV, EXPAND, HEADDIM = (64, 4, 2, 64)
        D_INNER = EXPAND * D_MODEL
        NHEADS = D_INNER // HEADDIM
        CONV_DIM = D_INNER + 2 * D_STATE
        D_IN_PROJ = 2 * D_INNER + 2 * D_STATE + NHEADS
        EPS = 1e-05

        def mamba2(X, W_in, conv_w, conv_b, dt_bias, A_log, D, norm_w, W_out):
            b, l, _ = X.shape
            zxbcdt = X @ W_in.T
            z, xBC, dt = jnp.split(zxbcdt, [D_INNER, D_INNER + CONV_DIM], axis=-1)
            dt = jax.nn.softplus(dt + dt_bias)
            xBC_t = xBC.transpose(0, 2, 1)
            ker = conv_w[:, None, :]
            xBC_c = jax.lax.conv_general_dilated(xBC_t, ker, window_strides=(1,), padding=[(D_CONV - 1, 0)], feature_group_count=CONV_DIM)
            xBC = jax.nn.silu(xBC_c.transpose(0, 2, 1) + conv_b)
            x, Bm, Cm = jnp.split(xBC, [D_INNER, D_INNER + D_STATE], axis=-1)
            xh = x.reshape(b, l, NHEADS, HEADDIM)
            A = -jnp.exp(A_log)
            dA = jnp.exp(dt * A)
            dBx = jnp.einsum('blh,bln,blhp->blhpn', dt, Bm, xh)

            def step(h, inp):
                dA_t, dBx_t, C_t = inp
                h = h * dA_t[:, :, None, None] + dBx_t
                y = jnp.einsum('bhpn,bn->bhp', h, C_t)
                return (h, y)
            h0 = jnp.zeros((b, NHEADS, HEADDIM, D_STATE), X.dtype)
            _, ys = jax.lax.scan(step, h0, (dA.transpose(1, 0, 2), dBx.transpose(1, 0, 2, 3, 4), Cm.transpose(1, 0, 2)))
            y = ys.transpose(1, 0, 2, 3) + D[None, None, :, None] * xh
            y = y.reshape(b, l, D_INNER)
            y = y * jax.nn.silu(z)
            y = y * jax.lax.rsqrt(jnp.mean(y * y, axis=-1, keepdims=True) + EPS) * norm_w
            return y @ W_out.T
        return mamba2(X, W_in, conv_w, conv_b, dt_bias, A_log, D, norm_w, W_out) + X

    def _L0_ffn_ref(x, router_w, router_b, w1, w2, w3, ln_g, ln_b):
        import jax, jax.numpy as jnp
        import numpy as np
        E, D, F = (16, 128, 256)
        B, N = (2, 256)
        LN_EPS = 1e-05
        'SparseMixtureOfExperts.forward (eval mode: no router noise, dropout=0).\n\n            Top-2 routing over softmax(router logits), renormalized; each selected\n            expert applies LayerNorm(SwiGLU(x)). Exact math of the torch masked loop,\n            expressed as a scan over experts with zero coefficients for unrouted tokens.\n            '
        Bx, Nx, Dx = x.shape
        xf = x.reshape(-1, Dx)
        logits = xf @ router_w.T + router_b
        probs = jax.nn.softmax(logits, axis=-1)
        top_w, top_e = jax.lax.top_k(probs, 2)
        top_w = top_w / jnp.sum(top_w, axis=-1, keepdims=True)

        def body(acc, params):
            W1, W2, W3, gm, bt, eid = params
            h = jax.nn.silu(xf @ W1.T) * (xf @ W3.T)
            y = h @ W2.T
            mu = jnp.mean(y, axis=-1, keepdims=True)
            var = jnp.var(y, axis=-1, keepdims=True)
            yn = (y - mu) / jnp.sqrt(var + LN_EPS) * gm + bt
            coeff = jnp.sum(jnp.where(top_e == eid, top_w, 0.0), axis=-1)
            return (acc + coeff[:, None] * yn, None)
        eids = jnp.arange(router_w.shape[0], dtype=top_e.dtype)
        out, _ = jax.lax.scan(body, jnp.zeros_like(xf), (w1, w2, w3, ln_g, ln_b, eids))
        return out.reshape(Bx, Nx, Dx)
    x = L0_attn_X
    xn = _layernorm(x, axis=-1)
    x = x + _L0_attn_ref(xn, L0_attn_W_in, L0_attn_conv_w, L0_attn_conv_b, L0_attn_dt_bias, L0_attn_A_log, L0_attn_D, L0_attn_norm_w, L0_attn_W_out) + _L0_ffn_ref(xn, L0_ffn_router_w, L0_ffn_router_b, L0_ffn_w1, L0_ffn_w2, L0_ffn_w3, L0_ffn_ln_g, L0_ffn_ln_b)
    return x

_drawn_inputs = setup_inputs


def setup_inputs(seed=0):
    import zlib

    import numpy as np

    out = dict(_drawn_inputs(seed))
    spreads = {'L0_attn_conv_b': (0.0, 0.1),
     'L0_attn_D': (1.0, 0.6),
     'L0_attn_norm_w': (1.0, 0.6),
     'L0_ffn_router_b': (0.0, 0.1),
     'L0_ffn_ln_g': (1.0, 0.2),
     'L0_ffn_ln_b': (0.0, 0.1)}
    factors = {'L0_attn_conv_w': 4.533, 'L0_attn_dt_bias': 24.052, 'L0_attn_A_log': 8.0}
    for name, (base, spread) in spreads.items():
        noise = np.random.default_rng([zlib.crc32(name.encode()), seed]).standard_normal(out[name].shape)
        drawn = base * np.exp(spread * noise) if base else spread * noise
        out[name] = jnp.asarray(drawn.astype(out[name].dtype))
    for name, factor in factors.items():
        out[name] = (out[name] * factor).astype(out[name].dtype)
    return out
```

```python
import concourse.bass as bass
from concourse import mybir
from concourse.alu_op_type import AluOpType as ALU
from contextlib import ExitStack

F32 = mybir.dt.float32
BF16 = mybir.dt.bfloat16
U32 = mybir.dt.uint32
I32 = mybir.dt.int32
ACT = mybir.ActivationFunctionType
AX = mybir.AxisListType

P = 128
NB, SEQ, D = 2, 2048, 128
T = NB * SEQ
NT = T // P
NC = SEQ // P
DI, NS, NH, HD = 256, 64, 4, 64
ZX = 2 * DI + 2 * NS
KC = 4
HALO = KC - 1
E, F = 16, 256
NSLOT = 2 * T
MT = (NSLOT + E * (P - 1)) // P
MT += -MT % 8
WIN = P + HALO
XB = SEQ + HALO
EPS = 1e-5


def build(nc, X, W_in, conv_w, conv_b, dt_bias, A_log, Dskip, norm_w, W_out,
          router_w, router_b, w1, w2, w3, ln_g, ln_b, out):
    ctx = ExitStack()
    with ctx:
        def sb(name, shape, dt=F32):
            return ctx.enter_context(nc.sbuf_tensor(name, shape, dt))

        def sem(name):
            return ctx.enter_context(nc.semaphore(name))

        def dram(name, shape, dt=F32):
            return nc.dram_tensor(name, shape, dt, kind="Internal").ap()

        def at_least(eng, s, v):
            if not (isinstance(v, int) and v <= 0):
                eng.wait_ge(s, v)

        def along(ap, axis, n):
            shape = list(ap.shape)
            return ap.unsqueeze(axis).broadcast_to(shape[:axis] + [n] + shape[axis:])

        xn_rows = dram("xn_rows", (T, D))
        y_rows = dram("y_rows", (MT * P, D))
        decay_rows = dram("decay_rows", (NT * NH * P,))
        prefix_rows = dram("prefix_rows", (NT * NH * P,))

        ident = sb("ident", [P, P])
        eye4 = sb("eye4", [P, NH, P])
        ones = sb("ones", [P, P])
        zeros = sb("zeros", [P, P])
        half = sb("half", [P, NT])
        eps_col = sb("eps_col", [P, 1])
        lane = sb("lane", [P, P])
        tile_no = sb("tile_no", [P, MT])

        winT = sb("winT", [P, ZX])
        smallT = sb("smallT", [P, NH + E])
        woT = sb("woT", [P, 2, D])
        w13T = sb("w13T", [P, E * 2 * F])
        w2T = sb("w2T", [P, E * F])
        g_all = sb("g_all", [P, E * D])
        b_all = sb("b_all", [P, E * D])
        cw = sb("cw", [P, 3, KC])
        cb = sb("cb", [P, 3])
        nw = sb("nw", [P, 2])
        dskip = sb("dskip", [P, 2])
        dtb = sb("dtb", [P, NH])
        a_log = sb("a_log", [P, NH])
        a_exp = sb("a_exp", [P, NH])
        rb = sb("rb", [P, E])

        x = sb("x", [P, NT, D])
        xnT = sb("xnT", [P, NB * XB])

        dt = sb("dt", [P, NT, NH])

        mix = sb("mix", [P, 2, NT])
        pos = sb("pos", [P, 2, NT])
        owner_i = sb("owner_i", [P, MT], I32)
        GRP = 4
        tok = sb("tok", [P, MT])

        R = 4
        RG = 8
        g_idx = [sb(f"g_idx{i}", [P, 1], U32) for i in range(RG)]
        xg = [sb(f"xg{i}", [P, D]) for i in range(RG)]
        xgT = [sb(f"xgT{i}", [P, P]) for i in range(R)]
        up = [sb(f"up{i}", [P, F]) for i in range(2)]
        hid = [sb(f"hid{i}", [P, F]) for i in range(2)]
        hidT = [sb(f"hidT{i}", [P, 2, P]) for i in range(2)]
        y_sq = [sb(f"y_sq{i}", [P, D]) for i in range(2)]
        y_ms = sb("y_ms", [P, R])
        y_mse = sb("y_mse", [P, R])
        y_rs = sb("y_rs", [P, R])
        y_g = [sb(f"y_g{i}", [P, D]) for i in range(R)]
        y_o = [sb(f"y_o{i}", [P, D]) for i in range(R)]

        bc_decay = [sb(f"bc_decay{i}", [P, NB, NH * P]) for i in range(2)]
        bc_prefix = [sb(f"bc_prefix{i}", [P, NH, P]) for i in range(2)]
        setup_only = ExitStack()

        def sb_setup(name, shape, dt=F32):
            return setup_only.enter_context(nc.sbuf_tensor(name, shape, dt))

        centre = sb_setup("centre", [P, P])
        before = sb_setup("before", [P, P], BF16)
        ones_bf = sb_setup("ones_bf", [P, P], BF16)
        rev_e = sb_setup("rev_e", [P, E])
        steps128 = sb_setup("steps128", [P, NT])
        restart = sb_setup("restart", [P, E, NT])
        token_id = sb_setup("token_id", [P, NT])
        win_st = sb_setup("win_st", [P, 5, D])
        dt_st = sb_setup("dt_st", [NH, D])
        rt_st = sb_setup("rt_st", [E, D])
        wo_st = sb_setup("wo_st", [P, DI])
        ex_st = [sb_setup(f"ex_st{i}", [P, 6, P]) for i in range(2)]
        xn = sb_setup("xn", [P, NT, D])
        mean = sb_setup("mean", [P, NT])
        var = sb_setup("var", [P, NT])
        rstd = sb_setup("rstd", [P, NT])
        dt_v = sb_setup("dt_v", [P, NT, NH])
        dt_n = sb_setup("dt_n", [P, NT, NH])
        dt_u = sb_setup("dt_u", [P, NT, NH])
        dt_w = sb_setup("dt_w", [P, NT, NH])
        dt_l = sb_setup("dt_l", [P, NT, NH])
        dt_r = sb_setup("dt_r", [P, NT, NH])
        dt_c = sb_setup("dt_c", [P, NT, NH])
        dt_d = sb_setup("dt_d", [P, NT, NH])
        dt_e = sb_setup("dt_e", [P, NT, NH])
        dt_a = sb_setup("dt_a", [P, NT, NH])
        decay = sb_setup("decay", [P, NT, NH])
        decayT = sb_setup("decayT", [P, P])
        prefixT = sb_setup("prefixT", [P, P])
        lg = sb_setup("lg", [P, NT, E])
        lg2 = sb_setup("lg2", [P, NT, E])
        key = sb_setup("key", [P, NT, E])
        pick = [sb_setup(f"pick{i}", [P, NT, E]) for i in range(2)]
        both = sb_setup("both", [P, NT, E], BF16)
        top = [sb_setup(f"top{i}", [P, NT]) for i in range(2)]
        first = [sb_setup(f"first{i}", [P, NT]) for i in range(2)]
        gap = sb_setup("gap", [P, NT])
        egap = sb_setup("egap", [P, NT])
        esum = sb_setup("esum", [P, NT])
        tot = sb_setup("tot", [P, E, NT])
        run = sb_setup("run", [P, E, NT])
        more = sb_setup("more", [P, E, NT])
        n_tiles = sb_setup("n_tiles", [P, E])
        end_tile = sb_setup("end_tile", [P, E])
        off = sb_setup("off", [P, E])
        off_all = sb_setup("off_all", [P, E, NT])
        posn = lg2
        pos_u = sb_setup("pos_u", [P, 2, NT], U32)
        hi_u = sb_setup("hi_u", [P, 2, NT], U32)
        lo_u = sb_setup("lo_u", [P, 2, NT], U32)
        hi = sb_setup("hi", [P, 2, NT])
        lo = sb_setup("lo", [P, 2, NT])
        scratch = sb_setup("scratch", [P, MT * E])
        ended = scratch[:, :].rearrange("p (s e) -> p s e", e=E)
        ln_sq = scratch[:, 0:8 * D].rearrange("p (j d) -> p j d", d=D)
        owner = sb_setup("owner", [P, MT])
        is_lane = [sb_setup(f"is_lane{i}", [P, GRP, P]) for i in range(2)]
        is_tile = [sb_setup(f"is_tile{i}", [P, GRP, MT]) for i in range(2)]
        tok_tile = [sb_setup(f"tok_tile{i}", [P, GRP, MT]) for i in range(2)]
        setup_only.close()

        raw = sb("raw", [P, 3, NB, WIN])
        conv = sb("conv", [P, 3, NB, P])
        xcT = [sb(f"xcT{i}", [P, 2, NB, P]) for i in range(2)]
        BT = [sb(f"BT{i}", [P, P]) for i in range(2)]
        CT = [sb(f"CT{i}", [P, P]) for i in range(2)]
        zT = [sb(f"zT{i}", [P, 2, NB, P]) for i in range(2)]
        dt_now = [sb(f"dt_now{i}", [P, NB, NH]) for i in range(2)]
        xdt = [sb(f"xdt{i}", [P, NB, NH, HD]) for i in range(2)]
        Bt = [sb(f"Bt{i}", [P, P]) for i in range(2)]
        L = [sb(f"L{i}", [P, NB, NH * P]) for i in range(2)]
        M = [sb(f"M{i}", [P, NB, NH * P]) for i in range(2)]
        xend = [sb(f"xend{i}", [P, NB, NH, HD]) for i in range(2)]
        CP = [sb(f"CP{i}", [P, NH, P]) for i in range(2)]
        H = [sb(f"H{i}", [P, NH * HD]) for i in range(2)]
        Hm = sb("Hm", [P, NH * HD])
        yD = sb("yD", [P, 2, NB, P])
        yg = [sb(f"yg{i}", [P, 2, NB, P]) for i in range(2)]
        ysq = [sb(f"ysq{i}", [P, 2, NB, P]) for i in range(2)]
        ms = [sb(f"ms{i}", [P, NB]) for i in range(2)]
        rs = [sb(f"rs{i}", [P, NB]) for i in range(2)]
        c_idx = [sb(f"c_idx{i}", [P, 2, NB], U32) for i in range(2)]
        c_mix = [sb(f"c_mix{i}", [P, 2, NB]) for i in range(2)]
        c_row = [sb(f"c_row{i}", [P, 2, NB, D]) for i in range(2)]
        acc = [sb(f"acc{i}", [P, NB, D]) for i in range(2)]

        bank = [ctx.enter_context(nc.psum_tensor(f"bank{i}", [P, 512], F32)) for i in range(8)]

        names = """c_done const_ok w_in x_in0 x_in1 x_in2 x_in3 vec_in gb_in e_in0 e_in1 ln_sum ln_c ln_v ln_act ln_pool
            xn_ok xn_st res_ok swt_ok sev_ok xT_ok xTe_ok lg_ok eT_ok eTe_ok a_ok r_dve r_act r_pe
            both_ok cum_ok oh_ok tk_ok tok_ok own_ok dtT_ok rows_ok rows_st pos_ok dtn_ok dtw_ok dta_ok gap_ok
            """.split()
        S = {n: sem(n) for n in names}
        x_in = [S[f"x_in{i}"] for i in range(4)]
        m_idx, m_x, m_t, m_xt, m_h, m_up, m_hid, m_ht, m_hte, m_y, m_sq, m_eps, m_rs, m_g, m_o = (
            sem(n) for n in ("m_idx", "m_x", "m_t", "m_xt", "m_h", "m_up", "m_hid", "m_ht", "m_hte",
                             "m_y", "m_sq", "m_eps", "m_rs", "m_g", "m_o"))
        m_xg = [sem(f"m_xg{i}") for i in range(RG)]
        m_st = [sem(f"m_st{i}") for i in range(R)]
        s_dec = [sem(f"s_dec{i}") for i in range(2)]
        s_pre = [sem(f"s_pre{i}") for i in range(2)]
        s_row = [sem(f"s_row{i}") for i in range(2)]
        s_sto = [sem(f"s_sto{i}") for i in range(2)]
        (s_px, s_pz, s_raw, s_t0, s_z, s_cv, s_sx, s_sbc, s_tr, s_g, s_dtn, s_xdt, s_bt, s_sc, s_m,
         s_cp, s_xe, s_hm, s_s, s_ha, s_y, s_yD, s_yg, s_sq, s_o, s_ms, s_mp, s_rs, s_ci, s_cm,
         s_f, s_f0, s_g0, s_y0) = (sem("s_" + n) for n in (
             "px", "pz", "raw", "t0", "z", "cv", "sx", "sbc", "tr", "g", "dtn", "xdt", "bt", "sc",
             "m", "cp", "xe", "hm", "s", "ha", "y", "yD", "yg", "sq", "o", "ms", "mp", "rs", "ci",
             "cm", "f", "f0", "g0", "y0"))

        x_v = X.rearrange("b (j p) d -> p (b j) d", p=P)
        xn_v = xn_rows.rearrange("(j p) d -> p j d", p=P)
        out_v = out.rearrange("b (j p) d -> p b j d", p=P)
        xnT_b = xnT[:, :].rearrange("d (b n) -> d b n", b=NB)
        pos_bj = pos[:, :, :].rearrange("p s (b j) -> p s b j", b=NB)
        mix_bj = mix[:, :, :].rearrange("p s (b j) -> p s b j", b=NB)
        dt_bj = dt[:, :, :].rearrange("p (b j) h -> p b j h", b=NB)
        res_bj = x[:, :, :].rearrange("p (b j) d -> p b j d", b=NB)
        LG = 8
        NG = NT // LG
        small_ps = [bank[4 + i][:, 0:16 * (NH + E)].rearrange("p (j n) -> p j n", j=16) for i in range(2)]

        def proj_ps(k):
            return bank[k][:, 0:NB * WIN].rearrange("p (b n) -> p b n", b=NB)

        def evac_tokens(act, A, g):
            act.wait_ge(S["xT_ok"], g + 1)
            b, at = g // 4, (g % 4) * 512
            A(xnT[:, b * XB + HALO + at:b * XB + HALO + at + 512], bank[2 + g % 2][:, :], ACT.Copy).then_inc(S["xTe_ok"], 1)

        bank_h, bank_x, bank_t, bank_y = bank[0:2], bank[2:4], bank[4:6], bank[6:8]

        block = ctx.enter_context(nc.Block())

        def decay_load(sp, c, q):
            at = [c * (NH * P) + b * NC * NH * P for b in range(NB)]
            pairs = c - 1
            if not isinstance(c, int):
                pairs, at = sp.snap(pairs), [sp.snap(a) for a in at]
            at_least(sp, s_hm, pairs)
            for b in range(NB):
                sp.dma_start(bc_decay[q][:, b, :],
                             decay_rows[bass.ds(at[b], NH * P)].partition_broadcast(P)).then_inc(s_dec[q], 16)
                sp.dma_start(bc_prefix[q][b * NS:(b + 1) * NS, :, :].rearrange("p h i -> p (h i)"),
                             prefix_rows[bass.ds(at[b], NH * P)].partition_broadcast(NS)).then_inc(s_pre[q], 16)

        def result_store(sp, c, q):
            sums = 4 * c + 4
            if not isinstance(c, int):
                c, sums = sp.snap(c), sp.snap(sums)
            sp.wait_ge(s_f, sums)
            sp.dma_start(out_v[:, :, bass.ds(c, 1), :].rearrange("p b j d -> p b (j d)"),
                         acc[q][:, :, :]).then_inc(s_sto[q], 16)

        @block.sync
        def _(sp):
            for g in range(NG):
                sp.dma_start(x[:, g * LG:(g + 1) * LG, :], x_v[:, g * LG:(g + 1) * LG, :]).then_inc(x_in[g], 16)
                if g == 0:
                    sp.dma_start(win_st[:, :, :], W_in[0:ZX, :].rearrange("(j p) d -> p j d", p=P)).then_inc(S["w_in"], 16)
                    sp.dma_start(dt_st[:, :], W_in[ZX:ZX + NH, :]).then_inc(S["w_in"], 16)
                    sp.dma_start(rt_st[:, :], router_w).then_inc(S["w_in"], 16)
                    sp.dma_start(wo_st[:, :], W_out).then_inc(S["w_in"], 16)
            for e in range(E):
                q = e % 2
                at_least(sp, S["eT_ok"], 2 * (e - 1))
                sp.dma_start(ex_st[q][:, 0:2, :], w1[e].rearrange("(c p) d -> p c d", p=P)).then_inc(S[f"e_in{q}"], 16)
                sp.dma_start(ex_st[q][:, 2:4, :], w3[e].rearrange("(c p) d -> p c d", p=P)).then_inc(S[f"e_in{q}"], 16)
                sp.dma_start(ex_st[q][:, 4:6, :].rearrange("p c n -> p (c n)"), w2[e]).then_inc(S[f"e_in{q}"], 16)
                if e < NG:
                    sp.wait_ge(S["xn_ok"], e + 1)
                    sp.dma_start(xn_v[:, e * LG:(e + 1) * LG, :], xn[:, e * LG:(e + 1) * LG, :]).then_inc(S["xn_st"], 16)
            sp.wait_ge(S["rows_ok"], 2)
            sp.dma_start(decay_rows.rearrange("(r i) -> r i", i=P), decayT[:, :]).then_inc(S["rows_st"], 16)
            sp.dma_start(prefix_rows.rearrange("(r i) -> r i", i=P), prefixT[:, :]).then_inc(S["rows_st"], 16)
            sp.wait_ge(S["rows_st"], 32)
            decay_load(sp, 0, 0)
            decay_load(sp, 1, 1)

            def tile_store(s, j):
                at, tiles = sp.snap(s * P), sp.snap(s + 1)
                sp.wait_ge(m_o, tiles)
                sp.dma_start(y_rows[bass.ds(at, P), :], y_o[j][:, :]).then_inc(m_st[j], 16)

            with sp.Fori(0 // R, MT // R) as turn_no:
                s0 = turn_no * R
                for j in range(R):
                    tile_store(s0 + j, j)
            decay_load(sp, 2, 0)
            with sp.Fori(0 // 2, (NC - 4) // 2) as turn_no:
                c0 = turn_no * 2
                for q in range(2):
                    decay_load(sp, c0 + q + 3, 1 - q)
                    result_store(sp, c0 + q, q)
            decay_load(sp, NC - 1, 1)
            for c in range(NC - 4, NC):
                result_store(sp, c, c % 2)
            for q in range(2):
                sp.wait_ge(s_sto[q], 16 * (NC // 2))

        @block.gpsimd
        def _(pool):
            pool.memset(ident[:, :], 0.0)
            pool.memset(eye4[:, :, :], 0.0)
            pool.memset(centre[:, :], -1.0 / D)
            pool.memset(before[:, :], 1.0)
            pool.memset(ones_bf[:, :], 1.0)
            pool.memset(ones[:, :], 1.0)
            pool.memset(zeros[:, :], 0.0)
            pool.memset(half[:, :], -0.5)
            pool.memset(eps_col[:, :], EPS)
            pool.memset(restart[:, :, :], 1.0)
            pool.memset(xnT_b[:, :, 0:HALO], 0.0).then_inc(S["c_done"], 1)
            pool.wait_ge(S["c_done"], 1)
            pool.affine_select(out=ident[:, :], in_=ident[:, :], compare_op=ALU.not_equal, fill=1.0,
                               base=0, pattern=[[-1, P]], channel_multiplier=1)
            pool.affine_select(out=eye4[:, :, :], in_=eye4[:, :, :], compare_op=ALU.not_equal, fill=1.0,
                               base=0, pattern=[[0, NH], [-1, P]], channel_multiplier=1)
            pool.affine_select(out=centre[:, :], in_=centre[:, :], compare_op=ALU.not_equal, fill=1.0 - 1.0 / D,
                               base=0, pattern=[[-1, P]], channel_multiplier=1)
            pool.affine_select(out=before[:, :], in_=before[:, :], compare_op=ALU.is_gt, fill=0.0,
                               base=0, pattern=[[1, P]], channel_multiplier=-1)
            pool.memset(restart[:, :, 0:1], 0.0)

            def count(ap, base, pattern, by=0):
                return pool.iota(ap, pattern=pattern, base=base, channel_multiplier=by,
                                 allow_small_or_imprecise_dtypes=True)

            count(rev_e[:, :], E, [[-1, E]])
            count(steps128[:, :], 0, [[P, NT]])
            count(lane[:, :], 0, [[1, P]])
            count(tile_no[:, :], 0, [[1, MT]])
            count(token_id[:, :], 0, [[P, NT]], 1).then_inc(S["const_ok"], 1)
            pool.dma_start(g_all[:, :], ln_g.rearrange("e d -> (e d)").partition_broadcast(P)).then_inc(S["gb_in"], 16)
            pool.dma_start(b_all[:, :], ln_b.rearrange("e d -> (e d)").partition_broadcast(P)).then_inc(S["gb_in"], 16)

            for g in range(NG):
                t = slice(g * LG, (g + 1) * LG)
                pool.wait_ge(S["ln_v"], g + 1)
                pool.tensor_scalar(var[:, t], var[:, t], 1.0 / D, EPS, ALU.mult, ALU.add).then_inc(S["ln_pool"], 1)
                pool.wait_ge(S["ln_pool"], 2 * g + 1)
                pool.tensor_tensor(rstd[:, t], var[:, t], half[:, t], ALU.pow).then_inc(S["ln_pool"], 1)
            for g in range(NG):
                t = slice(g * LG, (g + 1) * LG)
                pool.wait_ge(S["xn_ok"], g + 1)
                pool.tensor_tensor(x[:, t, :], x[:, t, :], xn[:, t, :], ALU.add).then_inc(S["res_ok"], 1)

            pool.wait_ge(S["xn_st"], 16 * NG)

            def gather(s, j):
                pool.indirect_dma_start(out=xg[j][:, :], out_offset=None, in_=xn_rows,
                                        in_offset=bass.IndirectOffsetOnAxis(ap=g_idx[j][:, 0:1], axis=0)
                                        ).then_inc(m_xg[j], 16)

            def step(s, j):
                fixed = isinstance(s, int)
                ahead = 2 if not fixed else min(2, MT - (s + 5))
                if ahead > 0:
                    pool.wait_ge(m_idx, s + 5 + ahead)
                    at_least(pool, m_t, s - 1)
                if fixed and s < 2:
                    for k in range(ahead):
                        gather(s + 5 + k, (j + 5 + k) % RG)
                    return
                f = (j - 2) % R
                at_least(pool, m_o, s - 4)
                pool.wait_ge(m_sq, s)
                pool.tensor_scalar(y_mse[:, f:f + 2], y_ms[:, f:f + 2], EPS, None, ALU.add).then_inc(m_eps, 2)
                for k in range(ahead):
                    gather(s + 5 + k, (j + 5 + k) % RG)
                pool.wait_ge(m_eps, s)
                pool.tensor_tensor(y_rs[:, f:f + 2], y_mse[:, f:f + 2], half[:, 0:2], ALU.pow).then_inc(m_rs, 2)

            pool.wait_ge(m_idx, 5)
            for s in range(5):
                gather(s, s)
            for s in range(0, 8, 2):
                step(s, s % RG)
            with pool.Fori(8 // RG, (MT - 8) // RG) as turn_no:
                s0 = turn_no * RG
                for j in range(0, RG, 2):
                    step(s0 + j, j)
            for s in range(MT - 8, MT + 1, 2):
                step(s, s % RG)

            def mixer_step(c, q, now=True, update=True, prev=True):
                if now:
                    pool.wait_ge(s_sbc, c + 1)
                    pool.wait_ge(s_pre[q], 16 * (c - q) + 32)
                    at_least(pool, s_y, c - 1)
                    pool.tensor_tensor(CP[q][:, :, :], along(CT[q][:, :], 1, NH), bc_prefix[q][:, :, :],
                                       ALU.mult).then_inc(s_cp, 1)
                if update:
                    pool.wait_ge(s_sc, 2 * c + 2)
                    pool.wait_ge(s_xdt, c + 1)
                    at_least(pool, s_s, c - 1)
                    last = L[q][:, :, :].rearrange("p b (h i) -> p (b h) i", i=P)[:, :, P - 1]
                    pool.tensor_tensor(xend[q][:, :, :, :].rearrange("p b h e -> p (b h) e"),
                                       xdt[q][:, :, :, :].rearrange("p b h e -> p (b h) e"),
                                       along(last, 2, HD), ALU.mult).then_inc(s_xe, 1)
                    pool.wait_ge(s_ha, c + 1)
                    pool.tensor_tensor(Hm[:, :].rearrange("p (h e) -> p h e", h=NH),
                                       H[q][:, :].rearrange("p (h e) -> p h e", h=NH),
                                       along(bc_prefix[q][:, :, P - 1], 2, HD), ALU.mult).then_inc(s_hm, 1)
                if prev:
                    o = 1 - q
                    pool.wait_ge(s_ci, c)
                    at_least(pool, s_f, 4 * (c - 2))
                    pool.wait_ge(s_ms, c)
                    pool.tensor_tensor(rs[o][:, :], ms[o][:, :], half[:, 0:NB], ALU.pow).then_inc(s_rs, 1)
                    for s in range(2):
                        for b in range(NB):
                            pool.indirect_dma_start(out=c_row[o][:, s, b, :], out_offset=None, in_=y_rows,
                                                    in_offset=bass.IndirectOffsetOnAxis(ap=c_idx[o][:, s, b:b + 1], axis=0)
                                                    ).then_inc(s_row[o], 16)

            for q in range(R):
                pool.wait_ge(m_st[q], 16 * (MT // R))
            mixer_step(0, 0, prev=False)
            mixer_step(1, 1)
            with pool.Fori(2 // 2, (NC - 2) // 2) as turn_no:
                c0 = turn_no * 2
                for q in range(2):
                    mixer_step(c0 + q, q)
            mixer_step(NC - 2, 0)
            mixer_step(NC - 1, 1, update=False)
            mixer_step(NC, 0, now=False, update=False)

        @block.scalar
        def _(act):
            A = nc.scalar.activation
            for ap, src in ((dtb[:, :], dt_bias.partition_broadcast(P)), (a_log[:, :], A_log.partition_broadcast(P)),
                            (rb[:, :], router_b.partition_broadcast(P)),
                            (cw[:, :, :], conv_w.rearrange("(c p) k -> p c k", p=P)),
                            (cb[:, :], conv_b.rearrange("(c p) -> p c", p=P)),
                            (nw[:, :], norm_w.rearrange("(c p) -> p c", p=P))):
                with nc.allow_non_contiguous_dma(reason="a few small vectors, once"):
                    act.dma_start(ap, src).then_inc(S["vec_in"], 16)
            for h in range(NH):
                act.dma_start(dskip[(h % 2) * HD:(h % 2 + 1) * HD, h // 2:h // 2 + 1],
                              Dskip[h:h + 1].partition_broadcast(HD)).then_inc(S["vec_in"], 16)
            act.wait_ge(S["vec_in"], 16 * 10)
            A(a_exp[:, :], a_log[:, :], ACT.Exp).then_inc(S["a_ok"], 1)
            act.wait_ge(S["swt_ok"], 1)
            A(winT[:, 0:512], bank[0][:, :], ACT.Copy)
            A(winT[:, 512:640], bank[1][:, 0:128], ACT.Copy)
            A(smallT[:, :], bank[1][:, 128:128 + NH + E], ACT.Copy).then_inc(S["sev_ok"], 1)
            for c in range(2):
                A(woT[:, c, :], bank[1][:, 256 + c * P:256 + (c + 1) * P], ACT.Copy,
                  scale=nw[:, c:c + 1]).then_inc(S["sev_ok"], 1)
            for g in range(NG):
                act.wait_ge(S["ln_c"], g + 1)
                at_least(act, S["ln_v"], g)
                A(ln_sq[:, :, :], xn[:, g * LG:(g + 1) * LG, :], ACT.Square).then_inc(S["ln_act"], 1)
                if g >= 1:
                    evac_tokens(act, A, 2 * (g - 1))
                    evac_tokens(act, A, 2 * (g - 1) + 1)
            evac_tokens(act, A, 2 * NG - 2)
            evac_tokens(act, A, 2 * NG - 1)

            act.wait_ge(S["dtn_ok"], 1)
            A(dt_u[:, :, :], dt_n[:, :, :], ACT.Exp).then_inc(S["r_act"], 1)
            act.wait_ge(S["dtw_ok"], 1)
            A(dt_l[:, :, :], dt_w[:, :, :], ACT.Ln).then_inc(S["r_act"], 1)
            act.wait_ge(S["gap_ok"], 1)
            A(egap[:, :], gap[:, :], ACT.Exp).then_inc(S["r_act"], 1)
            act.wait_ge(S["dta_ok"], 1)
            A(decay[:, :, :], dt_a[:, :, :], ACT.Exp).then_inc(S["r_act"], 1)

            for e in range(E):
                q = e % 2
                act.wait_ge(S["eT_ok"], 2 * e + 1)
                A(w13T[:, e * 2 * F:(e + 1) * 2 * F], bank[6 + q][:, :], ACT.Copy).then_inc(S["eTe_ok"], 1)
                act.wait_ge(S["eT_ok"], 2 * e + 2)
                A(w2T[:, e * F:(e + 1) * F], bank[2 + q][:, 0:F], ACT.Copy).then_inc(S["eTe_ok"], 1)

            act.wait_ge(S["tok_ok"], 1)

            def idx(s, j):
                if not (isinstance(s, int) and s < RG):
                    act.wait_ge(m_xg[j], 2 * (s - j))
                A(g_idx[j][:, 0:1], tok[:, bass.ds(s, 1)], ACT.Copy).then_inc(m_idx, 1)

            def silu(s, j):
                act.wait_ge(m_h, s + 1)
                at_least(act, m_hid, s - 1)
                A(up[j % 2][:, :], bank_h[j % 2][:, 0:F], ACT.Silu).then_inc(m_up, 1)

            def hidden_out(s, j):
                act.wait_ge(m_ht, s + 1)
                at_least(act, m_y, s - 1)
                A(hidT[j % 2][:, :, :].rearrange("p c n -> p (c n)"), bank_t[j % 2][:, 0:F], ACT.Copy).then_inc(m_hte, 1)

            def square(s, j):
                act.wait_ge(m_y, s + 1)
                at_least(act, m_rs, s - 3)
                A(y_sq[j % 2][:, :], bank_y[j % 2][:, 0:D], ACT.Square, scale=D ** -0.5,
                  accum_out=y_ms[:, j:j + 1]).then_inc(m_sq, 1)

            for s in range(RG):
                idx(s, s)

            def step(s, j):
                fixed = isinstance(s, int)
                if not fixed or s + 1 < MT:
                    silu(s + 1, (j + 1) % R)
                if not fixed or 0 <= s < MT:
                    hidden_out(s, j % R)
                if not fixed or 1 <= s <= MT:
                    square(s - 1, (j - 1) % R)
                if not fixed or 0 <= s and s + RG < MT:
                    idx(s + RG, j)

            for s in range(-1, 8):
                step(s, s % RG)
            with act.Fori(8 // RG, (MT - 8) // RG) as turn_no:
                s0 = turn_no * RG
                for j in range(RG):
                    step(s0 + j, j)
            for s in range(MT - 8, MT + 1):
                step(s, s % RG)

            def project_out(n, o):
                at_least(act, s_cv, 9 * n)
                for k in range(3):
                    act.wait_ge(s_px, 3 * n + k + 1)
                    A(raw[:, k, :, :], proj_ps(k), ACT.Copy).then_inc(s_raw, 1)
                at_least(act, s_sx, n)
                at_least(act, s_sbc, n)
                for k in range(3):
                    A(conv[:, k, :, :], proj_ps(k)[:, :, 0:P], ACT.Identity, bias=cb[:, k:k + 1],
                      scale=cw[:, k, 0:1]).then_inc(s_t0, 1)
                act.wait_ge(s_pz, n + 1)
                at_least(act, s_yg, n - 1)
                A(zT[o][:, :, :, :].rearrange("p c b i -> p (c b i)"), bank[3][:, :], ACT.Silu).then_inc(s_z, 1)

            def conv_out(n, o):
                act.wait_ge(s_cv, 9 * n + 9)
                at_least(act, s_tr, n - 1)
                at_least(act, s_yD, 2 * (n - 1))
                A(xcT[o][:, :, :, :], conv[:, 0:2, :, :], ACT.Silu).then_inc(s_sx, 1)
                at_least(act, s_g, n - 1)
                at_least(act, s_cp, n - 1)
                for b in range(NB):
                    A(BT[o][b * NS:(b + 1) * NS, :], conv[0:NS, 2, b, :], ACT.Silu)
                    ins = A(CT[o][b * NS:(b + 1) * NS, :], conv[NS:2 * NS, 2, b, :], ACT.Silu)
                ins.then_inc(s_sbc, 1)

            def mixer_step(c, q, now=True, nxt=True, prev=True):
                o = 1 - q
                if now:
                    at_least(act, s_xdt, c - 1)
                    A(dt_now[q][:, :, :], dt_bj[:, :, bass.ds(c, 1), :].rearrange("p b j h -> p b (j h)"),
                      ACT.Copy).then_inc(s_dtn, 1)
                    act.wait_ge(s_dtn, c + 1)
                    act.wait_ge(s_tr, c + 1)
                    at_least(act, s_y, c - 1)
                    at_least(act, s_xe, c - 1)
                    at_least(act, s_s, c - 1)
                    A(Bt[q][:, :], bank[2][:, 384:512], ACT.Copy).then_inc(s_bt, 1)
                    for b in range(NB):
                        for h in range(NH):
                            ins = A(xdt[q][:, b, h, :], bank[4][:, b * DI + h * HD:b * DI + (h + 1) * HD],
                                    ACT.Copy, scale=dt_now[q][:, b, h:h + 1])
                    ins.then_inc(s_xdt, 1)
                if nxt:
                    project_out(c + 1, o)
                if prev:
                    act.wait_ge(s_yg, c)
                    at_least(act, s_o, c - 2)
                    A(ysq[o][:, :, :, :], yg[o][:, :, :, :], ACT.Square).then_inc(s_sq, 1)
                if nxt:
                    conv_out(c + 1, o)
                if prev:
                    if not (isinstance(c, int) and c < 3):
                        act.wait_ge(s_row[o], 32 * (c - 1 - o))
                        act.wait_ge(s_f, 4 * (c - 2))
                    A(c_idx[o][:, :, :], pos_bj[:, :, :, bass.ds(c - 1, 1)].rearrange("p s b j -> p s (b j)"),
                      ACT.Copy).then_inc(s_ci, 1)
                    A(c_mix[o][:, :, :], mix_bj[:, :, :, bass.ds(c - 1, 1)].rearrange("p s b j -> p s (b j)"),
                      ACT.Copy).then_inc(s_cm, 1)
                    act.wait_ge(s_o, c)
                    at_least(act, s_rs, c - 2)
                    A(ms[o][:, :], bank[3][:, 256:256 + NB], ACT.Identity, bias=eps_col[:, 0:1],
                      scale=1.0 / DI).then_inc(s_ms, 1)

            act.wait_ge(S["pos_ok"], 1)
            act.wait_ge(S["own_ok"], 1)
            mixer_step(-1, 1, now=False, prev=False)
            mixer_step(0, 0, prev=False)
            mixer_step(1, 1)
            with act.Fori(2 // 2, (NC - 2) // 2) as turn_no:
                c0 = turn_no * 2
                for q in range(2):
                    mixer_step(c0 + q, q)
            mixer_step(NC - 2, 0)
            mixer_step(NC - 1, 1, nxt=False)
            mixer_step(NC, 0, now=False, nxt=False)


        @block.vector
        def _(dve):
            V = nc.vector
            chain = [0]

            def link(ins):
                chain[0] += 1
                ins.then_inc(S["r_dve"], 1)
                dve.wait_ge(S["r_dve"], chain[0])

            for g in range(NG + 2):
                if g < NG:
                    t = slice(g * LG, (g + 1) * LG)
                    dve.wait_ge(x_in[g], 16)
                    V.reduce_sum(mean[:, t], x[:, t, :], AX.X).then_inc(S["ln_sum"], 1)
                    dve.wait_ge(S["ln_sum"], g + 1)
                    V.scalar_tensor_tensor(xn[:, t, :], along(mean[:, t], 2, D), -1.0 / D, x[:, t, :],
                                           ALU.mult, ALU.add).then_inc(S["ln_c"], 1)
                if 1 <= g <= NG:
                    dve.wait_ge(S["ln_act"], g)
                    V.reduce_sum(var[:, (g - 1) * LG:g * LG], ln_sq[:, :, :], AX.X).then_inc(S["ln_v"], 1)
                if g >= 2:
                    t = slice((g - 2) * LG, (g - 1) * LG)
                    dve.wait_ge(S["ln_pool"], 2 * (g - 1))
                    V.tensor_tensor(xn[:, t, :], xn[:, t, :], along(rstd[:, t], 2, D), ALU.mult).then_inc(S["xn_ok"], 1)

            dve.wait_ge(S["vec_in"], 16 * 10)
            dve.wait_ge(S["const_ok"], 1)
            for i in range(2):
                dve.wait_ge(S["lg_ok"], i + 1)
                j = slice(16 * i, 16 * i + 16)
                V.tensor_tensor(dt_v[:, j, :], small_ps[i][:, :, 0:NH], along(dtb[:, :], 1, 16), ALU.add)
                link(V.tensor_tensor(lg[:, j, :], small_ps[i][:, :, NH:NH + E], along(rb[:, :], 1, 16), ALU.add))
            V.scalar_tensor_tensor(dt_n[:, :, :], dt_v[:, :, :], -1.0, dt_v[:, :, :], ALU.mult,
                                   ALU.min).then_inc(S["dtn_ok"], 1)
            logits = lg
            for s in range(2):
                link(V.reduce_max(top[s][:, :], logits[:, :, :], AX.X))
                link(V.tensor_tensor(key[:, :, :], logits[:, :, :], along(top[s][:, :], 2, E), ALU.is_equal))
                link(V.tensor_tensor(key[:, :, :], key[:, :, :], along(rev_e[:, :], 1, NT), ALU.mult))
                link(V.reduce_max(first[s][:, :], key[:, :, :], AX.X))
                link(V.tensor_tensor(pick[s][:, :, :], along(rev_e[:, :], 1, NT), along(first[s][:, :], 2, E),
                                     ALU.is_equal))
                if s == 0:
                    link(V.scalar_tensor_tensor(lg2[:, :, :], pick[0][:, :, :], -1e30, lg[:, :, :], ALU.mult, ALU.add))
                    logits = lg2
                    dve.wait_ge(S["r_act"], 1)
                    V.tensor_scalar(dt_w[:, :, :], dt_u[:, :, :], 1.0, None, ALU.add).then_inc(S["dtw_ok"], 1)
            V.tensor_tensor(both[:, :, :], pick[0][:, :, :], pick[1][:, :, :], ALU.add).then_inc(S["both_ok"], 1)
            V.tensor_tensor(gap[:, :], top[1][:, :], top[0][:, :], ALU.subtract).then_inc(S["gap_ok"], 1)

            dve.wait_ge(S["dtw_ok"], 1)
            dve.wait_ge(S["r_act"], 2)
            V.reciprocal(dt_r[:, :, :], dt_w[:, :, :])
            link(V.tensor_scalar(dt_c[:, :, :], dt_w[:, :, :], -1.0, None, ALU.add))
            link(V.tensor_tensor(dt_d[:, :, :], dt_u[:, :, :], dt_c[:, :, :], ALU.subtract))
            link(V.tensor_tensor(dt_e[:, :, :], dt_d[:, :, :], dt_r[:, :, :], ALU.mult))
            link(V.tensor_tensor(dt_d[:, :, :], dt_e[:, :, :], dt_l[:, :, :], ALU.add))
            link(V.scalar_tensor_tensor(dt[:, :, :], dt_v[:, :, :], 0.0, dt_d[:, :, :], ALU.max, ALU.add))
            dve.wait_ge(S["a_ok"], 1)
            V.scalar_tensor_tensor(dt_a[:, :, :], dt[:, :, :], -1.0, along(a_exp[:, :], 1, NT), ALU.mult,
                                   ALU.mult).then_inc(S["dta_ok"], 1)

            dve.wait_ge(S["cum_ok"], 1)
            link(V.tensor_copy(tot[:, :, :], bank[1][:, :].rearrange("p (j e) -> p e j", e=E)))
            flat = lambda ap: ap[:, :, :].rearrange("p a b -> p (a b)")
            link(V.tensor_tensor_scan(flat(run), flat(restart), flat(tot), 0.0, ALU.mult, ALU.add))
            link(V.tensor_tensor(more[:, :, :], along(run[:, :, NT - 1], 2, NT), along(steps128[:, :], 1, E), ALU.is_gt))
            link(V.reduce_sum(n_tiles[:, :], more[:, :, :], AX.X))
            link(V.tensor_tensor_scan(end_tile[:, :], ones[:, 0:E], n_tiles[:, :], 0.0, ALU.mult, ALU.add))
            V.tensor_tensor(more[:, :, :], run[:, :, :], tot[:, :, :], ALU.subtract)
            link(V.tensor_tensor(off[:, :], end_tile[:, :], n_tiles[:, :], ALU.subtract))
            link(V.scalar_tensor_tensor(off_all[:, :, :], along(off[:, :], 2, NT), float(P), more[:, :, :],
                                        ALU.mult, ALU.add))
            link(V.tensor_tensor(posn[:, :, :], bank[0][:, :].rearrange("p (j e) -> p j e", e=E),
                                 off_all[:, :, :].rearrange("p e j -> p j e"), ALU.add))
            for s in range(2):
                link(V.tensor_tensor(key[:, :, :], pick[s][:, :, :], posn[:, :, :], ALU.mult))
                link(V.reduce_sum(pos[:, s, :], key[:, :, :], AX.X))
            link(V.tensor_copy(pos_u[:, :, :], pos[:, :, :]))
            V.tensor_scalar(hi_u[:, :, :], pos_u[:, :, :], 7, None, ALU.logical_shift_right)
            link(V.tensor_scalar(lo_u[:, :, :], pos_u[:, :, :], P - 1, None, ALU.bitwise_and))
            V.tensor_copy(hi[:, :, :], hi_u[:, :, :])
            link(V.tensor_copy(lo[:, :, :], lo_u[:, :, :]))

            lo_f, hi_f = (t[:, :, :].rearrange("p s j -> p (s j)") for t in (lo, hi))
            for g in range(2 * NT // GRP):
                q, k, j = g % 2, g * GRP, g * GRP % NT
                at_least(dve, S["tk_ok"], g - 1)
                V.tensor_tensor(is_lane[q][:, :, :], along(lane[:, :], 1, GRP), along(lo_f[:, k:k + GRP], 2, P),
                                ALU.is_equal)
                link(V.tensor_tensor(is_tile[q][:, :, :], along(tile_no[:, :], 1, GRP),
                                     along(hi_f[:, k:k + GRP], 2, MT), ALU.is_equal))
                V.tensor_tensor(tok_tile[q][:, :, :], is_tile[q][:, :, :], along(token_id[:, j:j + GRP], 2, MT),
                                ALU.mult).then_inc(S["oh_ok"], 1)
            link(V.tensor_tensor(ended[:, :, :], along(end_tile[:, :], 1, MT), along(tile_no[:, :], 2, E), ALU.is_le))
            link(V.reduce_sum(owner[:, :], ended[:, :, :], AX.X))
            V.tensor_scalar(owner_i[:, :], owner[:, :], float(E - 1), None, ALU.min).then_inc(S["own_ok"], 1)
            dve.wait_ge(S["r_act"], 3)
            link(V.tensor_scalar(esum[:, :], egap[:, :], 1.0, None, ALU.add))
            link(V.reciprocal(mix[:, 0, :], esum[:, :]))
            V.tensor_tensor(mix[:, 1, :], egap[:, :], mix[:, 0, :], ALU.mult).then_inc(S["pos_ok"], 1)
            dve.wait_ge(S["dtT_ok"], 1)
            V.tensor_tensor_scan(prefixT[:, :], bank[5][:, 384:512], zeros[:, :], 1.0, ALU.mult,
                                 ALU.add).then_inc(S["rows_ok"], 1)
            link(V.tensor_copy(decayT[:, :], bank[5][:, 384:512]))
            V.memset(decayT[:, 0:1], 0.0).then_inc(S["rows_ok"], 1)
            dve.wait_ge(S["tk_ok"], 2 * NT // GRP)
            V.tensor_copy(tok[:, :], bank[0][:, 0:MT]).then_inc(S["tok_ok"], 1)

            dve.wait_ge(S["gb_in"], 32)
            dve.wait_ge(S["own_ok"], 1)

            def x_out(s, j):
                dve.wait_ge(m_t, s + 1)
                at_least(dve, m_h, s - 3)
                V.tensor_copy(xgT[j][:, :], bank_x[j % 2][:, 0:P]).then_inc(m_xt, 1)

            def hidden(s, j):
                dve.wait_ge(m_up, s + 1)
                at_least(dve, m_ht, s - 1)
                V.tensor_tensor(hid[j % 2][:, :], up[j % 2][:, :], bank_h[j % 2][:, F:2 * F], ALU.mult).then_inc(m_hid, 1)

            def gained(s, j):
                e = dve.value_load(owner_i[0:1, bass.ds(s, 1)], min_val=0, max_val=E - 1)
                dve.wait_ge(m_sq, s + 1)
                at_least(dve, m_o, s - R + 1)
                V.tensor_tensor(y_g[j][:, :], bank_y[j % 2][:, 0:D], g_all[:, bass.ds(e * D, D)],
                                ALU.mult).then_inc(m_g, 1)

            def shifted(s, j):
                e = dve.value_load(owner_i[0:1, bass.ds(s, 1)], min_val=0, max_val=E - 1)
                dve.wait_ge(m_rs, s + 1)
                dve.wait_ge(m_g, s + 1)
                if not (isinstance(s, int) and s < R):
                    dve.wait_ge(m_st[j], 4 * (s - j))
                V.scalar_tensor_tensor(y_o[j][:, :], y_g[j][:, :], y_rs[:, j:j + 1], b_all[:, bass.ds(e * D, D)],
                                       ALU.mult, ALU.add).then_inc(m_o, 1)

            def step(s, j):
                fixed = isinstance(s, int)
                if not fixed or s + 2 < MT:
                    x_out(s + 2, (j + 2) % R)
                if not fixed or 0 <= s + 1 < MT:
                    hidden(s + 1, (j + 1) % R)
                if not fixed or 1 <= s <= MT:
                    gained(s - 1, (j - 1) % R)
                if not fixed or 4 <= s:
                    shifted(s - 4, (s - 4) % R if fixed else j % R)

            for s in range(-2, 8):
                step(s, s % RG)
            with dve.Fori(8 // RG, (MT - 8) // RG) as turn_no:
                s0 = turn_no * RG
                for j in range(RG):
                    step(s0 + j, j)
            for s in range(MT - 8, MT + 4):
                step(s, s % RG)

            V.memset(H[0][:, :], 0.0).then_inc(s_ha, 1)

            def mask(c, q):
                dve.wait_ge(s_dec[q], 16 * (c - q) + 32)
                at_least(dve, s_xe, c - 1)
                for b in range(NB):
                    V.tensor_tensor_scan(L[q][:, b, :], bc_decay[q][:, b, :],
                                         eye4[:, :, :].rearrange("p h i -> p (h i)"), 0.0, ALU.mult,
                                         ALU.add).then_inc(s_sc, 1)
                dve.wait_ge(s_g, c + 1)
                at_least(dve, s_y, c - 1)
                for b in range(NB):
                    dve.wait_ge(s_sc, 2 * c + b + 1)
                    V.tensor_tensor(M[q][:, b, :].rearrange("p (h i) -> p h i", h=NH),
                                    L[q][:, b, :].rearrange("p (h i) -> p h i", h=NH),
                                    along(bank[5][:, b * P:(b + 1) * P], 1, NH), ALU.mult).then_inc(s_m, 1)

            def gate(c, q):
                dve.wait_ge(s_y, c + 1)
                for k in range(2):
                    V.scalar_tensor_tensor(yD[:, k, :, :], xcT[q][:, k, :, :], dskip[:, k:k + 1],
                                           bank[7][:, k * NB * P:(k + 1) * NB * P].rearrange("p (b i) -> p b i", b=NB),
                                           ALU.mult, ALU.add).then_inc(s_yD, 1)
                dve.wait_ge(s_z, c + 1)
                at_least(dve, s_o, c - 1)
                dve.wait_ge(s_yD, 2 * c + 2)
                V.tensor_tensor(yg[q][:, :, :, :], yD[:, :, :, :], zT[q][:, :, :, :], ALU.mult).then_inc(s_yg, 1)

            def taps(n):
                for t in range(1, KC):
                    for k in range(3):
                        if t == 1:
                            dve.wait_ge(s_t0, 3 * n + k + 1)
                        else:
                            dve.wait_ge(s_cv, 9 * n + 3 * (t - 2) + k + 1)
                        V.scalar_tensor_tensor(conv[:, k, :, :], raw[:, k, :, t:t + P], cw[:, k, t:t + 1],
                                               conv[:, k, :, :], ALU.mult, ALU.add).then_inc(s_cv, 1)

            def state(c, q):
                dve.wait_ge(s_s, c + 1)
                dve.wait_ge(s_hm, c + 1)
                at_least(dve, s_y, c)
                V.tensor_tensor(H[1 - q][:, :], Hm[:, :], bank[6][:, 0:NH * HD], ALU.add).then_inc(s_ha, 1)

            def scaled(c, q):
                dve.wait_ge(s_rs, c + 1)
                if not (isinstance(c, int) and c < 2):
                    dve.wait_ge(s_sto[q], 8 * (c - q))
                for b in range(NB):
                    V.scalar_tensor_tensor(acc[q][:, b, :], bank[3][:, b * D:(b + 1) * D], rs[q][:, b:b + 1],
                                           res_bj[:, b, bass.ds(c, 1), :].rearrange("p j d -> p (j d)"),
                                           ALU.mult, ALU.add).then_inc(s_f0, 1)

            def combined(c, q):
                dve.wait_ge(s_cm, c + 1)
                dve.wait_ge(s_row[q], 32 * (c - q) + 64)
                for s in range(2):
                    for b in range(NB):
                        if s == 0:
                            dve.wait_ge(s_f0, 2 * c + b + 1)
                        else:
                            dve.wait_ge(s_f, 4 * c + b + 1)
                        V.scalar_tensor_tensor(acc[q][:, b, :], c_row[q][:, s, b, :], c_mix[q][:, s, b:b + 1],
                                               acc[q][:, b, :], ALU.mult, ALU.add).then_inc(s_f, 1)

            def mixer_step(c, q, now=True, nxt=True, prev=True, prev2=True, update=True):
                if now:
                    mask(c, q)
                if prev2:
                    scaled(c - 2, q)
                if prev:
                    gate(c - 1, 1 - q)
                if nxt:
                    taps(c + 1)
                if update:
                    state(c, q)
                if prev2:
                    combined(c - 2, q)

            dve.wait_ge(S["res_ok"], NG)
            mixer_step(-1, 1, now=False, prev=False, prev2=False, update=False)
            mixer_step(0, 0, prev=False, prev2=False)
            mixer_step(1, 1, prev2=False)
            with dve.Fori(2 // 2, (NC - 2) // 2) as turn_no:
                c0 = turn_no * 2
                for q in range(2):
                    mixer_step(c0 + q, q)
            mixer_step(NC - 2, 0)
            mixer_step(NC - 1, 1, nxt=False, update=False)
            mixer_step(NC, 0, now=False, nxt=False, update=False)
            mixer_step(NC + 1, 1, now=False, nxt=False, update=False, prev=False)

        @block.tensor
        def _(pe):
            MM = nc.tensor.matmul
            TR = nc.tensor.transpose
            pe.wait_ge(S["const_ok"], 1)
            pe.wait_ge(S["w_in"], 64)
            for j in range(4):
                TR(bank[0][:, j * P:(j + 1) * P], win_st[:, j, :], ident[:, :])
            TR(bank[1][:, 0:P], win_st[:, 4, :], ident[:, :])
            TR(bank[1][:, P:P + NH], dt_st[:, :], ident[0:NH, 0:NH])
            TR(bank[1][:, P + NH:P + NH + E], rt_st[:, :], ident[0:E, 0:E])
            for c in range(2):
                ins = TR(bank[1][:, DI + c * P:DI + (c + 1) * P], wo_st[:, c * P:(c + 1) * P], ident[:, :])
            ins.then_inc(S["swt_ok"], 1)

            def small(g):
                pe.wait_ge(S["xTe_ok"], g + 1)
                if g == 0:
                    pe.wait_ge(S["sev_ok"], 1)
                for j in range(4 * g, 4 * g + 4):
                    b, at = j // NC, j % NC * P
                    ins = MM(small_ps[j // 16][:, j % 16, :], xnT_b[:, b, HALO + at:HALO + at + P], smallT[:, :],
                             start=True, stop=True)
                if g % 4 == 3:
                    ins.then_inc(S["lg_ok"], 1)

            for g in range(2 * NG):
                pe.wait_ge(S["xn_ok"], g // 2 + 1)
                at_least(pe, S["xTe_ok"], g - 1)
                for j in range(4):
                    ins = TR(bank[2 + g % 2][:, j * P:(j + 1) * P], xn[:, 4 * g + j, :], ident[:, :])
                ins.then_inc(S["xT_ok"], 1)
                if g >= 1:
                    small(g - 1)
            small(2 * NG - 1)

            def expert(e):
                q = e % 2
                pe.wait_ge(S[f"e_in{q}"], 24 * (e - q) + 48)
                at_least(pe, S["eTe_ok"], 2 * (e - 1))
                if e < 2:
                    pe.wait_ge(S["xTe_ok"], 2 * NG)
                for k in range(4):
                    ins = TR(bank[6 + q][:, k * P:(k + 1) * P], ex_st[q][:, k, :], ident[:, :])
                ins.then_inc(S["eT_ok"], 1)
                for k in range(2):
                    ins = MM(bank[2 + q][:, k * P:(k + 1) * P], ex_st[q][:, 4 + k, :], centre[:, :], start=True, stop=True)
                ins.then_inc(S["eT_ok"], 1)

            for e in range(4):
                expert(e)
            pe.wait_ge(S["both_ok"], 1)
            pe.wait_ge(S["sev_ok"], 3)
            picks = both[:, :, :].rearrange("p j e -> p (j e)")
            MM(bank[0][:, :], before[:, :], picks, start=True, stop=True)
            MM(bank[1][:, :], ones_bf[:, :], picks, start=True, stop=True).then_inc(S["cum_ok"], 1)
            pe.wait_ge(S["r_act"], 4)
            TR(bank[5][:, 384:512], decay[:, :, :].rearrange("p j h -> p (j h)"), ident[:, :]).then_inc(S["dtT_ok"], 1)
            ng = 2 * NT // GRP
            for g in range(ng):
                for e in range(4 + g * (E - 4) // ng, 4 + (g + 1) * (E - 4) // ng):
                    expert(e)
                pe.wait_ge(S["oh_ok"], g + 1)
                for k in range(GRP):
                    ins = MM(bank[0][:, 0:MT], is_lane[g % 2][:, k, :], tok_tile[g % 2][:, k, :],
                             start=(g == 0 and k == 0), stop=(g == ng - 1 and k == GRP - 1))
                ins.then_inc(S["tk_ok"], 1)

            pe.wait_ge(S["eTe_ok"], 2 * E)
            pe.wait_ge(S["own_ok"], 1)
            pe.wait_ge(S["tok_ok"], 1)
            pe.wait_ge(S["rows_ok"], 2)

            def turn_x(s, j):
                pe.wait_ge(m_xg[j], 2 * (s - j) + 16)
                at_least(pe, m_xt, s - 1)
                o = j % R
                TR(bank_x[o % 2][:, 0:P], xg[j][:, :], ident[:, :]).then_inc(m_t, 1)

            def up_proj(s, j):
                e = pe.value_load(owner_i[0:1, bass.ds(s, 1)], min_val=0, max_val=E - 1)
                pe.wait_ge(m_xt, s + 1)
                at_least(pe, m_hid, s - 1)
                MM(bank_h[j % 2][:, :], xgT[j][:, :], w13T[:, bass.ds(e * 2 * F, 2 * F)], start=True, stop=True).then_inc(m_h, 1)

            def turn_hidden(s, j):
                pe.wait_ge(m_hid, s + 1)
                at_least(pe, m_hte, s - 1)
                for k in range(2):
                    ins = TR(bank_t[j % 2][:, k * P:(k + 1) * P], hid[j % 2][:, k * P:(k + 1) * P],
                             ident[:, :])
                ins.then_inc(m_ht, 1)

            def down_proj(s, j):
                e = pe.value_load(owner_i[0:1, bass.ds(s, 1)], min_val=0, max_val=E - 1)
                pe.wait_ge(m_hte, s + 1)
                at_least(pe, m_g, s - 1)
                for k in range(2):
                    ins = MM(bank_y[j % 2][:, 0:D], hidT[j % 2][:, k, :], w2T[:, bass.ds(e * F + k * P, P)],
                             start=(k == 0), stop=(k == 1))
                ins.then_inc(m_y, 1)

            def step(s, j):
                fixed = isinstance(s, int)
                if not fixed or s + 2 < MT:
                    turn_x(s + 2, (j + 2) % RG)
                if not fixed or -1 <= s and s + 1 < MT:
                    up_proj(s + 1, (j + 1) % R)
                if not fixed or 0 <= s < MT:
                    turn_hidden(s, j % R)
                if not fixed or 1 <= s:
                    down_proj(s - 1, (j - 1) % R)

            for s in range(-2, 8):
                step(s, s % RG)
            with pe.Fori(8 // RG, (MT - 8) // RG) as turn_no:
                s0 = turn_no * RG
                for j in range(RG):
                    step(s0 + j, j)
            for s in range(MT - 8, MT + 1):
                step(s, s % RG)

            pe.wait_ge(m_o, MT)

            def project(n):
                at_least(pe, s_t0, 3 * n)
                at_least(pe, s_bt, n)
                for k in range(3):
                    MM(proj_ps(k), winT[:, DI + k * P:DI + (k + 1) * P], xnT_b[:, :, bass.ds(n * P, WIN)],
                       start=True, stop=True).then_inc(s_px, 1)
                at_least(pe, s_z, n)
                at_least(pe, s_f0, 2 * n - 4)
                for k in range(2):
                    ins = MM(bank[3][:, k * NB * P:(k + 1) * NB * P].rearrange("p (b n) -> p b n", b=NB),
                             winT[:, k * P:(k + 1) * P], xnT_b[:, :, bass.ds(n * P + HALO, P)], start=True, stop=True)
                ins.then_inc(s_pz, 1)

            def turn(c, q):
                pe.wait_ge(s_sx, c + 1)
                at_least(pe, s_xdt, c)
                for b in range(NB):
                    for k in range(2):
                        TR(bank[4][:, b * DI + k * P:b * DI + (k + 1) * P], xcT[q][:, k, b, :], ident[:, :])
                pe.wait_ge(s_sbc, c + 1)
                at_least(pe, s_m, 2 * c)
                MM(bank[5][:, 0:P], BT[q][0:NS, :], CT[q][0:NS, :], start=True, stop=True).then_inc(s_g0, 1)
                at_least(pe, s_bt, c)
                TR(bank[2][:, 384:512], BT[q][:, :], ident[:, :]).then_inc(s_tr, 1)
                pe.wait_ge(s_g0, c + 1)
                MM(bank[5][:, P:2 * P], BT[q][NS:2 * NS, :], CT[q][NS:2 * NS, :], start=True, stop=True).then_inc(s_g, 1)

            def chunk_state(c, q):
                pe.wait_ge(s_xe, c + 1)
                pe.wait_ge(s_bt, c + 1)
                pe.wait_ge(s_ha, c + 1)
                for b in range(NB):
                    ins = MM(bank[6][b * NS:(b + 1) * NS, 0:NH * HD], Bt[q][:, b * NS:(b + 1) * NS],
                             xend[q][:, b, :, :].rearrange("p h e -> p (h e)"), start=True, stop=True)
                ins.then_inc(s_s, 1)

            def mix_steps(c, q):
                pe.wait_ge(s_xdt, c + 1)
                pe.wait_ge(s_cp, c + 1)
                pe.wait_ge(s_ha, c + 1)
                pe.wait_ge(s_m, 2 * c + 2)
                at_least(pe, s_yD, 2 * c)
                for b in range(NB):
                    n = slice(b * NS, (b + 1) * NS)
                    for h in range(0, NH, 2):
                        at = (h // 2) * NB * P + b * P
                        for k in range(2):
                            if b == 1 and h == 0 and k == 1:
                                pe.wait_ge(s_y0, c + 1)
                            MM(bank[7][k * HD:(k + 1) * HD, at:at + P], xdt[q][:, b, h + k, :],
                               M[q][:, b, (h + k) * P:(h + k + 1) * P], start=True, stop=False)
                        for k in range(2):
                            ins = MM(bank[7][k * HD:(k + 1) * HD, at:at + P], H[q][n, (h + k) * HD:(h + k + 1) * HD],
                                     CP[q][n, h + k, :], start=False, stop=True)
                    ins.then_inc((s_y0, s_y)[b], 1)

            def project_back(c, q, after_z=True):
                pe.wait_ge(s_sq, c + 1)
                at_least(pe, s_f0, 2 * c)
                if after_z:
                    pe.wait_ge(s_z, c + 3)
                for b in range(NB):
                    for k in range(2):
                        MM(bank[3][:, b * D:(b + 1) * D], yg[q][:, k, b, :], woT[:, k, :],
                           start=(k == 0), stop=(k == 1))
                for b in range(NB):
                    for k in range(2):
                        ins = MM(bank[3][:, 256 + b:257 + b], ysq[q][:, k, b, :], ones[:, 0:1],
                                 start=(k == 0), stop=(k == 1))
                ins.then_inc(s_o, 1)

            def mixer_step(c, q, now=True, nxt=True, prev=True, update=True):
                if now:
                    turn(c, q)
                if nxt:
                    project(c + 1)
                if update:
                    chunk_state(c, q)
                if now:
                    mix_steps(c, q)
                if prev:
                    project_back(c - 1, 1 - q, nxt)

            mixer_step(-1, 1, now=False, prev=False, update=False)
            mixer_step(0, 0, prev=False)
            mixer_step(1, 1)
            with pe.Fori(2 // 2, (NC - 2) // 2) as turn_no:
                c0 = turn_no * 2
                for q in range(2):
                    mixer_step(c0 + q, q)
            mixer_step(NC - 2, 0)
            mixer_step(NC - 1, 1, nxt=False, update=False)
            mixer_step(NC, 0, now=False, nxt=False, update=False)


INS = ["L0_attn_X", "L0_attn_W_in", "L0_attn_conv_w", "L0_attn_conv_b", "L0_attn_dt_bias", "L0_attn_A_log",
       "L0_attn_D", "L0_attn_norm_w", "L0_attn_W_out", "L0_ffn_router_w", "L0_ffn_router_b", "L0_ffn_w1",
       "L0_ffn_w2", "L0_ffn_w3", "L0_ffn_ln_g", "L0_ffn_ln_b"]


def kernel(**inputs):
    import numpy as np
    import concourse.bacc as bacc
    from concourse.bass_utils import run_bass_kernel_spmd

    nc = bacc.Bacc("TRN2", target_bir_lowering=False, num_devices=1)
    arrays, args = {}, []
    for name in INS:
        a = np.ascontiguousarray(inputs[name])
        arrays[f"in_{name}"] = a
        args.append(nc.dram_tensor(f"in_{name}", a.shape, mybir.dt.from_np(a.dtype), kind="ExternalInput").ap())
    out = nc.dram_tensor("out", (NB, SEQ, D), F32, kind="ExternalOutput").ap()
    build(nc, *args, out)
    r = run_bass_kernel_spmd(nc, [arrays], core_ids=[0])
    return np.asarray(r.results[0]["out"])
```

```python
import concourse.bass as bass
from concourse import mybir
from concourse.alu_op_type import AluOpType as ALU
from contextlib import ExitStack

F32 = mybir.dt.float32
BF16 = mybir.dt.bfloat16
U32 = mybir.dt.uint32
I32 = mybir.dt.int32
ACT = mybir.ActivationFunctionType
AX = mybir.AxisListType

P = 128
NB, SEQ, D = 2, 2048, 128
T = NB * SEQ
NT = T // P
NC = SEQ // P
DI, NS, NH, HD = 256, 64, 4, 64
ZX = 2 * DI + 2 * NS
KC = 4
HALO = KC - 1
E, F = 16, 256
NSLOT = 2 * T
MT = (NSLOT + E * (P - 1)) // P
MT += -MT % 8
WIN = P + HALO
XB = SEQ + HALO
EPS = 1e-5


def build(nc, X, W_in, conv_w, conv_b, dt_bias, A_log, Dskip, norm_w, W_out,
          router_w, router_b, w1, w2, w3, ln_g, ln_b, out):
    ctx = ExitStack()
    with ctx:
        def sb(name, shape, dt=F32):
            return ctx.enter_context(nc.sbuf_tensor(name, shape, dt))

        def sem(name):
            return ctx.enter_context(nc.semaphore(name))

        def dram(name, shape, dt=F32):
            return nc.dram_tensor(name, shape, dt, kind="Internal").ap()

        def at_least(eng, s, v):
            if not (isinstance(v, int) and v <= 0):
                eng.wait_ge(s, v)

        def along(ap, axis, n):
            shape = list(ap.shape)
            return ap.unsqueeze(axis).broadcast_to(shape[:axis] + [n] + shape[axis:])

        xn_rows = dram("xn_rows", (T, D))
        y_rows = dram("y_rows", (MT * P, D))
        decay_rows = dram("decay_rows", (NT * NH * P,))
        prefix_rows = dram("prefix_rows", (NT * NH * P,))

        ident = sb("ident", [P, P])
        eye4 = sb("eye4", [P, NH, P])
        ones = sb("ones", [P, P])
        zeros = sb("zeros", [P, P])
        half = sb("half", [P, NT])
        eps_col = sb("eps_col", [P, 1])
        lane = sb("lane", [P, P])
        tile_no = sb("tile_no", [P, MT])

        winT = sb("winT", [P, ZX])
        smallT = sb("smallT", [P, NH + E])
        woT = sb("woT", [P, 2, D])
        w13T = sb("w13T", [P, E * 2 * F])
        w2T = sb("w2T", [P, E * F])
        g_all = sb("g_all", [P, E * D])
        b_all = sb("b_all", [P, E * D])
        cw = sb("cw", [P, 3, KC])
        cb = sb("cb", [P, 3])
        nw = sb("nw", [P, 2])
        dskip = sb("dskip", [P, 2])
        dtb = sb("dtb", [P, NH])
        a_log = sb("a_log", [P, NH])
        a_exp = sb("a_exp", [P, NH])
        rb = sb("rb", [P, E])

        x = sb("x", [P, NT, D])
        xnT = sb("xnT", [P, NB * XB])

        dt = sb("dt", [P, NT, NH])

        mix = sb("mix", [P, 2, NT])
        pos = sb("pos", [P, 2, NT])
        OW, OB = 6, 4
        owner_w = sb("owner_w", [P, MT // 8, 2], I32)
        GRP = 4
        tok = sb("tok", [P, MT])

        R = 4
        RG = 8
        g_idx = [sb(f"g_idx{i}", [P, 1], U32) for i in range(RG)]
        xg = [sb(f"xg{i}", [P, D]) for i in range(RG)]
        xgT = [sb(f"xgT{i}", [P, P]) for i in range(R)]
        up = [sb(f"up{i}", [P, F]) for i in range(2)]
        hid = [sb(f"hid{i}", [P, F]) for i in range(2)]
        hidT = [sb(f"hidT{i}", [P, 2, P]) for i in range(2)]
        y_sq = [sb(f"y_sq{i}", [P, D]) for i in range(2)]
        LAG = 6
        RY = 8
        y_ms = sb("y_ms", [P, RY])
        y_mse = sb("y_mse", [P, RY])
        y_rs = sb("y_rs", [P, RY])
        y_o = [sb(f"y_o{i}", [P, D]) for i in range(R)]

        bc_decay = [sb(f"bc_decay{i}", [P, NB, NH * P]) for i in range(2)]
        bc_prefix = [sb(f"bc_prefix{i}", [P, NH, P]) for i in range(2)]
        setup_only = ExitStack()

        def sb_setup(name, shape, dt=F32):
            return setup_only.enter_context(nc.sbuf_tensor(name, shape, dt))

        centre = sb_setup("centre", [P, P])
        before = sb_setup("before", [P, P], BF16)
        ones_bf = sb_setup("ones_bf", [P, P], BF16)
        rev_e = sb_setup("rev_e", [P, E])
        steps128 = sb_setup("steps128", [P, NT])
        restart = sb_setup("restart", [P, E, NT])
        token_id = sb_setup("token_id", [P, NT])
        win_st = sb_setup("win_st", [P, 5, D])
        dt_st = sb_setup("dt_st", [NH, D])
        rt_st = sb_setup("rt_st", [E, D])
        wo_st = sb_setup("wo_st", [P, DI])
        ex_st = [sb_setup(f"ex_st{i}", [P, 6, P]) for i in range(2)]
        xn = sb_setup("xn", [P, NT, D])
        mean = sb_setup("mean", [P, NT])
        var = sb_setup("var", [P, NT])
        rstd = sb_setup("rstd", [P, NT])
        dt_v = sb_setup("dt_v", [P, NT, NH])
        dt_n = sb_setup("dt_n", [P, NT, NH])
        dt_u = sb_setup("dt_u", [P, NT, NH])
        dt_w = sb_setup("dt_w", [P, NT, NH])
        dt_l = sb_setup("dt_l", [P, NT, NH])
        dt_r = sb_setup("dt_r", [P, NT, NH])
        dt_c = sb_setup("dt_c", [P, NT, NH])
        dt_d = sb_setup("dt_d", [P, NT, NH])
        dt_e = sb_setup("dt_e", [P, NT, NH])
        dt_a = dt_n
        decay = sb_setup("decay", [P, NT, NH])
        decayT = sb_setup("decayT", [P, P])
        prefixT = sb_setup("prefixT", [P, P])
        lg = sb_setup("lg", [P, NT, E])
        lg2 = sb_setup("lg2", [P, NT, E])
        key = sb_setup("key", [P, NT, E])
        pick = [sb_setup(f"pick{i}", [P, NT, E]) for i in range(2)]
        both = sb_setup("both", [P, NT, E], BF16)
        top = [sb_setup(f"top{i}", [P, NT]) for i in range(2)]
        first = [sb_setup(f"first{i}", [P, NT]) for i in range(2)]
        gap = sb_setup("gap", [P, NT])
        egap = sb_setup("egap", [P, NT])
        esum = sb_setup("esum", [P, NT])
        tot = sb_setup("tot", [P, E, NT])
        run = sb_setup("run", [P, E, NT])
        more = sb_setup("more", [P, E, NT])
        n_tiles = sb_setup("n_tiles", [P, E])
        end_tile = sb_setup("end_tile", [P, E])
        off = sb_setup("off", [P, E])
        off_all = sb_setup("off_all", [P, E, NT])
        posn = lg2
        pos_u = sb_setup("pos_u", [P, 2, NT], U32)
        hi_u = sb_setup("hi_u", [P, 2, NT], U32)
        lo_u = sb_setup("lo_u", [P, 2, NT], U32)
        hi = sb_setup("hi", [P, 2, NT])
        lo = sb_setup("lo", [P, 2, NT])
        scratch = sb_setup("scratch", [P, MT * E])
        ended = scratch[:, :].rearrange("p (s e) -> p s e", e=E)
        ln_sq = scratch[:, 0:8 * D].rearrange("p (j d) -> p j d", d=D)
        owner = sb_setup("owner", [P, MT])
        owner_p = sb_setup("owner_p", [P, MT + 8])
        owner_s = tot[:, :, :].rearrange("p e j -> p (e j)")[:, 0:MT // 8 * 2 * OW].rearrange(
            "p (t w k) -> p t w k", w=2, k=OW)
        word_f = sb_setup("word_f", [P, MT // 8, 2])
        nibble = sb_setup("nibble", [P, OW])
        is_lane = [sb_setup(f"is_lane{i}", [P, GRP, P]) for i in range(2)]
        is_tile = [sb_setup(f"is_tile{i}", [P, GRP, MT]) for i in range(2)]
        tok_tile = [sb_setup(f"tok_tile{i}", [P, GRP, MT]) for i in range(2)]
        setup_only.close()

        raw = sb("raw", [P, 3, NB, WIN])
        conv = sb("conv", [P, 3, NB, P])
        xcT = [sb(f"xcT{i}", [P, 2, NB, P]) for i in range(2)]
        BT = [sb(f"BT{i}", [P, P]) for i in range(2)]
        CT = [sb(f"CT{i}", [P, P]) for i in range(2)]
        zT = [sb(f"zT{i}", [P, 2, NB, P]) for i in range(2)]
        dt_now = [sb(f"dt_now{i}", [P, NB, NH]) for i in range(2)]
        xdt = [sb(f"xdt{i}", [P, NB, NH, HD]) for i in range(2)]
        Bt = [sb(f"Bt{i}", [P, P]) for i in range(2)]
        L = [sb(f"L{i}", [P, NB, NH * P]) for i in range(2)]
        M = [sb(f"M{i}", [P, NB, NH * P]) for i in range(2)]
        xend = [sb(f"xend{i}", [P, NB, NH, HD]) for i in range(2)]
        CP = [sb(f"CP{i}", [P, NH, P]) for i in range(2)]
        H = [sb(f"H{i}", [P, NH * HD]) for i in range(2)]
        Hm = sb("Hm", [P, NH * HD])
        yD = sb("yD", [P, 2, NB, P])
        yg = [sb(f"yg{i}", [P, 2, NB, P]) for i in range(2)]
        ysq = [sb(f"ysq{i}", [P, 2, NB, P]) for i in range(2)]
        ms = [sb(f"ms{i}", [P, NB]) for i in range(2)]
        rs = [sb(f"rs{i}", [P, NB]) for i in range(2)]
        c_idx = [sb(f"c_idx{i}", [P, 2, NB], U32) for i in range(2)]
        c_mix = [sb(f"c_mix{i}", [P, 2, NB]) for i in range(2)]
        c_row = [sb(f"c_row{i}", [P, 2, NB, D]) for i in range(2)]
        acc = [sb(f"acc{i}", [P, NB, D]) for i in range(2)]
        y_g = [sb(f"y_g{i}", [P, D]) for i in range(RY)]

        bank = [ctx.enter_context(nc.psum_tensor(f"bank{i}", [P, 512], F32)) for i in range(8)]

        names = """c_done const_ok w_in x_in0 x_in1 x_in2 x_in3 vec_in gb_in e_in0 e_in1 ln_sum ln_c ln_v ln_act ln_pool
            xn_ok xn_st res_ok swt_ok sev_ok xT_ok xTe_ok lg_ok eT_ok eTe_ok a_ok r_dve r_act r_pe
            both_ok cum_ok oh_ok tk_ok tok_ok own_ok dtT_ok rows_ok rows_st pos_ok dtn_ok dtw_ok dta_ok gap_ok word_ok
            """.split()
        S = {n: sem(n) for n in names}
        x_in = [S[f"x_in{i}"] for i in range(4)]
        m_idx, m_x, m_t, m_xt, m_h, m_up, m_hid, m_ht, m_hte, m_y, m_sq, m_eps, m_rs, m_g, m_o = (
            sem(n) for n in ("m_idx", "m_x", "m_t", "m_xt", "m_h", "m_up", "m_hid", "m_ht", "m_hte",
                             "m_y", "m_sq", "m_eps", "m_rs", "m_g", "m_o"))
        m_xg = [sem(f"m_xg{i}") for i in range(RG)]
        m_st = [sem(f"m_st{i}") for i in range(R)]
        s_dec = [sem(f"s_dec{i}") for i in range(2)]
        s_pre = [sem(f"s_pre{i}") for i in range(2)]
        s_row = [sem(f"s_row{i}") for i in range(2)]
        s_sto = [sem(f"s_sto{i}") for i in range(2)]
        (s_px, s_pz, s_raw, s_t0, s_z, s_cv, s_sx, s_sbc, s_tr, s_g, s_dtn, s_xdt, s_bt, s_sc, s_m,
         s_cp, s_xe, s_hm, s_s, s_ha, s_y, s_yD, s_yg, s_sq, s_o, s_ms, s_mp, s_rs, s_ci, s_cm,
         s_f, s_f0, s_g0, s_y0) = (sem("s_" + n) for n in (
             "px", "pz", "raw", "t0", "z", "cv", "sx", "sbc", "tr", "g", "dtn", "xdt", "bt", "sc",
             "m", "cp", "xe", "hm", "s", "ha", "y", "yD", "yg", "sq", "o", "ms", "mp", "rs", "ci",
             "cm", "f", "f0", "g0", "y0"))

        x_v = X.rearrange("b (j p) d -> p (b j) d", p=P)
        xn_v = xn_rows.rearrange("(j p) d -> p j d", p=P)
        out_v = out.rearrange("b (j p) d -> p b j d", p=P)
        xnT_b = xnT[:, :].rearrange("d (b n) -> d b n", b=NB)
        pos_bj = pos[:, :, :].rearrange("p s (b j) -> p s b j", b=NB)
        mix_bj = mix[:, :, :].rearrange("p s (b j) -> p s b j", b=NB)
        dt_bj = dt[:, :, :].rearrange("p (b j) h -> p b j h", b=NB)
        res_bj = x[:, :, :].rearrange("p (b j) d -> p b j d", b=NB)
        LG = 8
        NG = NT // LG
        small_ps = [bank[4 + i][:, 0:16 * (NH + E)].rearrange("p (j n) -> p j n", j=16) for i in range(2)]

        def read_owners(eng, words, t, w):
            if t < MT // RG:
                words[t, w] = eng.value_load(owner_w[0:1, t:t + 1, w], min_val=0, max_val=16 ** OW - 1)

        def read_ahead(eng, words, s):
            if s % RG >= RG - 2:
                read_owners(eng, words, s // RG + 1, s % RG - (RG - 2))

        def expert_of(words, s, ago):
            t = min(s // RG, MT // RG - 1)
            if s - ago - t * RG < -OB:
                t -= 1
            w, k = divmod(s - ago - t * RG + OB, OW)
            return (words[t, w] >> 4 * k) & 15

        def proj_ps(k):
            return bank[k][:, 0:NB * WIN].rearrange("p (b n) -> p b n", b=NB)

        def evac_tokens(act, A, g):
            act.wait_ge(S["xT_ok"], g + 1)
            b, at = g // 4, (g % 4) * 512
            A(xnT[:, b * XB + HALO + at:b * XB + HALO + at + 512], bank[2 + g % 2][:, :], ACT.Copy).then_inc(S["xTe_ok"], 1)

        bank_h, bank_x, bank_t, bank_y = bank[0:2], bank[2:4], bank[4:6], bank[6:8]

        block = ctx.enter_context(nc.Block())

        def decay_load(sp, c, q):
            at = [c * (NH * P) + b * NC * NH * P for b in range(NB)]
            pairs = c - 1
            if not isinstance(c, int):
                pairs, at = sp.snap(pairs), [sp.snap(a) for a in at]
            at_least(sp, s_hm, pairs)
            for b in range(NB):
                sp.dma_start(bc_decay[q][:, b, :],
                             decay_rows[bass.ds(at[b], NH * P)].partition_broadcast(P)).then_inc(s_dec[q], 16)
                sp.dma_start(bc_prefix[q][b * NS:(b + 1) * NS, :, :].rearrange("p h i -> p (h i)"),
                             prefix_rows[bass.ds(at[b], NH * P)].partition_broadcast(NS)).then_inc(s_pre[q], 16)

        def result_store(sp, c, q):
            sums = 4 * c + 4
            if not isinstance(c, int):
                c, sums = sp.snap(c), sp.snap(sums)
            sp.wait_ge(s_f, sums)
            sp.dma_start(out_v[:, :, bass.ds(c, 1), :].rearrange("p b j d -> p b (j d)"),
                         acc[q][:, :, :]).then_inc(s_sto[q], 16)

        @block.sync
        def _(sp):
            for g in range(NG):
                sp.dma_start(x[:, g * LG:(g + 1) * LG, :], x_v[:, g * LG:(g + 1) * LG, :]).then_inc(x_in[g], 16)
                if g == 0:
                    sp.dma_start(win_st[:, :, :], W_in[0:ZX, :].rearrange("(j p) d -> p j d", p=P)).then_inc(S["w_in"], 16)
                    sp.dma_start(dt_st[:, :], W_in[ZX:ZX + NH, :]).then_inc(S["w_in"], 16)
                    sp.dma_start(rt_st[:, :], router_w).then_inc(S["w_in"], 16)
                    sp.dma_start(wo_st[:, :], W_out).then_inc(S["w_in"], 16)
            for e in range(E):
                q = e % 2
                at_least(sp, S["eT_ok"], 2 * (e - 1))
                sp.dma_start(ex_st[q][:, 0:2, :], w1[e].rearrange("(c p) d -> p c d", p=P)).then_inc(S[f"e_in{q}"], 16)
                sp.dma_start(ex_st[q][:, 2:4, :], w3[e].rearrange("(c p) d -> p c d", p=P)).then_inc(S[f"e_in{q}"], 16)
                sp.dma_start(ex_st[q][:, 4:6, :].rearrange("p c n -> p (c n)"), w2[e]).then_inc(S[f"e_in{q}"], 16)
                if e < NG:
                    sp.wait_ge(S["xn_ok"], e + 1)
                    sp.dma_start(xn_v[:, e * LG:(e + 1) * LG, :], xn[:, e * LG:(e + 1) * LG, :]).then_inc(S["xn_st"], 16)
            sp.wait_ge(S["rows_ok"], 2)
            sp.dma_start(decay_rows.rearrange("(r i) -> r i", i=P), decayT[:, :]).then_inc(S["rows_st"], 16)
            sp.dma_start(prefix_rows.rearrange("(r i) -> r i", i=P), prefixT[:, :]).then_inc(S["rows_st"], 16)
            sp.wait_ge(S["rows_st"], 32)
            decay_load(sp, 0, 0)
            decay_load(sp, 1, 1)

            def tile_store(s, j):
                sp.wait_ge(m_o, s + 1)
                sp.dma_start(y_rows[s * P:(s + 1) * P, :], y_o[j][:, :]).then_inc(m_st[j], 16)

            for s in range(MT):
                tile_store(s, s % R)
            decay_load(sp, 2, 0)
            with sp.Fori(0 // 2, (NC - 4) // 2) as turn_no:
                c0 = turn_no * 2
                for q in range(2):
                    decay_load(sp, c0 + q + 3, 1 - q)
                    result_store(sp, c0 + q, q)
            decay_load(sp, NC - 1, 1)
            for c in range(NC - 4, NC):
                result_store(sp, c, c % 2)
            for q in range(2):
                sp.wait_ge(s_sto[q], 16 * (NC // 2))

        @block.gpsimd
        def _(pool):
            pool.memset(ident[:, :], 0.0)
            pool.memset(eye4[:, :, :], 0.0)
            pool.memset(centre[:, :], -1.0 / D)
            pool.memset(before[:, :], 1.0)
            pool.memset(ones_bf[:, :], 1.0)
            pool.memset(ones[:, :], 1.0)
            pool.memset(zeros[:, :], 0.0)
            pool.memset(half[:, :], -0.5)
            for k in range(OW):
                pool.memset(nibble[:, k:k + 1], float(16 ** k))
            pool.memset(eps_col[:, :], EPS)
            pool.memset(restart[:, :, :], 1.0)
            pool.memset(xnT_b[:, :, 0:HALO], 0.0).then_inc(S["c_done"], 1)
            pool.wait_ge(S["c_done"], 1)
            pool.affine_select(out=ident[:, :], in_=ident[:, :], compare_op=ALU.not_equal, fill=1.0,
                               base=0, pattern=[[-1, P]], channel_multiplier=1)
            pool.affine_select(out=eye4[:, :, :], in_=eye4[:, :, :], compare_op=ALU.not_equal, fill=1.0,
                               base=0, pattern=[[0, NH], [-1, P]], channel_multiplier=1)
            pool.affine_select(out=centre[:, :], in_=centre[:, :], compare_op=ALU.not_equal, fill=1.0 - 1.0 / D,
                               base=0, pattern=[[-1, P]], channel_multiplier=1)
            pool.affine_select(out=before[:, :], in_=before[:, :], compare_op=ALU.is_gt, fill=0.0,
                               base=0, pattern=[[1, P]], channel_multiplier=-1)
            pool.memset(restart[:, :, 0:1], 0.0)

            def count(ap, base, pattern, by=0):
                return pool.iota(ap, pattern=pattern, base=base, channel_multiplier=by,
                                 allow_small_or_imprecise_dtypes=True)

            count(rev_e[:, :], E, [[-1, E]])
            count(steps128[:, :], 0, [[P, NT]])
            count(lane[:, :], 0, [[1, P]])
            count(tile_no[:, :], 0, [[1, MT]])
            count(token_id[:, :], 0, [[P, NT]], 1).then_inc(S["const_ok"], 1)
            pool.dma_start(g_all[:, :], ln_g.rearrange("e d -> (e d)").partition_broadcast(P)).then_inc(S["gb_in"], 16)
            pool.dma_start(b_all[:, :], ln_b.rearrange("e d -> (e d)").partition_broadcast(P)).then_inc(S["gb_in"], 16)

            for g in range(NG):
                t = slice(g * LG, (g + 1) * LG)
                pool.wait_ge(S["ln_v"], g + 1)
                pool.tensor_scalar(var[:, t], var[:, t], 1.0 / D, EPS, ALU.mult, ALU.add).then_inc(S["ln_pool"], 1)
                pool.wait_ge(S["ln_pool"], 2 * g + 1)
                pool.tensor_tensor(rstd[:, t], var[:, t], half[:, t], ALU.pow).then_inc(S["ln_pool"], 1)
            for g in range(NG):
                t = slice(g * LG, (g + 1) * LG)
                pool.wait_ge(S["xn_ok"], g + 1)
                pool.tensor_tensor(x[:, t, :], x[:, t, :], xn[:, t, :], ALU.add).then_inc(S["res_ok"], 1)

            pool.wait_ge(S["xn_st"], 16 * NG)

            def gather(s, j):
                pool.indirect_dma_start(out=xg[j][:, :], out_offset=None, in_=xn_rows,
                                        in_offset=bass.IndirectOffsetOnAxis(ap=g_idx[j][:, 0:1], axis=0)
                                        ).then_inc(m_xg[j], 16)

            def step(s, j):
                ahead = min(2, MT - (s + 6))
                if ahead > 0:
                    pool.wait_ge(m_idx, s + 6 + ahead)
                    at_least(pool, m_t, s)
                for k in range(ahead):
                    gather(s + 6 + k, (j + 6 + k) % RG)
                if s >= 2:
                    f = (j - 2) % RY
                    at_least(pool, m_o, s - RY)
                    pool.wait_ge(m_eps, s)
                    pool.tensor_tensor(y_rs[:, f:f + 2], y_mse[:, f:f + 2], half[:, 0:2], ALU.pow).then_inc(m_rs, 2)

            pool.wait_ge(m_idx, 6)
            for s in range(6):
                gather(s, s)
            for s in range(0, MT + 1, 2):
                step(s, s % RG)

            def mixer_step(c, q, now=True, update=True, prev=True, prev2=True):
                if now:
                    pool.wait_ge(s_sbc, c + 1)
                    pool.wait_ge(s_pre[q], 16 * (c - q) + 32)
                    at_least(pool, s_y, c - 1)
                    pool.tensor_tensor(CP[q][:, :, :], along(CT[q][:, :], 1, NH), bc_prefix[q][:, :, :],
                                       ALU.mult).then_inc(s_cp, 1)
                if prev2:
                    pool.wait_ge(s_ms, c - 1)
                    pool.tensor_tensor(rs[q][:, :], ms[q][:, :], half[:, 0:NB], ALU.pow).then_inc(s_rs, 1)
                if update:
                    pool.wait_ge(s_sc, 2 * c + 2)
                    pool.wait_ge(s_xdt, c + 1)
                    at_least(pool, s_s, c - 1)
                    last = L[q][:, :, :].rearrange("p b (h i) -> p (b h) i", i=P)[:, :, P - 1]
                    pool.tensor_tensor(xend[q][:, :, :, :].rearrange("p b h e -> p (b h) e"),
                                       xdt[q][:, :, :, :].rearrange("p b h e -> p (b h) e"),
                                       along(last, 2, HD), ALU.mult).then_inc(s_xe, 1)
                if prev:
                    pool.wait_ge(s_ci, c)
                    at_least(pool, s_f, 4 * (c - 2))
                if update:
                    pool.wait_ge(s_ha, c + 1)
                    pool.tensor_tensor(Hm[:, :].rearrange("p (h e) -> p h e", h=NH),
                                       H[q][:, :].rearrange("p (h e) -> p h e", h=NH),
                                       along(bc_prefix[q][:, :, P - 1], 2, HD), ALU.mult).then_inc(s_hm, 1)
                if prev:
                    o = 1 - q
                    for s in range(2):
                        for b in range(NB):
                            pool.indirect_dma_start(out=c_row[o][:, s, b, :], out_offset=None, in_=y_rows,
                                                    in_offset=bass.IndirectOffsetOnAxis(ap=c_idx[o][:, s, b:b + 1], axis=0)
                                                    ).then_inc(s_row[o], 16)

            for q in range(R):
                pool.wait_ge(m_st[q], 16 * (MT // R))
            mixer_step(0, 0, prev=False, prev2=False)
            mixer_step(1, 1, prev2=False)
            with pool.Fori(2 // 2, (NC - 2) // 2) as turn_no:
                c0 = turn_no * 2
                for q in range(2):
                    mixer_step(c0 + q, q)
            mixer_step(NC - 2, 0)
            mixer_step(NC - 1, 1, update=False)
            mixer_step(NC, 0, now=False, update=False)
            mixer_step(NC + 1, 1, now=False, update=False, prev=False)

        @block.scalar
        def _(act):
            A = nc.scalar.activation
            for ap, src in ((dtb[:, :], dt_bias.partition_broadcast(P)), (a_log[:, :], A_log.partition_broadcast(P)),
                            (rb[:, :], router_b.partition_broadcast(P)),
                            (cw[:, :, :], conv_w.rearrange("(c p) k -> p c k", p=P)),
                            (cb[:, :], conv_b.rearrange("(c p) -> p c", p=P)),
                            (nw[:, :], norm_w.rearrange("(c p) -> p c", p=P))):
                with nc.allow_non_contiguous_dma(reason="a few small vectors, once"):
                    act.dma_start(ap, src).then_inc(S["vec_in"], 16)
            for h in range(NH):
                act.dma_start(dskip[(h % 2) * HD:(h % 2 + 1) * HD, h // 2:h // 2 + 1],
                              Dskip[h:h + 1].partition_broadcast(HD)).then_inc(S["vec_in"], 16)
            act.wait_ge(S["vec_in"], 16 * 10)
            A(a_exp[:, :], a_log[:, :], ACT.Exp).then_inc(S["a_ok"], 1)
            act.wait_ge(S["swt_ok"], 1)
            A(winT[:, 0:512], bank[0][:, :], ACT.Copy)
            A(winT[:, 512:640], bank[1][:, 0:128], ACT.Copy)
            A(smallT[:, :], bank[1][:, 128:128 + NH + E], ACT.Copy).then_inc(S["sev_ok"], 1)
            for c in range(2):
                A(woT[:, c, :], bank[1][:, 256 + c * P:256 + (c + 1) * P], ACT.Copy,
                  scale=nw[:, c:c + 1]).then_inc(S["sev_ok"], 1)
            for g in range(NG):
                act.wait_ge(S["ln_c"], g + 1)
                at_least(act, S["ln_v"], g)
                A(ln_sq[:, :, :], xn[:, g * LG:(g + 1) * LG, :], ACT.Square).then_inc(S["ln_act"], 1)
                if g >= 1:
                    evac_tokens(act, A, 2 * (g - 1))
                    evac_tokens(act, A, 2 * (g - 1) + 1)
            evac_tokens(act, A, 2 * NG - 2)
            evac_tokens(act, A, 2 * NG - 1)

            act.wait_ge(S["dtn_ok"], 1)
            A(dt_u[:, :, :], dt_n[:, :, :], ACT.Exp).then_inc(S["r_act"], 1)
            act.wait_ge(S["dtw_ok"], 1)
            A(dt_l[:, :, :], dt_w[:, :, :], ACT.Ln).then_inc(S["r_act"], 1)
            act.wait_ge(S["gap_ok"], 1)
            A(egap[:, :], gap[:, :], ACT.Exp).then_inc(S["r_act"], 1)
            act.wait_ge(S["dta_ok"], 1)
            A(decay[:, :, :], dt_a[:, :, :], ACT.Exp).then_inc(S["r_act"], 1)

            for e in range(E):
                q = e % 2
                act.wait_ge(S["eT_ok"], 2 * e + 1)
                A(w13T[:, e * 2 * F:(e + 1) * 2 * F], bank[6 + q][:, :], ACT.Copy).then_inc(S["eTe_ok"], 1)
                act.wait_ge(S["eT_ok"], 2 * e + 2)
                A(w2T[:, e * F:(e + 1) * F], bank[2 + q][:, 0:F], ACT.Copy).then_inc(S["eTe_ok"], 1)

            act.wait_ge(S["tok_ok"], 1)

            def idx(s, j):
                if s >= RG:
                    act.wait_ge(m_xg[j], 2 * (s - j))
                A(g_idx[j][:, 0:1], tok[:, bass.ds(s, 1)], ACT.Copy).then_inc(m_idx, 1)

            def silu(s, j):
                act.wait_ge(m_h, s + 1)
                at_least(act, m_hid, s - 1)
                A(up[j % 2][:, :], bank_h[j % 2][:, 0:F], ACT.Silu).then_inc(m_up, 1)

            def hidden_out(s, j):
                act.wait_ge(m_ht, s + 1)
                at_least(act, m_y, s - 1)
                A(hidT[j % 2][:, :, :].rearrange("p c n -> p (c n)"), bank_t[j % 2][:, 0:F], ACT.Copy).then_inc(m_hte, 1)

            def square(s, j):
                act.wait_ge(m_y, s + 1)
                at_least(act, m_eps, s - RY + 1)
                A(y_sq[j % 2][:, :], bank_y[j % 2][:, 0:D], ACT.Square, scale=D ** -0.5,
                  accum_out=y_ms[:, j:j + 1]).then_inc(m_sq, 1)

            def with_eps(s, j):
                act.wait_ge(m_sq, s + 2)
                at_least(act, m_rs, s - RY + 2)
                A(y_mse[:, j:j + 2], y_ms[:, j:j + 2], ACT.Identity, bias=eps_col[:, 0:1]).then_inc(m_eps, 2)

            for s in range(RG):
                idx(s, s)

            def step(s, j):
                if s + 1 < MT:
                    silu(s + 1, (j + 1) % R)
                if 0 <= s < MT:
                    hidden_out(s, j % R)
                if 1 <= s <= MT:
                    square(s - 1, (j - 1) % RY)
                if 3 <= s and s % 2 == 1:
                    with_eps(s - 3, (j - 3) % RY)
                if 0 <= s and s + RG < MT:
                    idx(s + RG, j)

            for s in range(-1, MT + 2):
                step(s, s % RG)

            def project_out(n, o):
                at_least(act, s_cv, 9 * n)
                for k in range(3):
                    act.wait_ge(s_px, 3 * n + k + 1)
                    A(raw[:, k, :, :], proj_ps(k), ACT.Copy).then_inc(s_raw, 1)
                at_least(act, s_sx, n)
                at_least(act, s_sbc, n)
                for k in range(3):
                    A(conv[:, k, :, :], proj_ps(k)[:, :, 0:P], ACT.Identity, bias=cb[:, k:k + 1],
                      scale=cw[:, k, 0:1]).then_inc(s_t0, 1)
                act.wait_ge(s_pz, n + 1)
                at_least(act, s_yg, n - 1)
                A(zT[o][:, :, :, :].rearrange("p c b i -> p (c b i)"), bank[3][:, :], ACT.Silu).then_inc(s_z, 1)

            def conv_out(n, o):
                act.wait_ge(s_cv, 9 * n + 9)
                at_least(act, s_tr, n - 1)
                at_least(act, s_yD, 2 * (n - 1))
                A(xcT[o][:, :, :, :], conv[:, 0:2, :, :], ACT.Silu).then_inc(s_sx, 1)
                at_least(act, s_g, n - 1)
                at_least(act, s_cp, n - 1)
                for b in range(NB):
                    A(BT[o][b * NS:(b + 1) * NS, :], conv[0:NS, 2, b, :], ACT.Silu)
                    ins = A(CT[o][b * NS:(b + 1) * NS, :], conv[NS:2 * NS, 2, b, :], ACT.Silu)
                ins.then_inc(s_sbc, 1)

            def mixer_step(c, q, now=True, nxt=True, prev=True):
                o = 1 - q
                if now:
                    at_least(act, s_xdt, c - 1)
                    A(dt_now[q][:, :, :], dt_bj[:, :, bass.ds(c, 1), :].rearrange("p b j h -> p b (j h)"),
                      ACT.Copy).then_inc(s_dtn, 1)
                    act.wait_ge(s_dtn, c + 1)
                    act.wait_ge(s_tr, c + 1)
                    at_least(act, s_y, c - 1)
                    at_least(act, s_xe, c - 1)
                    at_least(act, s_s, c - 1)
                    A(Bt[q][:, :], bank[2][:, 384:512], ACT.Copy).then_inc(s_bt, 1)
                    for b in range(NB):
                        for h in range(NH):
                            ins = A(xdt[q][:, b, h, :], bank[4][:, b * DI + h * HD:b * DI + (h + 1) * HD],
                                    ACT.Copy, scale=dt_now[q][:, b, h:h + 1])
                    ins.then_inc(s_xdt, 1)
                if prev:
                    if not (isinstance(c, int) and c < 3):
                        act.wait_ge(s_row[o], 32 * (c - 1 - o))
                        act.wait_ge(s_f, 4 * (c - 2))
                    A(c_idx[o][:, :, :], pos_bj[:, :, :, bass.ds(c - 1, 1)].rearrange("p s b j -> p s (b j)"),
                      ACT.Copy).then_inc(s_ci, 1)
                    A(c_mix[o][:, :, :], mix_bj[:, :, :, bass.ds(c - 1, 1)].rearrange("p s b j -> p s (b j)"),
                      ACT.Copy).then_inc(s_cm, 1)
                if nxt:
                    project_out(c + 1, o)
                if prev:
                    act.wait_ge(s_yg, c)
                    at_least(act, s_o, c - 2)
                    A(ysq[o][:, :, :, :], yg[o][:, :, :, :], ACT.Square).then_inc(s_sq, 1)
                if nxt:
                    conv_out(c + 1, o)
                if prev:
                    act.wait_ge(s_o, c)
                    at_least(act, s_rs, c - 2)
                    A(ms[o][:, :], bank[3][:, 256:256 + NB], ACT.Identity, bias=eps_col[:, 0:1],
                      scale=1.0 / DI).then_inc(s_ms, 1)

            act.wait_ge(S["pos_ok"], 1)
            act.wait_ge(S["own_ok"], 1)
            mixer_step(-1, 1, now=False, prev=False)
            mixer_step(0, 0, prev=False)
            mixer_step(1, 1)
            with act.Fori(2 // 2, (NC - 2) // 2) as turn_no:
                c0 = turn_no * 2
                for q in range(2):
                    mixer_step(c0 + q, q)
            mixer_step(NC - 2, 0)
            mixer_step(NC - 1, 1, nxt=False)
            mixer_step(NC, 0, now=False, nxt=False)


        @block.vector
        def _(dve):
            V = nc.vector
            chain = [0]

            def link(ins):
                chain[0] += 1
                ins.then_inc(S["r_dve"], 1)
                dve.wait_ge(S["r_dve"], chain[0])

            for g in range(NG + 2):
                if g < NG:
                    t = slice(g * LG, (g + 1) * LG)
                    dve.wait_ge(x_in[g], 16)
                    V.reduce_sum(mean[:, t], x[:, t, :], AX.X).then_inc(S["ln_sum"], 1)
                    dve.wait_ge(S["ln_sum"], g + 1)
                    V.scalar_tensor_tensor(xn[:, t, :], along(mean[:, t], 2, D), -1.0 / D, x[:, t, :],
                                           ALU.mult, ALU.add).then_inc(S["ln_c"], 1)
                if 1 <= g <= NG:
                    dve.wait_ge(S["ln_act"], g)
                    V.reduce_sum(var[:, (g - 1) * LG:g * LG], ln_sq[:, :, :], AX.X).then_inc(S["ln_v"], 1)
                if g >= 2:
                    t = slice((g - 2) * LG, (g - 1) * LG)
                    dve.wait_ge(S["ln_pool"], 2 * (g - 1))
                    V.tensor_tensor(xn[:, t, :], xn[:, t, :], along(rstd[:, t], 2, D), ALU.mult).then_inc(S["xn_ok"], 1)

            dve.wait_ge(S["vec_in"], 16 * 10)
            dve.wait_ge(S["const_ok"], 1)
            for i in range(2):
                dve.wait_ge(S["lg_ok"], i + 1)
                j = slice(16 * i, 16 * i + 16)
                V.tensor_tensor(dt_v[:, j, :], small_ps[i][:, :, 0:NH], along(dtb[:, :], 1, 16), ALU.add)
                link(V.tensor_tensor(lg[:, j, :], small_ps[i][:, :, NH:NH + E], along(rb[:, :], 1, 16), ALU.add))
            V.scalar_tensor_tensor(dt_n[:, :, :], dt_v[:, :, :], -1.0, dt_v[:, :, :], ALU.mult,
                                   ALU.min).then_inc(S["dtn_ok"], 1)
            logits = lg
            for s in range(2):
                link(V.reduce_max(top[s][:, :], logits[:, :, :], AX.X))
                link(V.tensor_tensor(key[:, :, :], logits[:, :, :], along(top[s][:, :], 2, E), ALU.is_equal))
                link(V.tensor_tensor(key[:, :, :], key[:, :, :], along(rev_e[:, :], 1, NT), ALU.mult))
                link(V.reduce_max(first[s][:, :], key[:, :, :], AX.X))
                link(V.tensor_tensor(pick[s][:, :, :], along(rev_e[:, :], 1, NT), along(first[s][:, :], 2, E),
                                     ALU.is_equal))
                if s == 0:
                    link(V.scalar_tensor_tensor(lg2[:, :, :], pick[0][:, :, :], -1e30, lg[:, :, :], ALU.mult, ALU.add))
                    logits = lg2
                    dve.wait_ge(S["r_act"], 1)
                    V.tensor_scalar(dt_w[:, :, :], dt_u[:, :, :], 1.0, None, ALU.add).then_inc(S["dtw_ok"], 1)
            V.tensor_tensor(both[:, :, :], pick[0][:, :, :], pick[1][:, :, :], ALU.add).then_inc(S["both_ok"], 1)
            V.tensor_tensor(gap[:, :], top[1][:, :], top[0][:, :], ALU.subtract).then_inc(S["gap_ok"], 1)

            dve.wait_ge(S["dtw_ok"], 1)
            dve.wait_ge(S["r_act"], 2)
            V.reciprocal(dt_r[:, :, :], dt_w[:, :, :])
            link(V.tensor_scalar(dt_c[:, :, :], dt_w[:, :, :], -1.0, None, ALU.add))
            link(V.tensor_tensor(dt_d[:, :, :], dt_u[:, :, :], dt_c[:, :, :], ALU.subtract))
            link(V.tensor_tensor(dt_e[:, :, :], dt_d[:, :, :], dt_r[:, :, :], ALU.mult))
            link(V.tensor_tensor(dt_d[:, :, :], dt_e[:, :, :], dt_l[:, :, :], ALU.add))
            link(V.scalar_tensor_tensor(dt[:, :, :], dt_v[:, :, :], 0.0, dt_d[:, :, :], ALU.max, ALU.add))
            dve.wait_ge(S["a_ok"], 1)
            V.scalar_tensor_tensor(dt_a[:, :, :], dt[:, :, :], -1.0, along(a_exp[:, :], 1, NT), ALU.mult,
                                   ALU.mult).then_inc(S["dta_ok"], 1)

            dve.wait_ge(S["cum_ok"], 1)
            link(V.tensor_copy(tot[:, :, :], bank[1][:, :].rearrange("p (j e) -> p e j", e=E)))
            flat = lambda ap: ap[:, :, :].rearrange("p a b -> p (a b)")
            link(V.tensor_tensor_scan(flat(run), flat(restart), flat(tot), 0.0, ALU.mult, ALU.add))
            link(V.tensor_tensor(more[:, :, :], along(run[:, :, NT - 1], 2, NT), along(steps128[:, :], 1, E), ALU.is_gt))
            link(V.reduce_sum(n_tiles[:, :], more[:, :, :], AX.X))
            link(V.tensor_tensor_scan(end_tile[:, :], ones[:, 0:E], n_tiles[:, :], 0.0, ALU.mult, ALU.add))
            V.tensor_tensor(more[:, :, :], run[:, :, :], tot[:, :, :], ALU.subtract)
            link(V.tensor_tensor(off[:, :], end_tile[:, :], n_tiles[:, :], ALU.subtract))
            link(V.scalar_tensor_tensor(off_all[:, :, :], along(off[:, :], 2, NT), float(P), more[:, :, :],
                                        ALU.mult, ALU.add))
            link(V.tensor_tensor(posn[:, :, :], bank[0][:, :].rearrange("p (j e) -> p j e", e=E),
                                 off_all[:, :, :].rearrange("p e j -> p j e"), ALU.add))
            for s in range(2):
                link(V.tensor_tensor(key[:, :, :], pick[s][:, :, :], posn[:, :, :], ALU.mult))
                link(V.reduce_sum(pos[:, s, :], key[:, :, :], AX.X))
            link(V.tensor_copy(pos_u[:, :, :], pos[:, :, :]))
            V.tensor_scalar(hi_u[:, :, :], pos_u[:, :, :], 7, None, ALU.logical_shift_right)
            link(V.tensor_scalar(lo_u[:, :, :], pos_u[:, :, :], P - 1, None, ALU.bitwise_and))
            V.tensor_copy(hi[:, :, :], hi_u[:, :, :])
            link(V.tensor_copy(lo[:, :, :], lo_u[:, :, :]))

            lo_f, hi_f = (t[:, :, :].rearrange("p s j -> p (s j)") for t in (lo, hi))
            for g in range(2 * NT // GRP):
                q, k, j = g % 2, g * GRP, g * GRP % NT
                at_least(dve, S["tk_ok"], g - 1)
                V.tensor_tensor(is_lane[q][:, :, :], along(lane[:, :], 1, GRP), along(lo_f[:, k:k + GRP], 2, P),
                                ALU.is_equal)
                link(V.tensor_tensor(is_tile[q][:, :, :], along(tile_no[:, :], 1, GRP),
                                     along(hi_f[:, k:k + GRP], 2, MT), ALU.is_equal))
                V.tensor_tensor(tok_tile[q][:, :, :], is_tile[q][:, :, :], along(token_id[:, j:j + GRP], 2, MT),
                                ALU.mult).then_inc(S["oh_ok"], 1)
            link(V.tensor_tensor(ended[:, :, :], along(end_tile[:, :], 1, MT), along(tile_no[:, :], 2, E), ALU.is_le))
            link(V.reduce_sum(owner[:, :], ended[:, :, :], AX.X))
            link(V.memset(owner_p[:, :], 0.0))
            link(V.tensor_scalar(owner_p[:, OB:OB + MT], owner[:, :], float(E - 1), None, ALU.min))
            for w in range(2):
                V.tensor_tensor(owner_s[:, :, w, :],
                                owner_p[:, w * OW:w * OW + MT].rearrange("p (t n) -> p t n", n=8)[:, :, 0:OW],
                                along(nibble[:, :], 1, MT // 8), ALU.mult).then_inc(S["word_ok"], 1)
            dve.wait_ge(S["word_ok"], 2)
            link(V.reduce_sum(word_f[:, :, :], owner_s[:, :, :, :], AX.X))
            V.tensor_copy(owner_w[:, :, :], word_f[:, :, :]).then_inc(S["own_ok"], 1)
            dve.wait_ge(S["r_act"], 3)
            link(V.tensor_scalar(esum[:, :], egap[:, :], 1.0, None, ALU.add))
            link(V.reciprocal(mix[:, 0, :], esum[:, :]))
            V.tensor_tensor(mix[:, 1, :], egap[:, :], mix[:, 0, :], ALU.mult).then_inc(S["pos_ok"], 1)
            dve.wait_ge(S["dtT_ok"], 1)
            V.tensor_tensor_scan(prefixT[:, :], bank[5][:, 384:512], zeros[:, :], 1.0, ALU.mult,
                                 ALU.add).then_inc(S["rows_ok"], 1)
            link(V.tensor_copy(decayT[:, :], bank[5][:, 384:512]))
            V.memset(decayT[:, 0:1], 0.0).then_inc(S["rows_ok"], 1)
            dve.wait_ge(S["tk_ok"], 2 * NT // GRP)
            V.tensor_copy(tok[:, :], bank[0][:, 0:MT]).then_inc(S["tok_ok"], 1)

            dve.wait_ge(S["gb_in"], 32)
            dve.wait_ge(S["own_ok"], 1)

            def x_out(s, j):
                dve.wait_ge(m_t, s + 1)
                at_least(dve, m_h, s - 3)
                V.tensor_copy(xgT[j][:, :], bank_x[j % 2][:, 0:P]).then_inc(m_xt, 1)

            def hidden(s, j):
                dve.wait_ge(m_up, s + 1)
                at_least(dve, m_ht, s - 1)
                V.tensor_tensor(hid[j % 2][:, :], up[j % 2][:, :], bank_h[j % 2][:, F:2 * F], ALU.mult).then_inc(m_hid, 1)

            def gained(s, j, e):
                at = dve.snap(e * D)
                dve.wait_ge(m_sq, s + 1)
                at_least(dve, m_o, s - RY + 1)
                V.tensor_tensor(y_g[j][:, :], bank_y[j % 2][:, 0:D], g_all[:, bass.ds(at, D)],
                                ALU.mult).then_inc(m_g, 1)

            def shifted(s, j, e):
                at = dve.snap(e * D)
                dve.wait_ge(m_rs, s + 1)
                dve.wait_ge(m_g, s + 1)
                o = j % R
                if s >= R:
                    dve.wait_ge(m_st[o], 4 * (s - o))
                V.scalar_tensor_tensor(y_o[o][:, :], y_g[j][:, :], y_rs[:, j:j + 1], b_all[:, bass.ds(at, D)],
                                       ALU.mult, ALU.add).then_inc(m_o, 1)

            def step(s, j):
                if s + 2 < MT:
                    x_out(s + 2, (j + 2) % R)
                if 0 <= s + 1 < MT:
                    hidden(s + 1, (j + 1) % R)
                if 0 <= s:
                    read_ahead(dve, words, s)
                if 2 <= s <= MT + 1:
                    gained(s - 2, (j - 2) % RY, expert_of(words, s, 2))
                if LAG <= s:
                    shifted(s - LAG, (j - LAG) % RY, expert_of(words, s, LAG))

            words = {}
            for w in range(2):
                read_owners(dve, words, 0, w)
            for s in range(-2, MT + LAG):
                step(s, s % RG)

            V.memset(H[0][:, :], 0.0).then_inc(s_ha, 1)

            def mask(c, q):
                dve.wait_ge(s_dec[q], 16 * (c - q) + 32)
                at_least(dve, s_xe, c - 1)
                for b in range(NB):
                    V.tensor_tensor_scan(L[q][:, b, :], bc_decay[q][:, b, :],
                                         eye4[:, :, :].rearrange("p h i -> p (h i)"), 0.0, ALU.mult,
                                         ALU.add).then_inc(s_sc, 1)
                dve.wait_ge(s_g, c + 1)
                at_least(dve, s_y, c - 1)
                for b in range(NB):
                    dve.wait_ge(s_sc, 2 * c + b + 1)
                    V.tensor_tensor(M[q][:, b, :].rearrange("p (h i) -> p h i", h=NH),
                                    L[q][:, b, :].rearrange("p (h i) -> p h i", h=NH),
                                    along(bank[5][:, b * P:(b + 1) * P], 1, NH), ALU.mult).then_inc(s_m, 1)

            def gate(c, q):
                dve.wait_ge(s_y, c + 1)
                for k in range(2):
                    V.scalar_tensor_tensor(yD[:, k, :, :], xcT[q][:, k, :, :], dskip[:, k:k + 1],
                                           bank[7][:, k * NB * P:(k + 1) * NB * P].rearrange("p (b i) -> p b i", b=NB),
                                           ALU.mult, ALU.add).then_inc(s_yD, 1)
                dve.wait_ge(s_z, c + 1)
                at_least(dve, s_o, c - 1)
                dve.wait_ge(s_yD, 2 * c + 2)
                V.tensor_tensor(yg[q][:, :, :, :], yD[:, :, :, :], zT[q][:, :, :, :], ALU.mult).then_inc(s_yg, 1)

            def taps(n):
                for t in range(1, KC):
                    for k in range(3):
                        if t == 1:
                            dve.wait_ge(s_t0, 3 * n + k + 1)
                        else:
                            dve.wait_ge(s_cv, 9 * n + 3 * (t - 2) + k + 1)
                        V.scalar_tensor_tensor(conv[:, k, :, :], raw[:, k, :, t:t + P], cw[:, k, t:t + 1],
                                               conv[:, k, :, :], ALU.mult, ALU.add).then_inc(s_cv, 1)

            def state(c, q):
                dve.wait_ge(s_s, c + 1)
                dve.wait_ge(s_hm, c + 1)
                at_least(dve, s_y, c)
                V.tensor_tensor(H[1 - q][:, :], Hm[:, :], bank[6][:, 0:NH * HD], ALU.add).then_inc(s_ha, 1)

            def scaled(c, q):
                dve.wait_ge(s_rs, c + 1)
                if not (isinstance(c, int) and c < 2):
                    dve.wait_ge(s_sto[q], 8 * (c - q))
                for b in range(NB):
                    V.scalar_tensor_tensor(acc[q][:, b, :], bank[3][:, b * D:(b + 1) * D], rs[q][:, b:b + 1],
                                           res_bj[:, b, bass.ds(c, 1), :].rearrange("p j d -> p (j d)"),
                                           ALU.mult, ALU.add).then_inc(s_f0, 1)

            def combined(c, q):
                dve.wait_ge(s_cm, c + 1)
                dve.wait_ge(s_row[q], 32 * (c - q) + 64)
                for s in range(2):
                    for b in range(NB):
                        if s == 0:
                            dve.wait_ge(s_f0, 2 * c + b + 1)
                        else:
                            dve.wait_ge(s_f, 4 * c + b + 1)
                        V.scalar_tensor_tensor(acc[q][:, b, :], c_row[q][:, s, b, :], c_mix[q][:, s, b:b + 1],
                                               acc[q][:, b, :], ALU.mult, ALU.add).then_inc(s_f, 1)

            def mixer_step(c, q, now=True, nxt=True, prev=True, prev2=True, update=True):
                if now:
                    mask(c, q)
                if prev2:
                    scaled(c - 2, q)
                if prev:
                    gate(c - 1, 1 - q)
                if nxt:
                    taps(c + 1)
                if update:
                    state(c, q)
                if prev2:
                    combined(c - 2, q)

            dve.wait_ge(S["res_ok"], NG)
            mixer_step(-1, 1, now=False, prev=False, prev2=False, update=False)
            mixer_step(0, 0, prev=False, prev2=False)
            mixer_step(1, 1, prev2=False)
            with dve.Fori(2 // 2, (NC - 2) // 2) as turn_no:
                c0 = turn_no * 2
                for q in range(2):
                    mixer_step(c0 + q, q)
            mixer_step(NC - 2, 0)
            mixer_step(NC - 1, 1, nxt=False, update=False)
            mixer_step(NC, 0, now=False, nxt=False, update=False)
            mixer_step(NC + 1, 1, now=False, nxt=False, update=False, prev=False)

        @block.tensor
        def _(pe):
            MM = nc.tensor.matmul
            TR = nc.tensor.transpose
            pe.wait_ge(S["const_ok"], 1)
            pe.wait_ge(S["w_in"], 64)
            for j in range(4):
                TR(bank[0][:, j * P:(j + 1) * P], win_st[:, j, :], ident[:, :])
            TR(bank[1][:, 0:P], win_st[:, 4, :], ident[:, :])
            TR(bank[1][:, P:P + NH], dt_st[:, :], ident[0:NH, 0:NH])
            TR(bank[1][:, P + NH:P + NH + E], rt_st[:, :], ident[0:E, 0:E])
            for c in range(2):
                ins = TR(bank[1][:, DI + c * P:DI + (c + 1) * P], wo_st[:, c * P:(c + 1) * P], ident[:, :])
            ins.then_inc(S["swt_ok"], 1)

            def small(g):
                pe.wait_ge(S["xTe_ok"], g + 1)
                if g == 0:
                    pe.wait_ge(S["sev_ok"], 1)
                for j in range(4 * g, 4 * g + 4):
                    b, at = j // NC, j % NC * P
                    ins = MM(small_ps[j // 16][:, j % 16, :], xnT_b[:, b, HALO + at:HALO + at + P], smallT[:, :],
                             start=True, stop=True)
                if g % 4 == 3:
                    ins.then_inc(S["lg_ok"], 1)

            for g in range(2 * NG):
                pe.wait_ge(S["xn_ok"], g // 2 + 1)
                at_least(pe, S["xTe_ok"], g - 1)
                for j in range(4):
                    ins = TR(bank[2 + g % 2][:, j * P:(j + 1) * P], xn[:, 4 * g + j, :], ident[:, :])
                ins.then_inc(S["xT_ok"], 1)
                if g >= 1:
                    small(g - 1)
            small(2 * NG - 1)

            def expert(e):
                q = e % 2
                pe.wait_ge(S[f"e_in{q}"], 24 * (e - q) + 48)
                at_least(pe, S["eTe_ok"], 2 * (e - 1))
                if e < 2:
                    pe.wait_ge(S["xTe_ok"], 2 * NG)
                for k in range(4):
                    ins = TR(bank[6 + q][:, k * P:(k + 1) * P], ex_st[q][:, k, :], ident[:, :])
                ins.then_inc(S["eT_ok"], 1)
                for k in range(2):
                    ins = MM(bank[2 + q][:, k * P:(k + 1) * P], ex_st[q][:, 4 + k, :], centre[:, :], start=True, stop=True)
                ins.then_inc(S["eT_ok"], 1)

            for e in range(4):
                expert(e)
            pe.wait_ge(S["both_ok"], 1)
            pe.wait_ge(S["sev_ok"], 3)
            picks = both[:, :, :].rearrange("p j e -> p (j e)")
            MM(bank[0][:, :], before[:, :], picks, start=True, stop=True)
            MM(bank[1][:, :], ones_bf[:, :], picks, start=True, stop=True).then_inc(S["cum_ok"], 1)
            pe.wait_ge(S["r_act"], 4)
            TR(bank[5][:, 384:512], decay[:, :, :].rearrange("p j h -> p (j h)"), ident[:, :]).then_inc(S["dtT_ok"], 1)
            ng = 2 * NT // GRP
            for g in range(ng):
                for e in range(4 + g * (E - 4) // ng, 4 + (g + 1) * (E - 4) // ng):
                    expert(e)
                pe.wait_ge(S["oh_ok"], g + 1)
                for k in range(GRP):
                    ins = MM(bank[0][:, 0:MT], is_lane[g % 2][:, k, :], tok_tile[g % 2][:, k, :],
                             start=(g == 0 and k == 0), stop=(g == ng - 1 and k == GRP - 1))
                ins.then_inc(S["tk_ok"], 1)

            pe.wait_ge(S["eTe_ok"], 2 * E)
            pe.wait_ge(S["own_ok"], 1)
            pe.wait_ge(S["tok_ok"], 1)
            pe.wait_ge(S["rows_ok"], 2)

            def turn_x(s, j):
                pe.wait_ge(m_xg[j], 2 * (s - j) + 16)
                at_least(pe, m_xt, s - 1)
                o = j % R
                TR(bank_x[o % 2][:, 0:P], xg[j][:, :], ident[:, :]).then_inc(m_t, 1)

            def up_proj(s, j, e):
                at = pe.snap(e * (2 * F))
                pe.wait_ge(m_xt, s + 1)
                at_least(pe, m_hid, s - 1)
                MM(bank_h[j % 2][:, :], xgT[j][:, :], w13T[:, bass.ds(at, 2 * F)], start=True, stop=True).then_inc(m_h, 1)

            def turn_hidden(s, j):
                pe.wait_ge(m_hid, s + 1)
                at_least(pe, m_hte, s - 1)
                for k in range(2):
                    ins = TR(bank_t[j % 2][:, k * P:(k + 1) * P], hid[j % 2][:, k * P:(k + 1) * P],
                             ident[:, :])
                ins.then_inc(m_ht, 1)

            def down_proj(s, j, e):
                at = pe.snap(e * F)
                pe.wait_ge(m_hte, s + 1)
                at_least(pe, m_g, s - 1)
                for k in range(2):
                    ins = MM(bank_y[j % 2][:, 0:D], hidT[j % 2][:, k, :], w2T[:, bass.ds(at + k * P, P)],
                             start=(k == 0), stop=(k == 1))
                ins.then_inc(m_y, 1)

            def step(s, j):
                if s + 1 < MT:
                    turn_x(s + 1, (j + 1) % RG)
                if 0 <= s < MT:
                    up_proj(s, j % R, expert_of(words, s, 0))
                    read_ahead(pe, words, s)
                if 1 <= s <= MT:
                    turn_hidden(s - 1, (j - 1) % R)
                if 2 <= s:
                    down_proj(s - 2, (j - 2) % R, expert_of(words, s, 2))

            words = {}
            for w in range(2):
                read_owners(pe, words, 0, w)
            for s in range(-1, MT + 2):
                step(s, s % RG)

            pe.wait_ge(m_o, MT)

            def project(n):
                at_least(pe, s_t0, 3 * n)
                at_least(pe, s_bt, n)
                for k in range(3):
                    MM(proj_ps(k), winT[:, DI + k * P:DI + (k + 1) * P], xnT_b[:, :, bass.ds(n * P, WIN)],
                       start=True, stop=True).then_inc(s_px, 1)
                at_least(pe, s_z, n)
                at_least(pe, s_f0, 2 * n - 4)
                for k in range(2):
                    ins = MM(bank[3][:, k * NB * P:(k + 1) * NB * P].rearrange("p (b n) -> p b n", b=NB),
                             winT[:, k * P:(k + 1) * P], xnT_b[:, :, bass.ds(n * P + HALO, P)], start=True, stop=True)
                ins.then_inc(s_pz, 1)

            def turn(c, q):
                pe.wait_ge(s_sx, c + 1)
                at_least(pe, s_xdt, c)
                for b in range(NB):
                    for k in range(2):
                        TR(bank[4][:, b * DI + k * P:b * DI + (k + 1) * P], xcT[q][:, k, b, :], ident[:, :])
                pe.wait_ge(s_sbc, c + 1)
                at_least(pe, s_m, 2 * c)
                MM(bank[5][:, 0:P], BT[q][0:NS, :], CT[q][0:NS, :], start=True, stop=True).then_inc(s_g0, 1)
                at_least(pe, s_bt, c)
                TR(bank[2][:, 384:512], BT[q][:, :], ident[:, :]).then_inc(s_tr, 1)
                pe.wait_ge(s_g0, c + 1)
                MM(bank[5][:, P:2 * P], BT[q][NS:2 * NS, :], CT[q][NS:2 * NS, :], start=True, stop=True).then_inc(s_g, 1)

            def chunk_state(c, q):
                pe.wait_ge(s_xe, c + 1)
                pe.wait_ge(s_bt, c + 1)
                pe.wait_ge(s_ha, c + 1)
                for b in range(NB):
                    ins = MM(bank[6][b * NS:(b + 1) * NS, 0:NH * HD], Bt[q][:, b * NS:(b + 1) * NS],
                             xend[q][:, b, :, :].rearrange("p h e -> p (h e)"), start=True, stop=True)
                ins.then_inc(s_s, 1)

            def mix_steps(c, q):
                pe.wait_ge(s_xdt, c + 1)
                pe.wait_ge(s_cp, c + 1)
                pe.wait_ge(s_ha, c + 1)
                pe.wait_ge(s_m, 2 * c + 2)
                at_least(pe, s_yD, 2 * c)
                for b in range(NB):
                    n = slice(b * NS, (b + 1) * NS)
                    for h in range(0, NH, 2):
                        at = (h // 2) * NB * P + b * P
                        for k in range(2):
                            if b == 1 and h == 0 and k == 1:
                                pe.wait_ge(s_y0, c + 1)
                            MM(bank[7][k * HD:(k + 1) * HD, at:at + P], xdt[q][:, b, h + k, :],
                               M[q][:, b, (h + k) * P:(h + k + 1) * P], start=True, stop=False)
                        for k in range(2):
                            ins = MM(bank[7][k * HD:(k + 1) * HD, at:at + P], H[q][n, (h + k) * HD:(h + k + 1) * HD],
                                     CP[q][n, h + k, :], start=False, stop=True)
                    ins.then_inc((s_y0, s_y)[b], 1)

            def project_back(c, q, after_z=True):
                pe.wait_ge(s_sq, c + 1)
                at_least(pe, s_f0, 2 * c)
                if after_z:
                    pe.wait_ge(s_z, c + 3)
                for b in range(NB):
                    for k in range(2):
                        MM(bank[3][:, b * D:(b + 1) * D], yg[q][:, k, b, :], woT[:, k, :],
                           start=(k == 0), stop=(k == 1))
                for b in range(NB):
                    for k in range(2):
                        ins = MM(bank[3][:, 256 + b:257 + b], ysq[q][:, k, b, :], ones[:, 0:1],
                                 start=(k == 0), stop=(k == 1))
                ins.then_inc(s_o, 1)

            def mixer_step(c, q, now=True, nxt=True, prev=True, update=True):
                if now:
                    turn(c, q)
                if nxt:
                    project(c + 1)
                if update:
                    chunk_state(c, q)
                if now:
                    mix_steps(c, q)
                if prev:
                    project_back(c - 1, 1 - q, nxt)

            mixer_step(-1, 1, now=False, prev=False, update=False)
            mixer_step(0, 0, prev=False)
            mixer_step(1, 1)
            with pe.Fori(2 // 2, (NC - 2) // 2) as turn_no:
                c0 = turn_no * 2
                for q in range(2):
                    mixer_step(c0 + q, q)
            mixer_step(NC - 2, 0)
            mixer_step(NC - 1, 1, nxt=False, update=False)
            mixer_step(NC, 0, now=False, nxt=False, update=False)


INS = ["L0_attn_X", "L0_attn_W_in", "L0_attn_conv_w", "L0_attn_conv_b", "L0_attn_dt_bias", "L0_attn_A_log",
       "L0_attn_D", "L0_attn_norm_w", "L0_attn_W_out", "L0_ffn_router_w", "L0_ffn_router_b", "L0_ffn_w1",
       "L0_ffn_w2", "L0_ffn_w3", "L0_ffn_ln_g", "L0_ffn_ln_b"]


def kernel(**inputs):
    import numpy as np
    import concourse.bacc as bacc
    from concourse.bass_utils import run_bass_kernel_spmd

    nc = bacc.Bacc("TRN2", target_bir_lowering=False, num_devices=1)
    arrays, args = {}, []
    for name in INS:
        a = np.ascontiguousarray(inputs[name])
        arrays[f"in_{name}"] = a
        args.append(nc.dram_tensor(f"in_{name}", a.shape, mybir.dt.from_np(a.dtype), kind="ExternalInput").ap())
    out = nc.dram_tensor("out", (NB, SEQ, D), F32, kind="ExternalOutput").ap()
    build(nc, *args, out)
    r = run_bass_kernel_spmd(nc, [arrays], core_ids=[0])
    return np.asarray(r.results[0]["out"])
```

```python
import concourse.bass as bass
from concourse import mybir
from concourse.alu_op_type import AluOpType as ALU
from contextlib import ExitStack

F32 = mybir.dt.float32
BF16 = mybir.dt.bfloat16
U32 = mybir.dt.uint32
I32 = mybir.dt.int32
ACT = mybir.ActivationFunctionType
AX = mybir.AxisListType

P = 128
NB, SEQ, D = 2, 2048, 128
T = NB * SEQ
NT = T // P
NC = SEQ // P
DI, NS, NH, HD = 256, 64, 4, 64
ZX = 2 * DI + 2 * NS
KC = 4
HALO = KC - 1
E, F = 16, 256
NSLOT = 2 * T
MT = (NSLOT + E * (P - 1)) // P
MT += -MT % 8
WIN = P + HALO
XB = SEQ + HALO
EPS = 1e-5


def build(nc, X, W_in, conv_w, conv_b, dt_bias, A_log, Dskip, norm_w, W_out,
          router_w, router_b, w1, w2, w3, ln_g, ln_b, out):
    ctx = ExitStack()
    with ctx:
        def sb(name, shape, dt=F32):
            return ctx.enter_context(nc.sbuf_tensor(name, shape, dt))

        def sem(name):
            return ctx.enter_context(nc.semaphore(name))

        def dram(name, shape, dt=F32):
            return nc.dram_tensor(name, shape, dt, kind="Internal").ap()

        def at_least(eng, s, v):
            if not (isinstance(v, int) and v <= 0):
                eng.wait_ge(s, v)

        def along(ap, axis, n):
            shape = list(ap.shape)
            return ap.unsqueeze(axis).broadcast_to(shape[:axis] + [n] + shape[axis:])

        xn_rows = dram("xn_rows", (T, D))
        y_rows = dram("y_rows", (MT * P, D))
        decay_rows = dram("decay_rows", (NT * NH * P,))
        prefix_rows = dram("prefix_rows", (NT * NH * P,))

        ident = sb("ident", [P, P])
        eye4 = sb("eye4", [P, NH, P])
        ones = sb("ones", [P, P])
        zeros = sb("zeros", [P, P])
        half = sb("half", [P, NT])
        eps_col = sb("eps_col", [P, 1])
        tile_no = sb("tile_no", [P, MT])

        winT = sb("winT", [P, ZX])
        smallT = sb("smallT", [P, NH + E])
        woT = sb("woT", [P, 2, D])
        w13T = sb("w13T", [P, E * 2 * F])
        w2T = sb("w2T", [P, E * F])
        g_all = sb("g_all", [P, E * D])
        b_all = sb("b_all", [P, E * D])
        cw = sb("cw", [P, 3, KC])
        cb = sb("cb", [P, 3])
        nw = sb("nw", [P, 2])
        dskip = sb("dskip", [P, 2])
        dtb = sb("dtb", [P, NH])
        a_log = sb("a_log", [P, NH])
        a_exp = sb("a_exp", [P, NH])
        rb = sb("rb", [P, E])

        x = sb("x", [P, NT, D])
        xnT = sb("xnT", [P, NB * XB])

        dt = sb("dt", [P, NT, NH])

        mix = sb("mix", [P, 2, NT])
        pos = sb("pos", [P, 2, NT])
        OW, OB = 6, 4
        owner_w = sb("owner_w", [P, MT // 8, 2], I32)
        GRP = 4
        tok = sb("tok", [P, MT])

        R = 4
        RG = 8
        g_idx = [sb(f"g_idx{i}", [P, 1], U32) for i in range(RG)]
        xg = [sb(f"xg{i}", [P, D]) for i in range(RG)]
        xgT = [sb(f"xgT{i}", [P, P]) for i in range(R)]
        up = [sb(f"up{i}", [P, F]) for i in range(2)]
        hid = [sb(f"hid{i}", [P, F]) for i in range(2)]
        hidT = [sb(f"hidT{i}", [P, 2, P]) for i in range(2)]
        y_sq = [sb(f"y_sq{i}", [P, D]) for i in range(2)]
        LAG = 6
        RY = 8
        y_ms = sb("y_ms", [P, RY])
        y_mse = sb("y_mse", [P, RY])
        y_rs = sb("y_rs", [P, RY])
        y_o = [sb(f"y_o{i}", [P, D]) for i in range(R)]

        bc_decay = [sb(f"bc_decay{i}", [P, NB, NH * P]) for i in range(2)]
        bc_prefix = [sb(f"bc_prefix{i}", [P, NH, P]) for i in range(2)]
        setup_only = ExitStack()

        def sb_setup(name, shape, dt=F32):
            return setup_only.enter_context(nc.sbuf_tensor(name, shape, dt))

        win_st = sb_setup("win_st", [P, 5, D])
        dt_st = sb_setup("dt_st", [NH, D])
        rt_st = sb_setup("rt_st", [E, D])
        wo_st = sb_setup("wo_st", [P, DI])
        NE = 4
        ex_st = [sb_setup(f"ex_st{i}", [P, 6, P]) for i in range(NE)]
        centre = sb_setup("centre", [P, P])
        before = sb_setup("before", [P, P], BF16)
        ones_bf = sb_setup("ones_bf", [P, P], BF16)
        rev_e = sb_setup("rev_e", [P, E])
        steps128 = sb_setup("steps128", [P, NT])
        restart = sb_setup("restart", [P, E, NT])
        lanes = sb_setup("lanes", [P, P, GRP], BF16)
        tiles = sb_setup("tiles", [P, MT, GRP], BF16)
        rows = sb_setup("rows", [P, NT], BF16)
        row = sb_setup("row", [P, 1])
        xn = sb_setup("xn", [P, NT, D])
        mean = sb_setup("mean", [P, NT])
        var = sb_setup("var", [P, NT])
        rstd = sb_setup("rstd", [P, NT])
        dt_v = sb_setup("dt_v", [P, NT, NH])
        dt_n = sb_setup("dt_n", [P, NT, NH])
        dt_u = sb_setup("dt_u", [P, NT, NH])
        dt_w = sb_setup("dt_w", [P, NT, NH])
        dt_l = sb_setup("dt_l", [P, NT, NH])
        dt_r = sb_setup("dt_r", [P, NT, NH])
        dt_c = sb_setup("dt_c", [P, NT, NH])
        dt_d = sb_setup("dt_d", [P, NT, NH])
        dt_e = dt_c
        dt_a = dt_n
        decay = sb_setup("decay", [P, NT, NH])
        decayT = sb_setup("decayT", [P, P])
        prefixT = sb_setup("prefixT", [P, P])
        lg = sb_setup("lg", [P, NT, E])
        lg2 = sb_setup("lg2", [P, NT, E])
        key = sb_setup("key", [P, NT, E])
        pick = [sb_setup(f"pick{i}", [P, NT, E]) for i in range(2)]
        both = sb_setup("both", [P, NT, E], BF16)
        top = [sb_setup(f"top{i}", [P, NT]) for i in range(2)]
        first = [sb_setup(f"first{i}", [P, NT]) for i in range(2)]
        gap = sb_setup("gap", [P, NT])
        egap = sb_setup("egap", [P, NT])
        esum = sb_setup("esum", [P, NT])
        tot = sb_setup("tot", [P, E, NT])
        run = sb_setup("run", [P, E, NT])
        more = sb_setup("more", [P, E, NT])
        n_tiles = sb_setup("n_tiles", [P, E])
        end_tile = sb_setup("end_tile", [P, E])
        off = sb_setup("off", [P, E])
        off_all = sb_setup("off_all", [P, E, NT])
        posn = lg2
        pos_u = sb_setup("pos_u", [P, 2, NT], U32)
        hi_u = sb_setup("hi_u", [P, 2, NT], U32)
        lo_u = sb_setup("lo_u", [P, 2, NT], U32)
        ln_sq = sb_setup("ln_sq", [P, 8, D])
        owner_p = sb_setup("owner_p", [P, MT + 8])
        owner_s = tot[:, :, :].rearrange("p e j -> p (e j)")[:, 0:MT // 8 * 2 * OW].rearrange(
            "p (t w k) -> p t w k", w=2, k=OW)
        word_f = sb_setup("word_f", [P, MT // 8, 2])
        nibble = sb_setup("nibble", [P, OW])
        lo_b = sb_setup("lo_b", [P, 2, NT], BF16)
        hi_b = sb_setup("hi_b", [P, 2, NT], BF16)
        end_col = sb_setup("end_col", [P, 1])
        end_pick = sb_setup("end_pick", [P, E])
        ended = sb_setup("ended", [P, MT])
        is_lane = [sb_setup(f"is_lane{i}", [P, P, GRP], BF16) for i in range(2)]
        is_tile = [sb_setup(f"is_tile{i}", [P, MT, GRP], BF16) for i in range(2)]
        tile_row = [sb_setup(f"tile_row{i}", [P, MT, GRP], BF16) for i in range(2)]
        tile_base = [sb_setup(f"tile_base{i}", [P, MT, GRP], BF16) for i in range(2)]
        setup_only.close()

        raw = sb("raw", [P, 3, NB, WIN])
        conv = sb("conv", [P, 3, NB, P])
        xcT = [sb(f"xcT{i}", [P, 2, NB, P]) for i in range(2)]
        BT = [sb(f"BT{i}", [P, P]) for i in range(2)]
        CT = [sb(f"CT{i}", [P, P]) for i in range(2)]
        zT = [sb(f"zT{i}", [P, 2, NB, P]) for i in range(2)]
        dt_now = [sb(f"dt_now{i}", [P, NB, NH]) for i in range(2)]
        xdt = [sb(f"xdt{i}", [P, NB, NH, HD]) for i in range(2)]
        Bt = [sb(f"Bt{i}", [P, P]) for i in range(2)]
        L = [sb(f"L{i}", [P, NB, NH * P]) for i in range(2)]
        M = [sb(f"M{i}", [P, NB, NH * P]) for i in range(2)]
        xend = [sb(f"xend{i}", [P, NB, NH, HD]) for i in range(2)]
        CP = [sb(f"CP{i}", [P, NH, P]) for i in range(2)]
        H = [sb(f"H{i}", [P, NH * HD]) for i in range(2)]
        Hm = sb("Hm", [P, NH * HD])
        skipT = sb("skipT", [P, 2, P])
        yg = [sb(f"yg{i}", [P, 2, NB, P]) for i in range(2)]
        ysq = [sb(f"ysq{i}", [P, 2, NB, P]) for i in range(2)]
        ms = [sb(f"ms{i}", [P, NB]) for i in range(2)]
        rs = [sb(f"rs{i}", [P, NB]) for i in range(2)]
        c_idx = [sb(f"c_idx{i}", [P, 2, NB], U32) for i in range(2)]
        c_mix = [sb(f"c_mix{i}", [P, 2, NB]) for i in range(2)]
        c_row = [sb(f"c_row{i}", [P, 2, NB, D]) for i in range(2)]
        acc = [sb(f"acc{i}", [P, NB, D]) for i in range(2)]
        y_g = [sb(f"y_g{i}", [P, D]) for i in range(RY)]

        bank = [ctx.enter_context(nc.psum_tensor(f"bank{i}", [P, 512], F32)) for i in range(8)]

        names = """c_done const_ok w_in x_in0 x_in1 x_in2 x_in3 vec_in gb_in e_in0 e_in1 e_in2 e_in3 ln_sum ln_c ln_act ln_v ln_pool
            xn_ok xn_st res_ok swt_ok sev_ok xT_ok xTe_ok0 xTe_ok1 lg_ok eT_ok eTe_ok a_ok skip_ok r_dve r_act
            both_ok cum_ok oh_ok tk_ok tok_ok own_ok dtT_ok rows_ok rows_st pos_ok dtn_ok dtw_ok dta_ok gap_ok word_ok ow_ok end_ok it_ok dtr_ok dt_pool
            """.split()
        S = {n: sem(n) for n in names}
        x_in = [S[f"x_in{i}"] for i in range(4)]
        m_idx, m_t, m_xt, m_h, m_up, m_hid, m_ht, m_hte, m_y, m_sq, m_eps, m_rs, m_g, m_o = (
            sem(n) for n in ("m_idx", "m_t", "m_xt", "m_h", "m_up", "m_hid", "m_ht", "m_hte",
                             "m_y", "m_sq", "m_eps", "m_rs", "m_g", "m_o"))
        m_xg = [sem(f"m_xg{i}") for i in range(RG)]
        m_st = [sem(f"m_st{i}") for i in range(R)]
        s_dec = [sem(f"s_dec{i}") for i in range(2)]
        s_pre = [sem(f"s_pre{i}") for i in range(2)]
        s_row = [sem(f"s_row{i}") for i in range(2)]
        s_sto = [sem(f"s_sto{i}") for i in range(2)]
        (s_px, s_pz, s_t0, s_z, s_cv, s_sx, s_sbc, s_tr, s_g, s_dtn, s_xdt, s_bt, s_sc, s_m,
         s_cp, s_xe, s_hm, s_s, s_ha, s_y, s_yg, s_sq, s_o, s_ms, s_rs, s_ci, s_cm,
         s_f, s_f0, s_g0, s_y0) = (sem("s_" + n) for n in (
             "px", "pz", "t0", "z", "cv", "sx", "sbc", "tr", "g", "dtn", "xdt", "bt", "sc",
             "m", "cp", "xe", "hm", "s", "ha", "y", "yg", "sq", "o", "ms", "rs", "ci",
             "cm", "f", "f0", "g0", "y0"))

        x_v = X.rearrange("b (j p) d -> p (b j) d", p=P)
        xn_v = xn_rows.rearrange("(j p) d -> p j d", p=P)
        out_v = out.rearrange("b (j p) d -> p b j d", p=P)
        xnT_b = xnT[:, :].rearrange("d (b n) -> d b n", b=NB)
        pos_bj = pos[:, :, :].rearrange("p s (b j) -> p s b j", b=NB)
        mix_bj = mix[:, :, :].rearrange("p s (b j) -> p s b j", b=NB)
        dt_bj = dt[:, :, :].rearrange("p (b j) h -> p b j h", b=NB)
        res_bj = x[:, :, :].rearrange("p (b j) d -> p b j d", b=NB)
        LG = 8
        NG = NT // LG
        EARLY = 6
        small_ps = [bank[4 + i][:, 0:16 * (NH + E)].rearrange("p (j n) -> p j n", j=16) for i in range(2)]

        def read_owners(eng, words, t, w):
            if t < MT // RG:
                words[t, w] = eng.value_load(owner_w[0:1, t:t + 1, w], min_val=0, max_val=16 ** OW - 1)

        def read_ahead(eng, words, s):
            if s % RG >= RG - 2:
                read_owners(eng, words, s // RG + 1, s % RG - (RG - 2))

        def expert_of(words, s, ago):
            t = min(s // RG, MT // RG - 1)
            if s - ago - t * RG < -OB:
                t -= 1
            w, k = divmod(s - ago - t * RG + OB, OW)
            return (words[t, w] >> 4 * k) & 15

        def proj_ps(k):
            return bank[k][:, 0:NB * WIN].rearrange("p (b n) -> p b n", b=NB)

        def tokens_T(g):
            at = g // 4 * XB + HALO + g % 4 * 512
            return xnT[:, at:at + 512]

        def back_ps(c):
            return bank[4] if isinstance(c, int) and c == NC - 1 else bank[3]

        bank_h, bank_x, bank_t, bank_y = bank[0:2], bank[2:4], bank[4:6], bank[6:8]

        block = ctx.enter_context(nc.Block())

        def decay_load(sp, c, q):
            at = [c * (NH * P) + b * NC * NH * P for b in range(NB)]
            pairs = c - 1
            if not isinstance(c, int):
                pairs, at = sp.snap(pairs), [sp.snap(a) for a in at]
            at_least(sp, s_hm, pairs)
            for b in range(NB):
                sp.dma_start(bc_decay[q][:, b, :],
                             decay_rows[bass.ds(at[b], NH * P)].partition_broadcast(P)).then_inc(s_dec[q], 16)
                sp.dma_start(bc_prefix[q][b * NS:(b + 1) * NS, :, :].rearrange("p h i -> p (h i)"),
                             prefix_rows[bass.ds(at[b], NH * P)].partition_broadcast(NS)).then_inc(s_pre[q], 16)

        def result_store(sp, c, q):
            sums = 4 * c + 4
            if not isinstance(c, int):
                c, sums = sp.snap(c), sp.snap(sums)
            sp.wait_ge(s_f, sums)
            sp.dma_start(out_v[:, :, bass.ds(c, 1), :].rearrange("p b j d -> p b (j d)"),
                         acc[q][:, :, :]).then_inc(s_sto[q], 16)

        @block.sync
        def _(sp):
            for g in range(NG):
                sp.dma_start(x[:, g * LG:(g + 1) * LG, :], x_v[:, g * LG:(g + 1) * LG, :]).then_inc(x_in[g], 16)
            for ap, src in ((dtb[:, :], dt_bias.partition_broadcast(P)), (a_log[:, :], A_log.partition_broadcast(P)),
                            (rb[:, :], router_b.partition_broadcast(P)),
                            (cw[:, :, :], conv_w.rearrange("(c p) k -> p c k", p=P)),
                            (cb[:, :], conv_b.rearrange("(c p) -> p c", p=P)),
                            (nw[:, :], norm_w.rearrange("(c p) -> p c", p=P))):
                with nc.allow_non_contiguous_dma(reason="a few small vectors, once"):
                    sp.dma_start(ap, src).then_inc(S["vec_in"], 16)
            for h in range(NH):
                sp.dma_start(dskip[(h % 2) * HD:(h % 2 + 1) * HD, h // 2:h // 2 + 1],
                             Dskip[h:h + 1].partition_broadcast(HD)).then_inc(S["vec_in"], 16)
            for e in range(E):
                q = e % NE
                at_least(sp, S["eT_ok"], 2 * (e - NE + 1))
                sp.dma_start(ex_st[q][:, 0:2, :], w1[e].rearrange("(c p) d -> p c d", p=P)).then_inc(S[f"e_in{q}"], 16)
                sp.dma_start(ex_st[q][:, 2:4, :], w3[e].rearrange("(c p) d -> p c d", p=P)).then_inc(S[f"e_in{q}"], 16)
                sp.dma_start(ex_st[q][:, 4:6, :].rearrange("p c n -> p (c n)"), w2[e]).then_inc(S[f"e_in{q}"], 16)
            sp.wait_ge(S["rows_ok"], 2)
            sp.dma_start(decay_rows.rearrange("(r i) -> r i", i=P), decayT[:, :]).then_inc(S["rows_st"], 16)
            sp.dma_start(prefix_rows.rearrange("(r i) -> r i", i=P), prefixT[:, :]).then_inc(S["rows_st"], 16)
            sp.wait_ge(S["rows_st"], 32)
            decay_load(sp, 0, 0)
            decay_load(sp, 1, 1)

            def tile_store(s, j):
                sp.wait_ge(m_o, s + 1)
                sp.dma_start(y_rows[s * P:(s + 1) * P, :], y_o[j][:, :]).then_inc(m_st[j], 16)

            for s in range(MT):
                tile_store(s, s % R)
            decay_load(sp, 2, 0)
            with sp.Fori(0, (NC - 4) // 2) as turn_no:
                c0 = turn_no * 2
                for q in range(2):
                    decay_load(sp, c0 + q + 3, 1 - q)
                    result_store(sp, c0 + q, q)
            decay_load(sp, NC - 1, 1)
            for c in range(NC - 4, NC):
                result_store(sp, c, c % 2)
            for q in range(2):
                sp.wait_ge(s_sto[q], 16 * (NC // 2))

        @block.gpsimd
        def _(pool):
            pool.memset(ident[:, :], 0.0)
            pool.memset(eye4[:, :, :], 0.0)
            pool.memset(centre[:, :], -1.0 / D)
            pool.memset(before[:, :], 1.0)
            pool.memset(ones_bf[:, :], 1.0)
            pool.memset(ones[:, :], 1.0)
            pool.memset(zeros[:, :], 0.0)
            pool.memset(half[:, :], -0.5)
            for k in range(OW):
                pool.memset(nibble[:, k:k + 1], float(16 ** k))
            pool.memset(eps_col[:, :], EPS)
            pool.memset(restart[:, :, :], 1.0)
            pool.memset(xnT_b[:, :, 0:HALO], 0.0).then_inc(S["c_done"], 1)
            pool.wait_ge(S["c_done"], 1)
            pool.affine_select(out=ident[:, :], in_=ident[:, :], compare_op=ALU.not_equal, fill=1.0,
                               base=0, pattern=[[-1, P]], channel_multiplier=1)
            pool.affine_select(out=eye4[:, :, :], in_=eye4[:, :, :], compare_op=ALU.not_equal, fill=1.0,
                               base=0, pattern=[[0, NH], [-1, P]], channel_multiplier=1)
            pool.affine_select(out=centre[:, :], in_=centre[:, :], compare_op=ALU.not_equal, fill=1.0 - 1.0 / D,
                               base=0, pattern=[[-1, P]], channel_multiplier=1)
            pool.affine_select(out=before[:, :], in_=before[:, :], compare_op=ALU.is_gt, fill=0.0,
                               base=0, pattern=[[1, P]], channel_multiplier=-1)
            pool.memset(restart[:, :, 0:1], 0.0)

            def count(ap, base, pattern, by=0):
                return pool.iota(ap, pattern=pattern, base=base, channel_multiplier=by,
                                 allow_small_or_imprecise_dtypes=True)

            count(rev_e[:, :], E, [[-1, E]])
            count(steps128[:, :], 0, [[P, NT]])
            count(lanes[:, :, :], 0, [[1, P], [0, GRP]])
            count(tiles[:, :, :], 0, [[1, MT], [0, GRP]])
            count(rows[:, :], 0, [[P, NT]])
            count(tile_no[:, :], 0, [[1, MT]])
            count(row[:, :], 0, [[0, 1]], 1).then_inc(S["const_ok"], 1)

            for g in range(NG):
                t = slice(g * LG, (g + 1) * LG)
                if g < 2:
                    pool.wait_ge(S["ln_act"], g + 1)
                else:
                    pool.wait_ge(S["ln_v"], g - 1)
                pool.tensor_scalar(var[:, t], var[:, t], 1.0 / D, EPS, ALU.mult, ALU.add).then_inc(S["ln_pool"], 1)
                pool.wait_ge(S["ln_pool"], 2 * g + 1)
                pool.tensor_tensor(rstd[:, t], var[:, t], half[:, t], ALU.pow).then_inc(S["ln_pool"], 1)
            pool.dma_start(g_all[:, :], ln_g.rearrange("e d -> (e d)").partition_broadcast(P)).then_inc(S["gb_in"], 16)
            pool.dma_start(b_all[:, :], ln_b.rearrange("e d -> (e d)").partition_broadcast(P)).then_inc(S["gb_in"], 16)
            for g in range(NG):
                t = slice(g * LG, (g + 1) * LG)
                pool.wait_ge(S["xn_ok"], g + 1)
                pool.tensor_tensor(x[:, t, :], x[:, t, :], xn[:, t, :], ALU.add).then_inc(S["res_ok"], 1)

            links = [0]

            def link(ins):
                links[0] += 1
                ins.then_inc(S["dt_pool"], 1)
                pool.wait_ge(S["dt_pool"], links[0])

            pool.wait_ge(S["dtr_ok"], 1)
            link(pool.tensor_scalar(dt_c[:, :, :], dt_w[:, :, :], -1.0, None, ALU.add))
            link(pool.tensor_tensor(dt_d[:, :, :], dt_u[:, :, :], dt_c[:, :, :], ALU.subtract))
            link(pool.tensor_tensor(dt_e[:, :, :], dt_d[:, :, :], dt_r[:, :, :], ALU.mult))
            pool.wait_ge(S["r_act"], 2)
            pool.tensor_tensor(dt_d[:, :, :], dt_e[:, :, :], dt_l[:, :, :], ALU.add)
            link(pool.tensor_scalar(dt_v[:, :, :], dt_v[:, :, :], 0.0, None, ALU.max))
            link(pool.tensor_tensor(dt[:, :, :], dt_v[:, :, :], dt_d[:, :, :], ALU.add))
            pool.wait_ge(S["a_ok"], 1)
            pool.tensor_tensor(dt_a[:, :, :], dt[:, :, :], along(a_exp[:, :], 1, NT), ALU.mult).then_inc(S["dta_ok"], 1)

            pool.wait_ge(S["xn_st"], 16 * NG)

            def gather(s, j):
                pool.indirect_dma_start(out=xg[j][:, :], out_offset=None, in_=xn_rows,
                                        in_offset=bass.IndirectOffsetOnAxis(ap=g_idx[j][:, 0:1], axis=0)
                                        ).then_inc(m_xg[j], 16)

            def step(s, j):
                ahead = min(2, MT - (s + 6))
                if ahead > 0:
                    pool.wait_ge(m_idx, s + 6 + ahead)
                    at_least(pool, m_t, s)
                for k in range(ahead):
                    gather(s + 6 + k, (j + 6 + k) % RG)
                if s >= 2:
                    f = (j - 2) % RY
                    at_least(pool, m_o, s - RY)
                    pool.wait_ge(m_eps, s)
                    pool.tensor_tensor(y_rs[:, f:f + 2], y_mse[:, f:f + 2], half[:, 0:2], ALU.pow).then_inc(m_rs, 2)

            pool.wait_ge(m_idx, 6)
            for s in range(6):
                gather(s, s)
            for s in range(0, MT + 1, 2):
                step(s, s % RG)

            def mixer_step(c, q, now=True, update=True, prev=True, prev2=True):
                if prev2:
                    pool.wait_ge(s_ms, c - 1)
                    pool.tensor_tensor(rs[q][:, :], ms[q][:, :], half[:, 0:NB], ALU.pow).then_inc(s_rs, 1)
                if now:
                    pool.wait_ge(s_sbc, c + 1)
                    pool.wait_ge(s_pre[q], 16 * (c - q) + 32)
                    at_least(pool, s_y, c - 1)
                    pool.tensor_tensor(CP[q][:, :, :], along(CT[q][:, :], 1, NH), bc_prefix[q][:, :, :],
                                       ALU.mult).then_inc(s_cp, 1)
                if update:
                    pool.wait_ge(s_sc, 2 * c + 2)
                    pool.wait_ge(s_xdt, c + 1)
                    at_least(pool, s_s, c - 1)
                    last = L[q][:, :, :].rearrange("p b (h i) -> p (b h) i", i=P)[:, :, P - 1]
                    pool.tensor_tensor(xend[q][:, :, :, :].rearrange("p b h e -> p (b h) e"),
                                       xdt[q][:, :, :, :].rearrange("p b h e -> p (b h) e"),
                                       along(last, 2, HD), ALU.mult).then_inc(s_xe, 1)
                if prev:
                    pool.wait_ge(s_ci, c)
                    at_least(pool, s_f, 4 * (c - 2))
                if update:
                    pool.wait_ge(s_ha, c + 1)
                    pool.tensor_tensor(Hm[:, :].rearrange("p (h e) -> p h e", h=NH),
                                       H[q][:, :].rearrange("p (h e) -> p h e", h=NH),
                                       along(bc_prefix[q][:, :, P - 1], 2, HD), ALU.mult).then_inc(s_hm, 1)
                if prev:
                    o = 1 - q
                    for s in range(2):
                        for b in range(NB):
                            pool.indirect_dma_start(out=c_row[o][:, s, b, :], out_offset=None, in_=y_rows,
                                                    in_offset=bass.IndirectOffsetOnAxis(ap=c_idx[o][:, s, b:b + 1], axis=0)
                                                    ).then_inc(s_row[o], 16)

            for q in range(R):
                pool.wait_ge(m_st[q], 16 * (MT // R))
            mixer_step(0, 0, prev=False, prev2=False)
            mixer_step(1, 1, prev2=False)
            mixer_step(2, 0)
            mixer_step(3, 1)
            with pool.Fori(2, (NC - 2) // 2) as turn_no:
                c0 = turn_no * 2
                for q in range(2):
                    mixer_step(c0 + q, q)
            mixer_step(NC - 2, 0)
            mixer_step(NC - 1, 1, update=False)
            mixer_step(NC, 0, now=False, update=False)
            mixer_step(NC + 1, 1, now=False, update=False, prev=False)

        @block.scalar
        def _(act):
            A = nc.scalar.activation
            for ap, src in ((win_st[:, :, :], W_in[0:ZX, :].rearrange("(j p) d -> p j d", p=P)),
                            (dt_st[:, :], W_in[ZX:ZX + NH, :]), (rt_st[:, :], router_w), (wo_st[:, :], W_out)):
                act.dma_start(ap, src).then_inc(S["w_in"], 16)
            for g in range(NG):
                act.wait_ge(S["ln_c"], g + 1)
                at_least(act, S["ln_act"], g)
                if g >= 2:
                    at_least(act, S["ln_v"], g - 2)
                    ins = A(ln_sq[:, :, :], xn[:, g * LG:(g + 1) * LG, :], ACT.Square)
                for j in range(LG if g < 2 else 0):
                    ins = A(ln_sq[:, j, :], xn[:, g * LG + j, :], ACT.Square, accum_out=var[:, g * LG + j:g * LG + j + 1])
                ins.then_inc(S["ln_act"], 1)
                if g == 1:
                    act.wait_ge(S["swt_ok"], 1)
                    A(winT[:, 0:512], bank[0][:, :], ACT.Copy)
                    A(winT[:, 512:640], bank[1][:, 0:128], ACT.Copy)
                    A(smallT[:, :], bank[1][:, 128:128 + NH + E], ACT.Copy).then_inc(S["sev_ok"], 1)
                    act.wait_ge(S["vec_in"], 16 * 10)
                    for c in range(2):
                        A(woT[:, c, :], bank[1][:, 256 + c * P:256 + (c + 1) * P], ACT.Copy,
                          scale=nw[:, c:c + 1]).then_inc(S["sev_ok"], 1)

            def expert_out(e):
                q = e % 2
                act.wait_ge(S["eT_ok"], 2 * e + 1)
                A(w13T[:, e * 2 * F:(e + 1) * 2 * F], bank[6 + q][:, :], ACT.Copy).then_inc(S["eTe_ok"], 1)
                act.wait_ge(S["eT_ok"], 2 * e + 2)
                A(w2T[:, e * F:(e + 1) * F], bank[0 + q][:, 0:F], ACT.Copy).then_inc(S["eTe_ok"], 1)

            for g in range(2 * NG):
                if g % 2 == 0:
                    act.wait_ge(S["xT_ok"], g + 1)
                    A(tokens_T(g), bank[2][:, :], ACT.Copy).then_inc(S["xTe_ok0"], 1)
                else:
                    act.wait_ge(S["xn_ok"], g // 2 + 1)
                    at = slice(g // 2 * LG, (g // 2 + 1) * LG)
                    act.dma_start(xn_v[:, at, :], xn[:, at, :]).then_inc(S["xn_st"], 16)
                if g >= EARLY:
                    expert_out(g - EARLY)
            for e in range(2 * NG - EARLY, E):
                expert_out(e)
                if e == 2 * NG - EARLY:
                    A(a_exp[:, :], a_log[:, :], ACT.Exp).then_inc(S["a_ok"], 1)
                    act.wait_ge(S["dtn_ok"], 1)
                    A(dt_u[:, :, :], dt_n[:, :, :], ACT.Exp).then_inc(S["r_act"], 1)
                if e == 9:
                    act.wait_ge(S["dtw_ok"], 1)
                    A(dt_l[:, :, :], dt_w[:, :, :], ACT.Ln).then_inc(S["r_act"], 1)
                    act.wait_ge(S["gap_ok"], 1)
                    A(egap[:, :], gap[:, :], ACT.Exp).then_inc(S["r_act"], 1)
                if e == E - 1:
                    act.wait_ge(S["dta_ok"], 1)
                    A(decay[:, :, :], dt_a[:, :, :], ACT.Exp, scale=-1.0).then_inc(S["r_act"], 1)

            def project_out(n, o):
                at_least(act, s_cv, 9 * n)
                at_least(act, s_sx, n)
                at_least(act, s_sbc, n)
                for k in range(3):
                    act.wait_ge(s_px, 3 * n + k + 1)
                    A(raw[:, k, :, :], proj_ps(k), ACT.Copy)
                    A(conv[:, k, :, :], proj_ps(k)[:, :, 0:P], ACT.Identity, bias=cb[:, k:k + 1],
                      scale=cw[:, k, 0:1]).then_inc(s_t0, 1)
                act.wait_ge(s_pz, n + 1)
                at_least(act, s_yg, n - 1)
                A(zT[o][:, :, :, :].rearrange("p c b i -> p (c b i)"), bank[3][:, :], ACT.Silu).then_inc(s_z, 1)

            def conv_out(n, o):
                act.wait_ge(s_cv, 9 * n + 9)
                at_least(act, s_tr, n - 1)
                at_least(act, s_y, n - 1)
                A(xcT[o][:, :, :, :], conv[:, 0:2, :, :], ACT.Silu).then_inc(s_sx, 1)
                at_least(act, s_g, n - 1)
                at_least(act, s_cp, n - 1)
                for b in range(NB):
                    A(BT[o][b * NS:(b + 1) * NS, :], conv[0:NS, 2, b, :], ACT.Silu)
                    ins = A(CT[o][b * NS:(b + 1) * NS, :], conv[NS:2 * NS, 2, b, :], ACT.Silu)
                ins.then_inc(s_sbc, 1)

            project_out(0, 0)

            act.wait_ge(S["tok_ok"], 1)

            def idx(s, j):
                if s >= RG:
                    act.wait_ge(m_xg[j], 2 * (s - j))
                A(g_idx[j][:, 0:1], tok[:, bass.ds(s, 1)], ACT.Copy).then_inc(m_idx, 1)

            def silu(s, j):
                act.wait_ge(m_h, s + 1)
                at_least(act, m_hid, s - 1)
                A(up[j % 2][:, :], bank_h[j % 2][:, 0:F], ACT.Silu).then_inc(m_up, 1)

            def hidden_out(s, j):
                act.wait_ge(m_ht, s + 1)
                at_least(act, m_y, s - 1)
                A(hidT[j % 2][:, :, :].rearrange("p c n -> p (c n)"), bank_t[j % 2][:, 0:F], ACT.Copy).then_inc(m_hte, 1)

            def square(s, j):
                act.wait_ge(m_y, s + 1)
                at_least(act, m_eps, s - RY + 1)
                A(y_sq[j % 2][:, :], bank_y[j % 2][:, 0:D], ACT.Square, scale=D ** -0.5,
                  accum_out=y_ms[:, j:j + 1]).then_inc(m_sq, 1)

            def with_eps(s, j):
                act.wait_ge(m_sq, s + 2)
                at_least(act, m_rs, s - RY + 2)
                A(y_mse[:, j:j + 2], y_ms[:, j:j + 2], ACT.Identity, bias=eps_col[:, 0:1]).then_inc(m_eps, 2)

            for s in range(RG):
                idx(s, s)
            conv_out(0, 0)

            def step(s, j):
                if s + 1 < MT:
                    silu(s + 1, (j + 1) % R)
                if 0 <= s < MT:
                    hidden_out(s, j % R)
                if 1 <= s <= MT:
                    square(s - 1, (j - 1) % RY)
                if 3 <= s and s % 2 == 1:
                    with_eps(s - 3, (j - 3) % RY)
                if 0 <= s and s + RG < MT:
                    idx(s + RG, j)

            for s in range(-1, MT + 2):
                step(s, s % RG)
                if s == 10:
                    for k in range(2):
                        A(skipT[:, k, :], ident[:, :], ACT.Copy, scale=dskip[:, k:k + 1]).then_inc(S["skip_ok"], 1)

            def mixer_step(c, q, now=True, nxt=True, prev=True):
                o = 1 - q
                if now:
                    at_least(act, s_xdt, c - 1)
                    A(dt_now[q][:, :, :], dt_bj[:, :, bass.ds(c, 1), :].rearrange("p b j h -> p b (j h)"),
                      ACT.Copy).then_inc(s_dtn, 1)
                    act.wait_ge(s_dtn, c + 1)
                    act.wait_ge(s_tr, c + 1)
                    at_least(act, s_y, c - 1)
                    at_least(act, s_xe, c - 1)
                    at_least(act, s_s, c - 1)
                    A(Bt[q][:, :], bank[2][:, 384:512], ACT.Copy).then_inc(s_bt, 1)
                    for b in range(NB):
                        for h in range(NH):
                            ins = A(xdt[q][:, b, h, :], bank[4][:, b * DI + h * HD:b * DI + (h + 1) * HD],
                                    ACT.Copy, scale=dt_now[q][:, b, h:h + 1])
                    ins.then_inc(s_xdt, 1)
                if prev:
                    if not (isinstance(c, int) and c < 3):
                        act.wait_ge(s_row[o], 32 * (c - 1 - o))
                        act.wait_ge(s_f, 4 * (c - 2))
                    A(c_idx[o][:, :, :], pos_bj[:, :, :, bass.ds(c - 1, 1)].rearrange("p s b j -> p s (b j)"),
                      ACT.Copy).then_inc(s_ci, 1)
                    A(c_mix[o][:, :, :], mix_bj[:, :, :, bass.ds(c - 1, 1)].rearrange("p s b j -> p s (b j)"),
                      ACT.Copy).then_inc(s_cm, 1)
                if nxt:
                    project_out(c + 1, o)
                if prev:
                    act.wait_ge(s_yg, c)
                    at_least(act, s_o, c - 2)
                    A(ysq[o][:, :, :, :], yg[o][:, :, :, :], ACT.Square).then_inc(s_sq, 1)
                if nxt:
                    conv_out(c + 1, o)
                if prev:
                    act.wait_ge(s_o, c)
                    at_least(act, s_rs, c - 2)
                    A(ms[o][:, :], back_ps(c - 1)[:, 256:256 + NB], ACT.Identity, bias=eps_col[:, 0:1],
                      scale=1.0 / DI).then_inc(s_ms, 1)

            act.wait_ge(S["pos_ok"], 1)
            act.wait_ge(S["own_ok"], 1)
            mixer_step(0, 0, prev=False)
            mixer_step(1, 1)
            mixer_step(2, 0)
            mixer_step(3, 1)
            with act.Fori(2, (NC - 2) // 2) as turn_no:
                c0 = turn_no * 2
                for q in range(2):
                    mixer_step(c0 + q, q)
            mixer_step(NC - 2, 0)
            mixer_step(NC - 1, 1, nxt=False)
            mixer_step(NC, 0, now=False, nxt=False)

        @block.vector
        def _(dve):
            V = nc.vector
            chain = [0]

            def link(ins):
                chain[0] += 1
                ins.then_inc(S["r_dve"], 1)
                dve.wait_ge(S["r_dve"], chain[0])

            def top_two(i):
                t = slice(16 * i, 16 * i + 16)
                logits = lg
                for s in range(2):
                    link(V.reduce_max(top[s][:, t], logits[:, t, :], AX.X))
                    link(V.tensor_tensor(key[:, t, :], logits[:, t, :], along(top[s][:, t], 2, E), ALU.is_equal))
                    link(V.tensor_tensor(key[:, t, :], key[:, t, :], along(rev_e[:, :], 1, 16), ALU.mult))
                    link(V.reduce_max(first[s][:, t], key[:, t, :], AX.X))
                    link(V.tensor_tensor(pick[s][:, t, :], along(rev_e[:, :], 1, 16), along(first[s][:, t], 2, E),
                                         ALU.is_equal))
                    if s == 0:
                        link(V.scalar_tensor_tensor(lg2[:, t, :], pick[0][:, t, :], -1e30, lg[:, t, :], ALU.mult, ALU.add))
                        logits = lg2

            for g in range(NG):
                t = slice(g * LG, (g + 1) * LG)
                dve.wait_ge(x_in[g], 16)
                V.reduce_sum(mean[:, t], x[:, t, :], AX.X).then_inc(S["ln_sum"], 1)
                dve.wait_ge(S["ln_sum"], g + 1)
                V.scalar_tensor_tensor(xn[:, t, :], along(mean[:, t], 2, D), -1.0 / D, x[:, t, :],
                                       ALU.mult, ALU.add).then_inc(S["ln_c"], 1)
            for g in range(NG):
                t = slice(g * LG, (g + 1) * LG)
                dve.wait_ge(S["ln_pool"], 2 * (g + 1))
                V.tensor_tensor(xn[:, t, :], xn[:, t, :], along(rstd[:, t], 2, D), ALU.mult).then_inc(S["xn_ok"], 1)
                if g < 2:
                    n = slice((g + 2) * LG, (g + 3) * LG)
                    dve.wait_ge(S["ln_act"], g + 3)
                    V.reduce_sum(var[:, n], ln_sq[:, :, :], AX.X).then_inc(S["ln_v"], 1)

            def taps(n):
                order = [(1, 0), (2, 0), (1, 1), (3, 0), (2, 1), (1, 2), (3, 1), (2, 2), (3, 2)]
                for t, k in order:
                    if t == 1:
                        dve.wait_ge(s_t0, 3 * n + k + 1)
                    else:
                        dve.wait_ge(s_cv, 9 * n + order.index((t - 1, k)) + 1)
                    V.scalar_tensor_tensor(conv[:, k, :, :], raw[:, k, :, t:t + P], cw[:, k, t:t + 1],
                                           conv[:, k, :, :], ALU.mult, ALU.add).then_inc(s_cv, 1)

            dve.wait_ge(S["vec_in"], 16 * 10)
            dve.wait_ge(S["const_ok"], 1)

            def tokens_out(g):
                dve.wait_ge(S["xT_ok"], g + 1)
                V.tensor_copy(tokens_T(g), bank[3][:, :]).then_inc(S["xTe_ok1"], 1)

            for i in range(2):
                tokens_out(4 * i + 1)
                tokens_out(4 * i + 3)
                if i == 1:
                    top_two(0)
                dve.wait_ge(S["lg_ok"], i + 1)
                j = slice(16 * i, 16 * i + 16)
                V.tensor_tensor(dt_v[:, j, :], small_ps[i][:, :, 0:NH], along(dtb[:, :], 1, 16), ALU.add)
                link(V.tensor_tensor(lg[:, j, :], small_ps[i][:, :, NH:NH + E], along(rb[:, :], 1, 16), ALU.add))
            V.scalar_tensor_tensor(dt_n[:, :, :], dt_v[:, :, :], -1.0, dt_v[:, :, :], ALU.mult,
                                   ALU.min).then_inc(S["dtn_ok"], 1)
            top_two(1)
            V.tensor_tensor(both[:, :, :], pick[0][:, :, :], pick[1][:, :, :], ALU.add).then_inc(S["both_ok"], 1)
            V.tensor_tensor(gap[:, :], top[1][:, :], top[0][:, :], ALU.subtract).then_inc(S["gap_ok"], 1)
            dve.wait_ge(S["r_act"], 1)
            V.tensor_scalar(dt_w[:, :, :], dt_u[:, :, :], 1.0, None, ALU.add).then_inc(S["dtw_ok"], 1)
            dve.wait_ge(S["dtw_ok"], 1)
            V.reciprocal(dt_r[:, :, :], dt_w[:, :, :]).then_inc(S["dtr_ok"], 1)
            dve.wait_ge(S["cum_ok"], 1)
            link(V.tensor_copy(tot[:, :, :], bank[3][:, :].rearrange("p (j e) -> p e j", e=E)))
            flat = lambda ap: ap[:, :, :].rearrange("p a b -> p (a b)")
            link(V.tensor_tensor_scan(flat(run), flat(restart), flat(tot), 0.0, ALU.mult, ALU.add))
            link(V.tensor_tensor(more[:, :, :], along(run[:, :, NT - 1], 2, NT), along(steps128[:, :], 1, E), ALU.is_gt))
            link(V.reduce_sum(n_tiles[:, :], more[:, :, :], AX.X))
            link(V.tensor_tensor_scan(end_tile[:, :], ones[:, 0:E], n_tiles[:, :], 0.0, ALU.mult, ALU.add))
            link(V.tensor_tensor(end_pick[:, :], end_tile[:, :], ident[:, 0:E], ALU.mult))
            link(V.reduce_sum(end_col[:, :], end_pick[:, :], AX.X))
            V.tensor_scalar(ended[:, :], tile_no[:, :], end_col[:, 0:1], None, ALU.is_ge).then_inc(S["end_ok"], 1)
            V.tensor_tensor(more[:, :, :], run[:, :, :], tot[:, :, :], ALU.subtract)
            link(V.tensor_tensor(off[:, :], end_tile[:, :], n_tiles[:, :], ALU.subtract))
            link(V.scalar_tensor_tensor(off_all[:, :, :], along(off[:, :], 2, NT), float(P), more[:, :, :],
                                        ALU.mult, ALU.add))
            link(V.tensor_tensor(posn[:, :, :], bank[2][:, :].rearrange("p (j e) -> p j e", e=E),
                                 off_all[:, :, :].rearrange("p e j -> p j e"), ALU.add))
            for s in range(2):
                link(V.tensor_tensor(key[:, :, :], pick[s][:, :, :], posn[:, :, :], ALU.mult))
                link(V.reduce_sum(pos[:, s, :], key[:, :, :], AX.X))
            link(V.tensor_copy(pos_u[:, :, :], pos[:, :, :]))
            V.tensor_scalar(hi_u[:, :, :], pos_u[:, :, :], 7, None, ALU.logical_shift_right)
            link(V.tensor_scalar(lo_u[:, :, :], pos_u[:, :, :], P - 1, None, ALU.bitwise_and))
            V.tensor_copy(hi_b[:, :, :], hi_u[:, :, :])
            link(V.tensor_copy(lo_b[:, :, :], lo_u[:, :, :]))

            lo_f, hi_f = (t[:, :, :].rearrange("p s j -> p (s j)") for t in (lo_b, hi_b))
            for g in range(2 * NT // GRP):
                q, k, j = g % 2, g * GRP, g * GRP % NT
                at_least(dve, S["tk_ok"], g - 1)
                V.tensor_tensor(is_tile[q][:, :, :], tiles[:, :, :], along(hi_f[:, k:k + GRP], 1, MT),
                                ALU.is_equal).then_inc(S["it_ok"], 1)
                V.tensor_tensor(is_lane[q][:, :, :], lanes[:, :, :], along(lo_f[:, k:k + GRP], 1, P), ALU.is_equal)
                dve.wait_ge(S["it_ok"], g + 1)
                V.tensor_scalar(tile_row[q][:, :, :], is_tile[q][:, :, :], row[:, 0:1], None, ALU.mult)
                V.tensor_tensor(tile_base[q][:, :, :], is_tile[q][:, :, :], along(rows[:, j:j + GRP], 1, MT),
                                ALU.mult).then_inc(S["oh_ok"], 1)
            dve.wait_ge(S["ow_ok"], 1)
            link(V.memset(owner_p[:, :], 0.0))
            link(V.tensor_scalar(owner_p[:, OB:OB + MT], bank[4][:, 384:384 + MT], float(E - 1), None, ALU.min))
            for w in range(2):
                V.tensor_tensor(owner_s[:, :, w, :],
                                owner_p[:, w * OW:w * OW + MT].rearrange("p (t n) -> p t n", n=8)[:, :, 0:OW],
                                along(nibble[:, :], 1, MT // 8), ALU.mult).then_inc(S["word_ok"], 1)
            dve.wait_ge(S["word_ok"], 2)
            link(V.reduce_sum(word_f[:, :, :], owner_s[:, :, :, :], AX.X))
            V.tensor_copy(owner_w[:, :, :], word_f[:, :, :]).then_inc(S["own_ok"], 1)
            dve.wait_ge(S["tk_ok"], 2 * NT // GRP)
            V.tensor_copy(tok[:, :], bank[6][:, 0:MT]).then_inc(S["tok_ok"], 1)
            taps(0)

            dve.wait_ge(S["gb_in"], 32)
            dve.wait_ge(S["own_ok"], 1)

            def shares():
                dve.wait_ge(S["r_act"], 3)
                link(V.tensor_scalar(esum[:, :], egap[:, :], 1.0, None, ALU.add))
                link(V.reciprocal(mix[:, 0, :], esum[:, :]))
                V.tensor_tensor(mix[:, 1, :], egap[:, :], mix[:, 0, :], ALU.mult).then_inc(S["pos_ok"], 1)

            def decay_rows_out():
                dve.wait_ge(S["dtT_ok"], 1)
                V.tensor_tensor_scan(prefixT[:, :], bank[5][:, 384:512], zeros[:, :], 1.0, ALU.mult,
                                     ALU.add).then_inc(S["rows_ok"], 1)
                link(V.tensor_copy(decayT[:, :], bank[5][:, 384:512]))
                V.memset(decayT[:, 0:1], 0.0).then_inc(S["rows_ok"], 1)

            def x_out(s, j):
                dve.wait_ge(m_t, s + 1)
                at_least(dve, m_h, s - 3)
                V.tensor_copy(xgT[j][:, :], bank_x[j % 2][:, 0:P]).then_inc(m_xt, 1)

            def hidden(s, j):
                dve.wait_ge(m_up, s + 1)
                at_least(dve, m_ht, s - 1)
                V.tensor_tensor(hid[j % 2][:, :], up[j % 2][:, :], bank_h[j % 2][:, F:2 * F], ALU.mult).then_inc(m_hid, 1)

            def gained(s, j, e):
                at = dve.snap(e * D)
                dve.wait_ge(m_sq, s + 1)
                at_least(dve, m_o, s - RY + 1)
                V.tensor_tensor(y_g[j][:, :], bank_y[j % 2][:, 0:D], g_all[:, bass.ds(at, D)],
                                ALU.mult).then_inc(m_g, 1)

            def shifted(s, j, e):
                at = dve.snap(e * D)
                dve.wait_ge(m_rs, s + 1)
                dve.wait_ge(m_g, s + 1)
                o = j % R
                if s >= R:
                    dve.wait_ge(m_st[o], 4 * (s - o))
                V.scalar_tensor_tensor(y_o[o][:, :], y_g[j][:, :], y_rs[:, j:j + 1], b_all[:, bass.ds(at, D)],
                                       ALU.mult, ALU.add).then_inc(m_o, 1)

            def step(s, j):
                if s + 2 < MT:
                    x_out(s + 2, (j + 2) % R)
                if 0 <= s + 1 < MT:
                    hidden(s + 1, (j + 1) % R)
                if 0 <= s:
                    read_ahead(dve, words, s)
                if 2 <= s <= MT + 1:
                    gained(s - 2, (j - 2) % RY, expert_of(words, s, 2))
                if LAG <= s:
                    shifted(s - LAG, (j - LAG) % RY, expert_of(words, s, LAG))

            words = {}
            for w in range(2):
                read_owners(dve, words, 0, w)
            for s in range(-2, MT + LAG):
                step(s, s % RG)
                if s == -1:
                    decay_rows_out()
                if s == 3:
                    shares()

            V.memset(H[0][:, :], 0.0).then_inc(s_ha, 1)

            def decay_products(c, q):
                dve.wait_ge(s_dec[q], 16 * (c - q) + 32)
                at_least(dve, s_xe, c - 1)
                for b in range(NB):
                    V.tensor_tensor_scan(L[q][:, b, :], bc_decay[q][:, b, :],
                                         eye4[:, :, :].rearrange("p h i -> p (h i)"), 0.0, ALU.mult,
                                         ALU.add).then_inc(s_sc, 1)

            def mask(c, q):
                dve.wait_ge(s_g, c + 1)
                at_least(dve, s_y, c - 1)
                for b in range(NB):
                    dve.wait_ge(s_sc, 2 * c + b + 1)
                    V.tensor_tensor(M[q][:, b, :].rearrange("p (h i) -> p h i", h=NH),
                                    L[q][:, b, :].rearrange("p (h i) -> p h i", h=NH),
                                    along(bank[5][:, b * P:(b + 1) * P], 1, NH), ALU.mult).then_inc(s_m, 1)

            def gate(c, q):
                dve.wait_ge(s_y, c + 1)
                dve.wait_ge(s_z, c + 1)
                at_least(dve, s_o, c - 1)
                V.tensor_tensor(yg[q][:, :, :, :].rearrange("p k b i -> p (k b i)"), bank[7][:, :],
                                zT[q][:, :, :, :].rearrange("p k b i -> p (k b i)"), ALU.mult).then_inc(s_yg, 1)

            def state(c, q):
                dve.wait_ge(s_s, c + 1)
                dve.wait_ge(s_hm, c + 1)
                at_least(dve, s_y, c)
                V.tensor_tensor(H[1 - q][:, :], Hm[:, :], bank[6][:, 0:NH * HD], ALU.add).then_inc(s_ha, 1)

            def scaled(c, q):
                dve.wait_ge(s_rs, c + 1)
                if not (isinstance(c, int) and c < 2):
                    dve.wait_ge(s_sto[q], 8 * (c - q))
                for b in range(NB):
                    V.scalar_tensor_tensor(acc[q][:, b, :], back_ps(c)[:, b * D:(b + 1) * D], rs[q][:, b:b + 1],
                                           res_bj[:, b, bass.ds(c, 1), :].rearrange("p j d -> p (j d)"),
                                           ALU.mult, ALU.add).then_inc(s_f0, 1)

            def combined(c, q):
                dve.wait_ge(s_cm, c + 1)
                dve.wait_ge(s_row[q], 32 * (c - q) + 64)
                for s in range(2):
                    for b in range(NB):
                        if s == 0:
                            dve.wait_ge(s_f0, 2 * c + b + 1)
                        else:
                            dve.wait_ge(s_f, 4 * c + b + 1)
                        V.scalar_tensor_tensor(acc[q][:, b, :], c_row[q][:, s, b, :], c_mix[q][:, s, b:b + 1],
                                               acc[q][:, b, :], ALU.mult, ALU.add).then_inc(s_f, 1)

            def mixer_step(c, q, now=True, nxt=True, prev=True, prev2=True, update=True):
                if now:
                    decay_products(c, q)
                if prev2 and now:
                    scaled(c - 2, q)
                if now:
                    mask(c, q)
                if prev:
                    gate(c - 1, 1 - q)
                if prev2 and not now:
                    scaled(c - 2, q)
                if nxt:
                    taps(c + 1)
                if update:
                    state(c, q)
                if prev2:
                    combined(c - 2, q)

            dve.wait_ge(S["res_ok"], NG)
            mixer_step(0, 0, prev=False, prev2=False)
            mixer_step(1, 1, prev2=False)
            mixer_step(2, 0)
            mixer_step(3, 1)
            with dve.Fori(2, (NC - 2) // 2) as turn_no:
                c0 = turn_no * 2
                for q in range(2):
                    mixer_step(c0 + q, q)
            mixer_step(NC - 2, 0)
            mixer_step(NC - 1, 1, nxt=False, update=False)
            mixer_step(NC, 0, now=False, nxt=False, update=False)
            mixer_step(NC + 1, 1, now=False, nxt=False, update=False, prev=False)

        @block.tensor
        def _(pe):
            MM = nc.tensor.matmul
            TR = nc.tensor.transpose
            pe.wait_ge(S["const_ok"], 1)

            def keep_warm(n):
                for _ in range(n):
                    MM(bank[7][:, :], ident[:, :], eye4[:, :, :].rearrange("p h i -> p (h i)"), start=True, stop=True)

            pe.wait_ge(S["w_in"], 64)
            for j in range(4):
                TR(bank[0][:, j * P:(j + 1) * P], win_st[:, j, :], ident[:, :])
            TR(bank[1][:, 0:P], win_st[:, 4, :], ident[:, :])
            TR(bank[1][:, P:P + NH], dt_st[:, :], ident[0:NH, 0:NH])
            TR(bank[1][:, P + NH:P + NH + E], rt_st[:, :], ident[0:E, 0:E])
            for c in range(2):
                ins = TR(bank[1][:, DI + c * P:DI + (c + 1) * P], wo_st[:, c * P:(c + 1) * P], ident[:, :])
            ins.then_inc(S["swt_ok"], 1)
            keep_warm(3)

            def small(g):
                pe.wait_ge(S[f"xTe_ok{g % 2}"], g // 2 + 1)
                if g == 0:
                    pe.wait_ge(S["sev_ok"], 1)
                for j in range(4 * g, 4 * g + 4):
                    b, at = j // NC, j % NC * P
                    ins = MM(small_ps[j // 16][:, j % 16, :], xnT_b[:, b, HALO + at:HALO + at + P], smallT[:, :],
                             start=True, stop=True)
                if g % 4 == 3:
                    ins.then_inc(S["lg_ok"], 1)

            def expert(e):
                q = e % 2
                pe.wait_ge(S[f"e_in{e % NE}"], 48 * (e // NE) + 48)
                at_least(pe, S["eTe_ok"], 2 * (e - 1))
                for k in range(4):
                    ins = TR(bank[6 + q][:, k * P:(k + 1) * P], ex_st[e % NE][:, k, :], ident[:, :])
                ins.then_inc(S["eT_ok"], 1)
                pe.wait_ge(S["sev_ok"], 3)
                for k in range(2):
                    ins = MM(bank[q][:, k * P:(k + 1) * P], ex_st[e % NE][:, 4 + k, :], centre[:, :], start=True, stop=True)
                ins.then_inc(S["eT_ok"], 1)

            for g in range(2 * NG):
                pe.wait_ge(S["xn_ok"], g // 2 + 1)
                at_least(pe, S[f"xTe_ok{g % 2}"], g // 2)
                for j in range(4):
                    ins = TR(bank[2 + g % 2][:, j * P:(j + 1) * P], xn[:, 4 * g + j, :], ident[:, :])
                ins.then_inc(S["xT_ok"], 1)
                if g >= 1:
                    small(g - 1)
                if g >= EARLY:
                    expert(g - EARLY)
            small(2 * NG - 1)
            for e in range(2 * NG - EARLY, 7):
                expert(e)
            pe.wait_ge(S["both_ok"], 1)
            for q in range(2):
                pe.wait_ge(S[f"xTe_ok{q}"], NG)
            picks = both[:, :, :].rearrange("p j e -> p (j e)")
            MM(bank[2][:, :], before[:, :], picks, start=True, stop=True)
            MM(bank[3][:, :], ones_bf[:, :], picks, start=True, stop=True).then_inc(S["cum_ok"], 1)
            for e in range(7, E):
                expert(e)
            pe.wait_ge(S["r_act"], 4)
            TR(bank[5][:, 384:512], decay[:, :, :].rearrange("p j h -> p (j h)"), ident[:, :]).then_inc(S["dtT_ok"], 1)
            pe.wait_ge(S["end_ok"], 1)
            MM(bank[4][:, 384:384 + MT], ones[0:E, :], ended[0:E, :], start=True, stop=True).then_inc(S["ow_ok"], 1)

            def project(n):
                for k in range(3):
                    at_least(pe, s_t0, 3 * n + k - 2)
                    if k == 2:
                        at_least(pe, s_bt, n)
                    MM(proj_ps(k), winT[:, DI + k * P:DI + (k + 1) * P], xnT_b[:, :, bass.ds(n * P, WIN)],
                       start=True, stop=True).then_inc(s_px, 1)
                at_least(pe, s_z, n)
                at_least(pe, s_f0, 2 * n - 4)
                for k in range(2):
                    ins = MM(bank[3][:, k * NB * P:(k + 1) * NB * P].rearrange("p (b n) -> p b n", b=NB),
                             winT[:, k * P:(k + 1) * P], xnT_b[:, :, bass.ds(n * P + HALO, P)], start=True, stop=True)
                ins.then_inc(s_pz, 1)

            ng = 2 * NT // GRP
            pe.wait_ge(S["eTe_ok"], 2 * E)
            for g in range(ng):
                pe.wait_ge(S["oh_ok"], g + 1)
                if g == 2:
                    project(0)
                for k in range(GRP):
                    for part, moving in enumerate((tile_row, tile_base)):
                        ins = MM(bank[6][:, 0:MT], is_lane[g % 2][:, :, k], moving[g % 2][:, :, k],
                                 start=(g == 0 and k == 0 and part == 0),
                                 stop=(g == ng - 1 and k == GRP - 1 and part == 1))
                ins.then_inc(S["tk_ok"], 1)

            pe.wait_ge(S["own_ok"], 1)
            pe.wait_ge(s_t0, 3)
            pe.wait_ge(s_z, 1)
            pe.wait_ge(S["tok_ok"], 1)

            def turn_x(s, j):
                pe.wait_ge(m_xg[j], 2 * (s - j) + 16)
                at_least(pe, m_xt, s - 1)
                o = j % R
                TR(bank_x[o % 2][:, 0:P], xg[j][:, :], ident[:, :]).then_inc(m_t, 1)

            def up_proj(s, j, e):
                at = pe.snap(e * (2 * F))
                pe.wait_ge(m_xt, s + 1)
                at_least(pe, m_hid, s - 1)
                MM(bank_h[j % 2][:, :], xgT[j][:, :], w13T[:, bass.ds(at, 2 * F)], start=True, stop=True).then_inc(m_h, 1)

            def turn_hidden(s, j):
                pe.wait_ge(m_hid, s + 1)
                at_least(pe, m_hte, s - 1)
                for k in range(2):
                    ins = TR(bank_t[j % 2][:, k * P:(k + 1) * P], hid[j % 2][:, k * P:(k + 1) * P],
                             ident[:, :])
                ins.then_inc(m_ht, 1)

            def down_proj(s, j, e):
                at = pe.snap(e * F)
                pe.wait_ge(m_hte, s + 1)
                at_least(pe, m_g, s - 1)
                for k in range(2):
                    ins = MM(bank_y[j % 2][:, 0:D], hidT[j % 2][:, k, :], w2T[:, bass.ds(at + k * P, P)],
                             start=(k == 0), stop=(k == 1))
                ins.then_inc(m_y, 1)

            def step(s, j):
                if s + 1 < MT:
                    turn_x(s + 1, (j + 1) % RG)
                if 0 <= s < MT:
                    up_proj(s, j % R, expert_of(words, s, 0))
                    read_ahead(pe, words, s)
                if 1 <= s <= MT:
                    turn_hidden(s - 1, (j - 1) % R)
                if 2 <= s:
                    down_proj(s - 2, (j - 2) % R, expert_of(words, s, 2))

            words = {}
            for w in range(2):
                read_owners(pe, words, 0, w)
            for s in range(-1, MT + 2):
                if s == 2:
                    pe.wait_ge(S["rows_ok"], 2)
                step(s, s % RG)

            pe.wait_ge(m_hid, MT)
            pe.wait_ge(m_xt, MT)
            pe.wait_ge(m_hte, MT)
            pe.wait_ge(m_g, MT)
            pe.wait_ge(S["skip_ok"], 2)

            def turn(c, q):
                pe.wait_ge(s_sx, c + 1)
                at_least(pe, s_xdt, c)
                for b in range(NB):
                    for k in range(2):
                        TR(bank[4][:, b * DI + k * P:b * DI + (k + 1) * P], xcT[q][:, k, b, :], ident[:, :])
                pe.wait_ge(s_sbc, c + 1)
                at_least(pe, s_m, 2 * c)
                MM(bank[5][:, 0:P], BT[q][0:NS, :], CT[q][0:NS, :], start=True, stop=True).then_inc(s_g0, 1)
                at_least(pe, s_bt, c)
                TR(bank[2][:, 384:512], BT[q][:, :], ident[:, :]).then_inc(s_tr, 1)
                pe.wait_ge(s_g0, c + 1)
                MM(bank[5][:, P:2 * P], BT[q][NS:2 * NS, :], CT[q][NS:2 * NS, :], start=True, stop=True).then_inc(s_g, 1)

            def chunk_state(c, q):
                pe.wait_ge(s_xe, c + 1)
                pe.wait_ge(s_bt, c + 1)
                pe.wait_ge(s_ha, c + 1)
                for b in range(NB):
                    ins = MM(bank[6][b * NS:(b + 1) * NS, 0:NH * HD], Bt[q][:, b * NS:(b + 1) * NS],
                             xend[q][:, b, :, :].rearrange("p h e -> p (h e)"), start=True, stop=True)
                ins.then_inc(s_s, 1)

            def mix_steps(c, q):
                pe.wait_ge(s_xdt, c + 1)
                pe.wait_ge(s_cp, c + 1)
                pe.wait_ge(s_ha, c + 1)
                pe.wait_ge(s_m, 2 * c + 2)
                at_least(pe, s_yg, c)
                for b in range(NB):
                    n = slice(b * NS, (b + 1) * NS)
                    for h in range(0, NH, 2):
                        at = (h // 2) * NB * P + b * P
                        MM(bank[7][:, at:at + P], skipT[:, h // 2, :], xcT[q][:, h // 2, b, :], start=True, stop=False)
                        for k in range(2):
                            if b == 1 and h == 0 and k == 1:
                                pe.wait_ge(s_y0, c + 1)
                            MM(bank[7][k * HD:(k + 1) * HD, at:at + P], xdt[q][:, b, h + k, :],
                               M[q][:, b, (h + k) * P:(h + k + 1) * P], start=False, stop=False)
                        for k in range(2):
                            ins = MM(bank[7][k * HD:(k + 1) * HD, at:at + P], H[q][n, (h + k) * HD:(h + k + 1) * HD],
                                     CP[q][n, h + k, :], start=False, stop=True)
                    ins.then_inc((s_y0, s_y)[b], 1)

            def project_back(c, q, after_z=True):
                pe.wait_ge(s_sq, c + 1)
                if isinstance(c, int) and c == NC - 1:
                    pe.wait_ge(s_xdt, NC)
                else:
                    at_least(pe, s_f0, 2 * c)
                if after_z:
                    pe.wait_ge(s_z, c + 3)
                for b in range(NB):
                    for k in range(2):
                        MM(back_ps(c)[:, b * D:(b + 1) * D], yg[q][:, k, b, :], woT[:, k, :],
                           start=(k == 0), stop=(k == 1))
                for b in range(NB):
                    for k in range(2):
                        ins = MM(back_ps(c)[:, 256 + b:257 + b], ysq[q][:, k, b, :], ones[:, 0:1],
                                 start=(k == 0), stop=(k == 1))
                ins.then_inc(s_o, 1)

            def mixer_step(c, q, now=True, nxt=True, prev=True, update=True):
                if now:
                    turn(c, q)
                if nxt:
                    project(c + 1)
                if now:
                    mix_steps(c, q)
                if update:
                    chunk_state(c, q)
                if prev:
                    project_back(c - 1, 1 - q, nxt)

            mixer_step(0, 0, prev=False)
            mixer_step(1, 1)
            mixer_step(2, 0)
            mixer_step(3, 1)
            with pe.Fori(2, (NC - 2) // 2) as turn_no:
                c0 = turn_no * 2
                for q in range(2):
                    mixer_step(c0 + q, q)
            mixer_step(NC - 2, 0)
            mixer_step(NC - 1, 1, nxt=False, update=False)
            mixer_step(NC, 0, now=False, nxt=False, update=False)


INS = ["L0_attn_X", "L0_attn_W_in", "L0_attn_conv_w", "L0_attn_conv_b", "L0_attn_dt_bias", "L0_attn_A_log",
       "L0_attn_D", "L0_attn_norm_w", "L0_attn_W_out", "L0_ffn_router_w", "L0_ffn_router_b", "L0_ffn_w1",
       "L0_ffn_w2", "L0_ffn_w3", "L0_ffn_ln_g", "L0_ffn_ln_b"]


def kernel(**inputs):
    import numpy as np
    import concourse.bacc as bacc
    from concourse.bass_utils import run_bass_kernel_spmd

    nc = bacc.Bacc("TRN2", target_bir_lowering=False, num_devices=1)
    arrays, args = {}, []
    for name in INS:
        a = np.ascontiguousarray(inputs[name])
        arrays[f"in_{name}"] = a
        args.append(nc.dram_tensor(f"in_{name}", a.shape, mybir.dt.from_np(a.dtype), kind="ExternalInput").ap())
    out = nc.dram_tensor("out", (NB, SEQ, D), F32, kind="ExternalOutput").ap()
    build(nc, *args, out)
    r = run_bass_kernel_spmd(nc, [arrays], core_ids=[0])
    return np.asarray(r.results[0]["out"])
```
